# Optimizing a Trainium2 kernel written in Bass

```python
import numpy as np
import jax
import jax.numpy as jnp

def _softmax(x, axis=-1):
    return jax.nn.softmax(x, axis=axis)

def _gelu(x):
    return jax.nn.gelu(x, approximate=True)

def _silu(x):
    return jax.nn.silu(x)

def _sigmoid(x):
    return jax.nn.sigmoid(x)

def _layernorm(x, axis=-1, eps=1e-05):
    m = jnp.mean(x, axis=axis, keepdims=True)
    v = jnp.var(x, axis=axis, keepdims=True)
    return (x - m) / jnp.sqrt(v + eps)

def _scatter_add(tgt, idx, src, axis=0):
    return tgt.at[idx].add(src)

def _segment_sum(src, seg, n):
    return jax.ops.segment_sum(src, seg, n)
kernel_name = 'mk_adj_seq_d1_adj_r2_591a93'

def setup_inputs(seed: int=0):
    np.random.seed(seed)
    _w = jnp.asarray

    def _rec_inputs():
        import jax
        import jax.numpy as jnp
        _gk = jax.random.key(seed)
        x = -0.0005207 + 1.001 * jax.random.normal(jax.random.fold_in(_gk, 1), (4096, 256), jnp.float32)
        _a = jax.random.bernoulli(jax.random.fold_in(_gk, 2), 0.000488281, (4096, 4096))
        adj = _a.astype(jnp.int32)
        return (x, adj)
    x, adj = _rec_inputs()

    def _L0_gnn_setup():
        import jax, jax.numpy as jnp
        import numpy as np
        D_MODEL = 256
        N_HEADS = 8
        D_K = D_MODEL // N_HEADS
        D_FF = 1024
        N = 2048
        EPS = 1e-05

        def _layer_norm(x, g, b):
            mu = jnp.mean(x, axis=-1, keepdims=True)
            var = jnp.mean(jnp.square(x - mu), axis=-1, keepdims=True)
            return (x - mu) * jax.lax.rsqrt(var + EPS) * g + b
        key = jax.random.key(seed)
        ks = jax.random.split(key, 16)
        s = 1.0 / np.sqrt(D_MODEL)
        sf = 1.0 / np.sqrt(D_FF)
        inp = {'h': jax.random.normal(ks[0], (N, D_MODEL), dtype=jnp.float32), 'adj': jax.random.randint(ks[1], (N, N), 0, 2, dtype=jnp.int32), 'Wq': jax.random.uniform(ks[2], (D_MODEL, D_MODEL), jnp.float32, -s, s), 'bq': jnp.zeros((D_MODEL,), jnp.float32), 'Wk': jax.random.uniform(ks[3], (D_MODEL, D_MODEL), jnp.float32, -s, s), 'bk': jnp.zeros((D_MODEL,), jnp.float32), 'Wv': jax.random.uniform(ks[4], (D_MODEL, D_MODEL), jnp.float32, -s, s), 'bv': jnp.zeros((D_MODEL,), jnp.float32), 'Wo': jax.random.uniform(ks[5], (D_MODEL, D_MODEL), jnp.float32, -s, s), 'bo': jnp.zeros((D_MODEL,), jnp.float32), 'W1': jax.random.uniform(ks[6], (D_FF, D_MODEL), jnp.float32, -s, s), 'b1': jnp.zeros((D_FF,), jnp.float32), 'W2': jax.random.uniform(ks[7], (D_MODEL, D_FF), jnp.float32, -sf, sf), 'b2': jnp.zeros((D_MODEL,), jnp.float32), 'ln1_g': jnp.ones((D_MODEL,), jnp.float32), 'ln1_b': jnp.zeros((D_MODEL,), jnp.float32), 'ln2_g': jnp.ones((D_MODEL,), jnp.float32), 'ln2_b': jnp.zeros((D_MODEL,), jnp.float32)}
        return inp
    _L0_gnn_all = _L0_gnn_setup()
    _L0_gnn_in = {k: v for k, v in _L0_gnn_all.items() if k in ('Wq', 'bq', 'Wk', 'bk', 'Wv', 'bv', 'Wo', 'bo', 'W1', 'b1', 'W2', 'b2', 'ln1_g', 'ln1_b', 'ln2_g', 'ln2_b')}
    del _L0_gnn_all
    return {'x': x, 'adj': adj, 'L0_gnn_Wq': _L0_gnn_in['Wq'], 'L0_gnn_bq': _L0_gnn_in['bq'], 'L0_gnn_Wk': _L0_gnn_in['Wk'], 'L0_gnn_bk': _L0_gnn_in['bk'], 'L0_gnn_Wv': _L0_gnn_in['Wv'], 'L0_gnn_bv': _L0_gnn_in['bv'], 'L0_gnn_Wo': _L0_gnn_in['Wo'], 'L0_gnn_bo': _L0_gnn_in['bo'], 'L0_gnn_W1': _L0_gnn_in['W1'], 'L0_gnn_b1': _L0_gnn_in['b1'], 'L0_gnn_W2': _L0_gnn_in['W2'], 'L0_gnn_b2': _L0_gnn_in['b2'], 'L0_gnn_ln1_g': _L0_gnn_in['ln1_g'], 'L0_gnn_ln1_b': _L0_gnn_in['ln1_b'], 'L0_gnn_ln2_g': _L0_gnn_in['ln2_g'], 'L0_gnn_ln2_b': _L0_gnn_in['ln2_b']}

def reference(x, adj, L0_gnn_Wq, L0_gnn_bq, L0_gnn_Wk, L0_gnn_bk, L0_gnn_Wv, L0_gnn_bv, L0_gnn_Wo, L0_gnn_bo, L0_gnn_W1, L0_gnn_b1, L0_gnn_W2, L0_gnn_b2, L0_gnn_ln1_g, L0_gnn_ln1_b, L0_gnn_ln2_g, L0_gnn_ln2_b):
    import jax
    import jax.numpy as jnp

    def _L0_gnn_ref(h, adj, Wq, bq, Wk, bk, Wv, bv, Wo, bo, W1, b1, W2, b2, ln1_g, ln1_b, ln2_g, ln2_b):
        import jax, jax.numpy as jnp
        import numpy as np
        D_MODEL = 256
        N_HEADS = 8
        D_K = D_MODEL // N_HEADS
        D_FF = 1024
        N = 2048
        EPS = 1e-05

        def _layer_norm(x, g, b):
            mu = jnp.mean(x, axis=-1, keepdims=True)
            var = jnp.mean(jnp.square(x - mu), axis=-1, keepdims=True)
            return (x - mu) * jax.lax.rsqrt(var + EPS) * g + b
        n = h.shape[0]
        mask = adj.astype(jnp.float32) + jnp.eye(n, dtype=jnp.float32)
        q = (h @ Wq.T + bq).reshape(n, N_HEADS, D_K)
        k = (h @ Wk.T + bk).reshape(n, N_HEADS, D_K)
        v = (h @ Wv.T + bv).reshape(n, N_HEADS, D_K)
        scores = jnp.einsum('nhd,mhd->hnm', q, k) / jnp.sqrt(jnp.float32(D_K))
        scores = jnp.where(mask[None, :, :] == 0, jnp.float32(-1000000000.0), scores)
        attn = jax.nn.softmax(scores, axis=-1)
        ctx = jnp.einsum('hnm,mhd->nhd', attn, v).reshape(n, D_MODEL)
        attn_out = ctx @ Wo.T + bo
        h1 = _layer_norm(h + attn_out, ln1_g, ln1_b)
        ff = jax.nn.relu(h1 @ W1.T + b1) @ W2.T + b2
        h2 = _layer_norm(h1 + ff, ln2_g, ln2_b)
        return h2
    x = _L0_gnn_ref(x, adj, L0_gnn_Wq, L0_gnn_bq, L0_gnn_Wk, L0_gnn_bk, L0_gnn_Wv, L0_gnn_bv, L0_gnn_Wo, L0_gnn_bo, L0_gnn_W1, L0_gnn_b1, L0_gnn_W2, L0_gnn_b2, L0_gnn_ln1_g, L0_gnn_ln1_b, L0_gnn_ln2_g, L0_gnn_ln2_b)
    return x

_drawn_inputs = setup_inputs


def setup_inputs(seed=0):
    import zlib

    import numpy as np

    out = dict(_drawn_inputs(seed))
    spreads = {'L0_gnn_bq': (0.0, 0.8),
     'L0_gnn_bk': (0.0, 0.8),
     'L0_gnn_bv': (0.0, 0.1),
     'L0_gnn_bo': (0.0, 0.1),
     'L0_gnn_b1': (0.0, 0.1),
     'L0_gnn_b2': (0.0, 0.1),
     'L0_gnn_ln1_g': (1.0, 0.2),
     'L0_gnn_ln1_b': (0.0, 0.1),
     'L0_gnn_ln2_g': (1.0, 0.2),
     'L0_gnn_ln2_b': (0.0, 0.1)}
    factors = {}
    for name, (base, spread) in spreads.items():
        noise = np.random.default_rng([zlib.crc32(name.encode()), seed]).standard_normal(out[name].shape)
        drawn = base * np.exp(spread * noise) if base else spread * noise
        out[name] = jnp.asarray(drawn.astype(out[name].dtype))
    for name, factor in factors.items():
        out[name] = (out[name] * factor).astype(out[name].dtype)
    return out
```

```python
import concourse.bass as bass
from concourse import mybir
from contextlib import ExitStack


def build(nc, x, xT, adj, WqT, bq, WkT, bk, WvT, bv, WoT, bo, W1T, b1, W2T, b2, g1, n1, g2, n2, kv, out):
    F32, I32, U32, U8 = mybir.dt.float32, mybir.dt.int32, mybir.dt.uint32, mybir.dt.uint8
    ALU, ACT, AX = mybir.AluOpType, mybir.ActivationFunctionType, mybir.AxisListType.X

    P = 128
    N, D = x.shape
    FF = W1T.shape[1]
    H = 8
    DK = D // H
    NT = N // P
    J = 4
    NG = NT // J
    KD = D // P
    KF = FF // P
    HALF = N // 2
    FOUND = 8
    LIST = 2 * FOUND
    CAP = 10
    UW = HALF + FOUND
    SCALE = float(DK) ** -0.5
    EPS = 1e-5
    MASKED = -1e9
    LIFT = 8e34
    EARLY = 16
    BETWEEN = 4
    GS = (NT - EARLY - BETWEEN) // 2

    def at(i, n=1):
        return slice(i, i + n) if isinstance(i, int) else bass.DynSlice(i, n)

    ctx = ExitStack()
    with ctx:
        def sb(name, shape, dt=F32):
            return ctx.enter_context(nc.sbuf_tensor(name, shape, dt))

        def sem(name):
            return ctx.enter_context(nc.semaphore(name))

        wo = sb("wo", [P, KD, D])
        w1 = sb("w1", [P, KD, FF])
        w2 = sb("w2", [P, KF, D])
        bo_b, b2_b, g1_b, n1_b, g2_b, n2_b = (sb(n, [P, D]) for n in ("bo_b", "b2_b", "g1_b", "n1_b", "g2_b", "n2_b"))
        b1_c = sb("b1_c", [P, KF])
        bkT = sb("bkT", [P, KD])
        bqT = sb("bqT", [P, KD])
        ident = sb("ident", [P, P])
        ones8 = sb("ones8", [P, FOUND])
        onesc = sb("onesc", [P, 1])
        eps_c = sb("eps_c", [P, 1])
        selfkey = sb("selfkey", [P, NT])
        headmask = sb("headmask", [P, J])

        adjb = sb("adjb", [P, J * UW], I32)
        sqjunk = sb("sqjunk", [P, HALF], U8)
        Qs = sb("Qs", [P, NT, D])
        Vs = sb("Vs", [P, NT, D])
        s0 = sb("s0", [P, NT, H])
        keys = sb("keys", [P, NT + J, LIST])
        sq = sb("sq", [P, 2 * NT])
        cnt = sb("cnt", [P, NT])
        G = [sb(f"G{i}", [P, CAP, 2 * D]) for i in range(2)]
        wself = sb("wself", [P, D])
        g0, g1f = (g[:, :, :].rearrange("p s d -> p (s d)") for g in G)
        hh = sb("hh", [P, (KF + KD) * J * P])
        hid = hh[:, 0:KF * J * P].rearrange("p (c n) -> p c n", c=KF)
        h1T = hh[:, KF * J * P:(KF + KD) * J * P].rearrange("p (k n) -> p k n", k=KD)
        xTb = [g0[:, i * 1024:(i + 1) * 1024].rearrange("p (k n) -> p k n", k=KD) for i in range(2)]
        kst = [g0[:, 2048 + i * 1024:3072 + i * 1024].rearrange("p (j d) -> p j d", j=J) for i in range(2)]
        tmp = [g1f[:, i * 768:(i + 1) * 768] for i in range(2)]
        sprod = g1f[:, 1536:2560].rearrange("p (j d) -> p j d", j=J)
        wqkv = hh[:, 0:1536].rearrange("p (k n) -> p k n", k=KD)
        bkvq = hh[:, 1536:2304]
        xr = sb("xr", [P, J, D])
        h1 = [sb(f"h1_{i}", [P, D]) for i in range(2)]
        ctxT = [sb(f"ctxT{i}", [P, KD, P]) for i in range(2)]
        y1 = sb("y1", [P, D])
        z2 = [sb(f"z2_{i}", [P, D]) for i in range(2)]
        ob = [sb(f"ob{i}", [P, D]) for i in range(2)]
        st6 = [sb(f"st6_{i}", [P, 6]) for i in range(3)]
        mv = [sb(f"mv{i}", [P, 2]) for i in range(3)]
        lnv = [sb(f"lnv{i}", [P, 1]) for i in range(3)]
        rstd = [sb(f"rstd{i}", [P, 1]) for i in range(3)]
        raw = sb("raw", [P, 2, LIST], U32)
        neg = sb("neg", [P, 2, LIST])
        off = sb("off", [P, 2, FOUND])
        hit = sb("hit", [P, 2, LIST])
        val = sb("val", [P, 2, LIST])
        ne = sb("ne", [P, 2, LIST])
        val2 = sb("val2", [P, 2, LIST])
        top = sb("top", [P, 2, LIST])
        gidx = sb("gidx", [P, J, CAP], U32)
        lim = sb("lim", [P, J, CAP])
        sc = sb("sc", [P, CAP + 1, H])
        mx = sb("mx", [P, H])
        dsh = sb("dsh", [P, CAP + 1, H])
        pe_ = sb("pe_", [P, CAP + 1, H])
        den = sb("den", [P, H])
        rden = sb("rden", [P, H])
        pn = sb("pn", [P, CAP + 1, H])
        bad = sb("bad", [P, NT])
        bad2 = sb("bad2", [P, NT])
        tsum = sb("tsum", [1, NT])
        tfl = sb("tfl", [1, NT])
        tkey = sb("tkey", [1, NT])
        tdown = sb("tdown", [1, NT])
        tlist = sb("tlist", [1, NT + 1])
        flags = sb("flags", [1, NT + 1], I32)

        KT = Qs[:, :, :].rearrange("p t d -> p (t d)").rearrange("p (k n) -> p k n", k=KD)
        S = g0[:, 0:N]
        vmask = g1f[:, 0:N]
        fadj = adjb[:, 0:N]
        pen = adjb[:, N:2 * N].bitcast(F32)
        qz = hh[:, 0:1024].rearrange("p (h n) -> p h n", h=H)
        stg = hh[:, 1024:1536]
        PT = hh[:, 1536:2048].rearrange("p (c n) -> p c n", c=J)
        fw = hh[:, 2048:3584].rearrange("p (k n) -> p k n", k=KD)
        fxT = h1T
        fctx = z2[1]
        fx = ctxT[1]
        fsm = sb("fsm", [P, 4])
        fmax, fnmax, fden, frden = (fsm[:, i:i + 1] for i in range(4))

        ps = [ctx.enter_context(nc.psum_tensor(f"ps{i}", [P, 1024], F32)) for i in range(4)]
        qkv_p = ps[0:2]
        ff1_p = [ps[0][:, 0:512], ps[0][:, 512:1024]]
        fs_p = ps[1][:, 0:512]
        ff2_p = [ps[1][:, 0:D], ps[1][:, 512:512 + D]]
        ctx_p = [ps[2][:, 0:D], ps[2][:, 512:512 + D]]
        ao_p = ps[3][:, 0:D]
        h1T_p = ps[3][:, 512:512 + D]

        w_in = sem("w_in"); wq_in = sem("wq_in"); bias_in = sem("bias_in"); colb_in = sem("colb_in")
        pool_const = sem("pool_const"); dve_const = sem("dve_const")
        adj_in = [sem(f"adj_in{i}") for i in range(J)]
        adj_scanned = sem("adj_scanned"); adj_squared = sem("adj_squared")
        xT_in = [sem(f"xT_in{i}") for i in range(2)]
        qkv_done = sem("qkv_done"); qkv_copied = sem("qkv_copied")
        k_ready = sem("k_ready"); v_ready = sem("v_ready"); q_ready = sem("q_ready")
        self_scored = sem("self_scored"); k_stored = [sem(f"k_stored{i}") for i in range(2)]; v_stored = sem("v_stored")
        staged = sem("staged"); gathered = [sem(f"gathered{i}") for i in range(2)]
        shifted = sem("shifted"); exp_done = sem("exp_done"); weighted = sem("weighted")
        ctx_summed = sem("ctx_summed"); ctxT_ready = sem("ctxT_ready"); ao_done = sem("ao_done")
        x_in = [sem(f"x_in{i}") for i in range(J)]
        x_biased = sem("x_biased"); y_done = sem("y_done")
        var1_ready = sem("var1_ready"); ln_act = sem("ln_act"); rstd1_ready = sem("rstd1_ready")
        h1_ready = sem("h1_ready"); h1T_done = sem("h1T_done"); h1T_ready = sem("h1T_ready")
        ff1_done = sem("ff1_done"); hid_ready = sem("hid_ready"); ff2_done = sem("ff2_done"); z_done = sem("z_done")
        var2_ready = sem("var2_ready"); rstd2_ready = sem("rstd2_ready")
        out_ready = sem("out_ready"); out_stored = [sem(f"out_stored{i}") for i in range(2)]
        carried = sem("carried"); dstep = sem("dstep")
        bad_ready = sem("bad_ready"); bad_summed = sem("bad_summed"); flags_ready = sem("flags_ready")
        f_w = sem("f_w"); f_x = sem("f_x"); f_ktmm = sem("f_ktmm"); f_kt = sem("f_kt"); f_in = sem("f_in"); f_q = sem("f_q")
        f_qz = sem("f_qz"); f_s = sem("f_s"); f_sread = sem("f_sread"); f_max = sem("f_max"); f_e = sem("f_e")
        f_st = sem("f_st"); f_t = sem("f_t"); f_pt = sem("f_pt"); f_pv = sem("f_pv"); f_acc = sem("f_acc")
        f_baton = sem("f_baton"); f_step = sem("f_step"); f_out = sem("f_out"); f_ctx = sem("f_ctx")

        xT_v = xT.rearrange("(k p) n -> p k n", p=P)
        kv_rows = kv.rearrange("(t p) c -> p t c", p=P)

        def apart(eng):
            eng.sem_inc(carried, 1)

        class Steps:
            def __init__(self, eng, s, base=0):
                self.eng, self.s, self.base, self.n = eng, s, base, 0

            def mark(self, ins):
                ins.then_inc(self.s, 1)
                self.n += 1

            def wait(self):
                self.eng.wait_ge(self.s, self.base + self.n)

        F_CSUM, F_CTXT, F_AO, F_VAR1, F_RSTD1, F_H1, F_H1T, F_FF = range(1, 9)
        F_FF2 = F_FF + 2 * KF + 1
        F_VAR2, F_RSTD2, F_TAIL = F_FF2 + 1, F_FF2 + 2, F_FF2 + 3
        F_STEPS = 3 + H * (NG + 4) + 9

        block = ctx.enter_context(nc.Block())

        @block.sync
        def _(sp):
            def load_unit(u_tile, half, b, k):
                sp.wait_ge(adj_scanned, k + 1)
                sp.wait_ge(adj_squared, k + 1)
                sp.dma_start(adjb[:, b * UW:b * UW + HALF],
                             adj[at(u_tile * P, P), half * HALF:(half + 1) * HALF]).then_inc(adj_in[b], 16)

            def load_wqkv(dst, s):
                for wT, c in ((WkT, 0), (WvT, 1), (WqT, 2)):
                    sp.dma_start(dst[:, :, c * D:(c + 1) * D], wT.rearrange("(k p) n -> p k n", p=P)).then_inc(s, 16)

            load_wqkv(wqkv, wq_in)
            with sp.Fori(0, NG // 2) as i:
                for s in range(2):
                    g = i * 2 + s
                    sp.wait_ge(qkv_done, g * J)
                    sp.dma_start(xTb[s], xT_v[:, :, at(g * J * P, J * P)]).then_inc(xT_in[s], 16)
                    for k in range(J):
                        load_unit(g * 2 + k // 2, k % 2, k, g * J + k)
            for k in range(2 * BETWEEN):
                load_unit(EARLY + k // 2, k % 2, k % J, 2 * EARLY + k)

            def step(g, j, search, prev):
                sp.wait_ge(y_done, g * J + j + 1)
                sp.dma_start(xr[:, j, :], x[at((g * J + j) * P, P), :]).then_inc(x_in[j], 16)
                if search:
                    load_unit(g * 2 + (EARLY + BETWEEN + j // 2), j % 2, j, g * J + (2 * (EARLY + BETWEEN) + j))
                if prev and j >= 2:
                    for i in range(2):
                        store((g - 1) * J + 2 * (j - 2) + i, i, (g - 1) * J + 2 * (j - 2) + i)

            def store(t, i, n):
                sp.wait_ge(out_ready, n + 1)
                sp.dma_start(out[at(t * P, P), :], ob[i][:, :]).then_inc(out_stored[i], 16)

            for j in range(J):
                step(0, j, True, False)
            with sp.Fori(1, GS) as g:
                for j in range(J):
                    step(g, j, True, True)
            with sp.Fori(GS, NG) as g:
                for j in range(J):
                    step(g, j, False, True)
            for j in range(J):
                store((NG - 1) * J + j, j % 2, (NG - 1) * J + j)
            for i in range(2):
                sp.wait_ge(out_stored[i], 16 * NT // 2)

            sp.wait_ge(flags_ready, 1)
            nf = sp.value_load(flags[0:1, 0:1], min_val=0, max_val=NT)
            with sp.If(nf > 0):
                sp.wait_ge(out_ready, NT)
                load_wqkv(fw, f_w)
                with sp.Fori(0, NG) as c:
                    sp.wait_ge(f_kt, c * KD)
                    sp.dma_start(fxT, xT_v[:, :, at(c * 512, 512)]).then_inc(f_x, 16)
                with sp.Fori(0, nf) as r:
                    f = sp.value_load(flags[0:1, at(r + 1, 1)], min_val=0, max_val=NT - 1)
                    sp.wait_ge(f_kt, KD * NG)
                    sp.wait_ge(f_out, r * 16)
                    sp.dma_start(fadj, adj[at(f * P, P), :]).then_inc(f_in, 16)
                    load_wqkv(fw, f_w)
                    sp.dma_start(fx[:, :, :], xT_v[:, :, at(f * P, P)]).then_inc(f_in, 16)
                    sp.dma_start(xr[:, 0, :], x[at(f * P, P), :]).then_inc(f_in, 16)
                    sp.wait_ge(f_baton, r * F_TAIL + F_TAIL)
                    sp.dma_start(out[at(f * P, P), :], ob[0][:, :]).then_inc(f_out, 16)
                    sp.wait_ge(f_out, r * 16 + 16)
                    apart(sp)

        @block.gpsimd
        def _(pool):
            for s in (k_ready, v_ready, q_ready):
                pool.sem_inc(s, 2)
            nc.gpsimd.memset(ident[:, :], 0.0).then_inc(pool_const, 1)
            nc.gpsimd.iota(selfkey[:, :], pattern=[[-P, NT]], base=N, channel_multiplier=-1,
                           allow_small_or_imprecise_dtypes=True).then_inc(pool_const, 1)
            nc.gpsimd.iota(tdown[:, :], pattern=[[-1, NT]], base=NT, channel_multiplier=0,
                           allow_small_or_imprecise_dtypes=True).then_inc(pool_const, 1)
            nc.gpsimd.memset(headmask[:, :], 1.0).then_inc(pool_const, 1)
            pool.wait_ge(pool_const, 4)
            nc.gpsimd.affine_select(out=ident[:, :], in_=ident[:, :], compare_op=ALU.not_equal, fill=1.0,
                                    base=0, pattern=[[-1, P]], channel_multiplier=1).then_inc(pool_const, 1)
            nc.gpsimd.affine_select(out=headmask[:, :], in_=headmask[:, :], compare_op=ALU.is_ge, fill=0.0,
                                    base=0, pattern=[[-DK, J]], channel_multiplier=1).then_inc(pool_const, 1)
            pool.wait_ge(pool_const, 6)
            nc.gpsimd.affine_select(out=headmask[:, :], in_=headmask[:, :], compare_op=ALU.is_ge, fill=0.0,
                                    base=DK - 1, pattern=[[DK, J]], channel_multiplier=-1).then_inc(pool_const, 1)

            pool.wait_ge(bias_in, 16 * 9)
            with pool.Fori(0, NG // 2) as i:
                for s in range(2):
                    g = i * 2 + s
                    pool.wait_ge(self_scored, g + 1)
                    pool.wait_ge(k_stored[s], i * 16)
                    for j in range(J):
                        t = g * J + j
                        pool.wait_ge(qkv_copied, t + 3)
                        nc.gpsimd.tensor_tensor(kst[s][:, j, :], tmp[j % 2][:, 0:D], bkvq[:, 0:D],
                                                ALU.add).then_inc(k_ready, 1)
                        nc.gpsimd.tensor_tensor(Vs[:, at(t), :], tmp[j % 2][:, D:2 * D].unsqueeze(1),
                                                bkvq[:, D:2 * D].unsqueeze(1), ALU.add).then_inc(v_ready, 1)
                        nc.gpsimd.tensor_tensor(Qs[:, at(t), :], tmp[j % 2][:, 2 * D:3 * D].unsqueeze(1),
                                                bkvq[:, 2 * D:3 * D].unsqueeze(1), ALU.add).then_inc(q_ready, 1)
                    pool.wait_ge(k_ready, g * J + J + 2)
                    pool.dma_start(kv_rows[:, at(g * J, J), 0:D], kst[s]).then_inc(k_stored[s], 16)
                    pool.wait_ge(v_ready, g * J + J + 2)
                    pool.dma_start(kv_rows[:, at(g * J, J), D:2 * D], Vs[:, at(g * J, J), :]).then_inc(v_stored, 16)

            for s in range(2):
                pool.wait_ge(k_stored[s], 16 * NG // 2)
            pool.wait_ge(v_stored, 16 * NG)
            pool.wait_ge(self_scored, NG + 2)
            pool.wait_ge(q_ready, NT + 2)
            pool.wait_ge(dve_const, 5)
            with pool.Fori(0, NG) as g:
                for j in range(J):
                    t = g * J + j
                    pool.wait_ge(staged, t + 1)
                    pool.wait_ge(ctx_summed, t)
                    apart(pool)
                    for s in range(CAP):
                        pool.indirect_dma_start(out=G[j % 2][:, s, :], out_offset=None, in_=kv[:, :],
                                                in_offset=bass.IndirectOffsetOnAxis(ap=gidx[:, j, s:s + 1], axis=0),
                                                bounds_check=N - 1, oob_is_err=False).then_inc(gathered[j % 2], 16)
                    pool.wait_ge(x_in[j], g * 16 + 16)
                    nc.gpsimd.tensor_tensor(xr[:, j, :], xr[:, j, :], bo_b[:, :], ALU.add).then_inc(x_biased, 1)

        @block.scalar
        def _(act):
            act.sem_inc(adj_squared, J)
            act.sem_inc(qkv_copied, 2)
            for c, b in enumerate((bk, bv, bq)):
                act.dma_start(bkvq[:, c * D:(c + 1) * D], b.partition_broadcast(P)).then_inc(bias_in, 16)
            for dst, b in ((bo_b, bo), (b2_b, b2), (g1_b, g1), (n1_b, n1), (g2_b, g2), (n2_b, n2)):
                act.dma_start(dst[:, :], b.partition_broadcast(P)).then_inc(bias_in, 16)
            act.dma_start(wo[:, :, :], WoT.rearrange("(k p) n -> p k n", p=P)).then_inc(w_in, 16)
            act.dma_start(w1[:, :, :], W1T.rearrange("(k p) n -> p k n", p=P)).then_inc(w_in, 16)
            act.dma_start(w2[:, :, :], W2T.rearrange("(k p) n -> p k n", p=P)).then_inc(w_in, 16)
            with nc.allow_non_contiguous_dma("per-partition biases"):
                act.dma_start(b1_c[:, :], b1.rearrange("(c p) -> p c", p=P)).then_inc(colb_in, 16)
                act.dma_start(bkT[:, :], bk.rearrange("(c p) -> p c", p=P)).then_inc(colb_in, 16)
                act.dma_start(bqT[:, :], bq.rearrange("(c p) -> p c", p=P)).then_inc(colb_in, 16)

            def square(k, b, visit):
                act.wait_ge(adj_in[b], visit * 16 + 16)
                act.wait_ge(adj_squared, k + J)
                nc.scalar.activation(sqjunk[:, :], adjb[:, b * UW:b * UW + HALF], ACT.Square,
                                     accum_out=sq[:, at(k)]).then_inc(adj_squared, 1)

            def copy_qkv(t, b):
                act.wait_ge(qkv_done, t + 1 + J)
                act.wait_ge(q_ready, t + 1)
                act.wait_ge(v_ready, t + 1)
                act.wait_ge(k_ready, t + 1)
                nc.scalar.copy(tmp[b], qkv_p[b][:, 0:3 * D]).then_inc(qkv_copied, 1)

            with act.Fori(0, NG // 2) as i:
                for s in range(2):
                    g = i * 2 + s
                    for j in range(J):
                        copy_qkv(g * J + j, j % 2)
                        square(g * J + j, j, g)
            for k in range(2 * BETWEEN):
                square(2 * EARLY + k, k % J, NG + k // J)

            act.wait_ge(colb_in, 48)
            act.wait_ge(dve_const, 5)

            def rstd_of(i, ready, done, n, m):
                act.wait_ge(ready, n + 1)
                nc.scalar.activation(lnv[i][:, :], mv[i][:, 1:2], ACT.Ln, bias=eps_c[:, 0:1]).then_inc(ln_act, 1)
                act.wait_ge(ln_act, m + 1)
                nc.scalar.activation(rstd[i][:, :], lnv[i][:, :], ACT.Exp, scale=-0.5).then_inc(done, 1)

            def relu(c, n):
                act.wait_ge(ff1_done, n + 1)
                nc.scalar.activation(hid[:, c, :], ff1_p[c % 2], ACT.Relu, bias=b1_c[:, c:c + 1]).then_inc(hid_ready, 1)

            def copy_h1T(j, t):
                act.wait_ge(h1T_done, t + 1)
                nc.scalar.copy(h1T[:, :, j * P:(j + 1) * P],
                               h1T_p.rearrange("p (k n) -> p k n", k=KD)).then_inc(h1T_ready, 1)

            def step(g, j, search, prev, first=False):
                t = g * J + j
                if prev and j == 1:
                    for c in range(KF // 2, KF):
                        relu(c, (g - 1) * KF + c)
                act.wait_ge(shifted, t + 1)
                nc.scalar.activation(pe_[:, :, :], dsh[:, :, :], ACT.Exp, scale=SCALE).then_inc(exp_done, 1)
                seconds = ((g - 1) * J if prev else 0) + (2 if prev and j == 3 else 0)
                firsts = t - 1
                if not first:
                    rstd_of(0, var1_ready, rstd1_ready, firsts, firsts + seconds)
                if search:
                    square(g * J + (2 * (EARLY + BETWEEN) + j), j, g + (NG + 2 * BETWEEN // J))
                if not first:
                    copy_h1T((j - 1) % J, t - 1)
                if prev and j == 0:
                    for c in range(KF // 2):
                        relu(c, (g - 1) * KF + c)
                act.wait_ge(ctx_summed, t + 2)
                nc.scalar.copy(ctxT[j % 2][:, :, :], ctx_p[j % 2].rearrange("p (k n) -> p k n", k=KD)).then_inc(ctxT_ready, 1)
                if prev and j >= 2:
                    for i in range(2):
                        n = (g - 1) * J + 2 * (j - 2) + i
                        rstd_of(1 + i, var2_ready, rstd2_ready, n, t + n)

            for j in range(J):
                step(0, j, True, False, first=j == 0)
            with act.Fori(1, GS) as g:
                for j in range(J):
                    step(g, j, True, True)
            with act.Fori(GS, NG) as g:
                for j in range(J):
                    step(g, j, False, True)
            last = (NG - 1) * J
            rstd_of(0, var1_ready, rstd1_ready, NT - 1, NT - 1 + last)
            copy_h1T(J - 1, NT - 1)
            for c in range(KF):
                relu(c, (NG - 1) * KF + c)
            for j in range(J):
                rstd_of(1 + j % 2, var2_ready, rstd2_ready, last + j, NT + last + j)

            act.wait_ge(flags_ready, 1)
            nf = act.value_load(flags[0:1, 0:1], min_val=0, max_val=NT)
            with act.If(nf > 0):
                act.wait_ge(out_ready, NT)
                with act.Fori(0, NG) as c:
                    for dh in range(KD):
                        act.wait_ge(f_ktmm, c * KD + dh + 1)
                        nc.scalar.activation(KT[:, dh, at(c * 512, 512)], ff1_p[dh], ACT.Identity,
                                             bias=bkT[:, dh:dh + 1]).then_inc(f_kt, 1)
                with act.Fori(0, nf) as r:
                    for h in range(H):
                        act.wait_ge(f_max, r * H + h + 1)
                        nc.scalar.activation(S, S, ACT.Exp, bias=fnmax, accum_out=fden).then_inc(f_e, 1)
                        with act.Fori(0, NG) as c:
                            act.wait_ge(f_t, r * (H * NG) + h * NG + c + 1)
                            act.wait_ge(f_pv, r * (H * NG) + h * NG + c)
                            nc.scalar.copy(PT, ff1_p[0].rearrange("p (c n) -> p c n", c=J)).then_inc(f_pt, 1)
                    act.wait_ge(f_baton, r * F_TAIL + F_CSUM)
                    nc.scalar.copy(ctxT[0][:, :, :], ctx_p[0].rearrange("p (k n) -> p k n", k=KD)).then_inc(f_baton, 1)
                    act.wait_ge(f_baton, r * F_TAIL + F_VAR1)
                    nc.scalar.activation(lnv[0][:, :], mv[0][:, 1:2], ACT.Ln, bias=eps_c[:, 0:1]).then_inc(ln_act, 1)
                    act.wait_ge(ln_act, 2 * NT + r * 2 + 1)
                    nc.scalar.activation(rstd[0][:, :], lnv[0][:, :], ACT.Exp, scale=-0.5).then_inc(f_baton, 1)
                    act.wait_ge(f_baton, r * F_TAIL + F_H1T)
                    nc.scalar.copy(h1T[:, :, 0:P], h1T_p.rearrange("p (k n) -> p k n", k=KD)).then_inc(f_baton, 1)
                    for c in range(KF):
                        act.wait_ge(f_baton, r * F_TAIL + F_FF + 2 * c + 1)
                        nc.scalar.activation(hid[:, c, 0:P], ff1_p[c % 2][:, 0:P], ACT.Relu,
                                             bias=b1_c[:, c:c + 1]).then_inc(f_baton, 1)
                    act.wait_ge(f_baton, r * F_TAIL + F_VAR2)
                    nc.scalar.activation(lnv[1][:, :], mv[1][:, 1:2], ACT.Ln, bias=eps_c[:, 0:1]).then_inc(ln_act, 1)
                    act.wait_ge(ln_act, 2 * NT + r * 2 + 2)
                    nc.scalar.activation(rstd[1][:, :], lnv[1][:, :], ACT.Exp, scale=-0.5).then_inc(f_baton, 1)

        @block.vector
        def _(dve):
            nc.vector.memset(ones8[:, :], 1.0).then_inc(dve_const, 1)
            nc.vector.memset(onesc[:, :], 1.0).then_inc(dve_const, 1)
            nc.vector.memset(eps_c[:, :], EPS).then_inc(dve_const, 1)
            for b in range(J):
                nc.vector.memset(adjb[:, b * UW + HALF:(b + 1) * UW], 1).then_inc(adj_scanned, 1)
            nc.vector.memset(g0[:, 4096:], 0.0).then_inc(dve_const, 1)
            nc.vector.memset(g1f[:, 2560:], 0.0).then_inc(dve_const, 1)
            nc.vector.memset(keys[:, NT:NT + J, :], 0.0).then_inc(dstep, 1)
            for s, n in ((self_scored, 2), (weighted, 4), (y_done, J)):
                dve.sem_inc(s, n)
            st = Steps(dve, dstep)
            st.n = 1

            def find(k, b, visit):
                dve.wait_ge(adj_in[b], visit * 16 + 16)
                apart(dve)
                i = b // 2
                nc.vector.max_index(raw[:, i, (b % 2) * FOUND:(b % 2 + 1) * FOUND], ones8[:, :],
                                    adjb[:, b * UW:(b + 1) * UW]).then_inc(adj_scanned, 1)

            def lists(t, k):
                dve.wait_ge(adj_scanned, k + J)
                st.mark(nc.vector.tensor_scalar(neg[:, :, :], raw[:, :, :], float(HALF), 0.0, ALU.subtract, ALU.min))
                st.wait()
                st.mark(nc.vector.tensor_scalar(off[:, :, :], neg[:, :, 0:FOUND], 0.0, float(HALF), ALU.is_lt, ALU.mult))
                st.mark(nc.vector.tensor_scalar(val[:, :, FOUND:LIST], neg[:, :, FOUND:LIST], -1.0, None, ALU.mult))
                st.mark(nc.vector.tensor_scalar(hit[:, :, :], neg[:, :, :], 0.0, None, ALU.is_lt))
                st.wait()
                st.mark(nc.vector.tensor_tensor(val[:, :, 0:FOUND], off[:, :, :], neg[:, :, 0:FOUND], ALU.subtract))
                st.mark(nc.vector.tensor_reduce(cnt[:, at(t, 2)], hit[:, :, :], AX, ALU.add))
                st.wait()
                st.mark(nc.vector.tensor_tensor(ne[:, :, :], val[:, :, :],
                                                selfkey[:, at(t, 2)].unsqueeze(2).to_broadcast([P, 2, LIST]), ALU.not_equal))
                st.wait()
                st.mark(nc.vector.tensor_tensor(val[:, :, :], val[:, :, :], ne[:, :, :], ALU.mult))
                st.wait()
                apart(dve)
                for i in range(2):
                    st.mark(nc.vector.max(top[:, i, 0:FOUND], val[:, i, :]))
                st.wait()
                apart(dve)
                for i in range(2):
                    st.mark(nc.vector.match_replace(val2[:, i, :], top[:, i, 0:FOUND], val[:, i, :], 0.0))
                st.wait()
                apart(dve)
                for i in range(2):
                    st.mark(nc.vector.max(top[:, i, FOUND:LIST], val2[:, i, :]))
                st.wait()
                st.mark(nc.vector.tensor_copy(keys[:, at(t, 2), :], top[:, :, :]))
                st.wait()

            LISTS = 15
            dve.wait_ge(pool_const, 7)
            dve.wait_ge(dve_const, 5)
            with dve.Fori(0, NG // 2) as i:
                st.base, st.n = i * (2 * (LISTS + 1)) + 1, 0
                for s in range(2):
                    g = i * 2 + s
                    for k in range(J):
                        find(g * J + k, k, g)
                    lists(g * 2, g * J + J)
                    dve.wait_ge(k_ready, g * J + J + 2)
                    dve.wait_ge(q_ready, g * J + J + 2)
                    st.mark(nc.vector.tensor_tensor(sprod, kst[s], Qs[:, at(g * J, J), :], ALU.mult))
                    st.wait()
                    nc.vector.tensor_reduce(s0[:, at(g * J, J), :], sprod.rearrange("p j (h d) -> p j h d", h=H),
                                            AX, ALU.add).then_inc(self_scored, 1)
                assert st.n == 2 * (LISTS + 1), st.n
            st.base, st.n = 1 + NG * (LISTS + 1), 0
            for i in range(BETWEEN // 2):
                for k in range(J):
                    find(2 * EARLY + i * J + k, k, NG + i)
                lists(EARLY + 2 * i, 2 * EARLY + (i + 1) * J)

            def stage(t, j):
                nc.vector.tensor_scalar(gidx[:, j, :].unsqueeze(1), keys[:, at(t), 0:CAP], -1.0, float(N),
                                        ALU.mult, ALU.add).then_inc(staged, 1)
                st.mark(nc.vector.tensor_scalar(lim[:, j, :].unsqueeze(1), keys[:, at(t), 0:CAP], LIFT, MASKED,
                                                ALU.mult, ALU.add))

            for j in range(J):
                stage(j, j)
            st.wait()
            dve.wait_ge(self_scored, NG + 2)

            def stats(y, i, ready):
                st.mark(nc.vector.bn_stats(st6[i][:, :], y))
                st.wait()
                apart(dve)
                nc.vector.bn_aggr(mv[i][:, :], st6[i][:, :]).then_inc(ready, 1)

            def norm(dst, y, i, g_b, n_b, ready):
                st.mark(nc.vector.tensor_scalar(dst, y, mv[i][:, 0:1], rstd[i][:, 0:1], ALU.subtract, ALU.mult))
                st.wait()
                st.mark(nc.vector.tensor_tensor(dst, dst, g_b[:, :], ALU.mult))
                st.wait()
                nc.vector.tensor_tensor(dst, dst, n_b[:, :], ALU.add).then_inc(ready, 1)

            def first_norm_stats(t, j):
                dve.wait_ge(ao_done, t + 1)
                dve.wait_ge(x_biased, t + 1)
                nc.vector.tensor_tensor(y1[:, :], ao_p, xr[:, j, :], ALU.add).then_inc(y_done, 1)
                dve.wait_ge(y_done, t + 1 + J)
                stats(y1[:, :], 0, var1_ready)

            def first_norm(t, j):
                dve.wait_ge(rstd1_ready, t + 1)
                dve.wait_ge(h1T_done, t)
                norm(h1[j % 2][:, :], y1[:, :], 0, g1_b, n1_b, h1_ready)
                dve.wait_ge(h1_ready, t + 1)
                st.mark(nc.vector.tensor_tensor(Qs[:, at(t), :], h1[j % 2][:, :].unsqueeze(1), b2_b[:, :].unsqueeze(1), ALU.add))

            def second_norm_pair(t, stored):
                for i in range(2):
                    dve.wait_ge(ff2_done, t + i + 1)
                    nc.vector.tensor_tensor(z2[i][:, :], ff2_p[i], Qs[:, at(t + i), :].rearrange("p o d -> p (o d)"),
                                            ALU.add).then_inc(z_done, 1)
                for i in range(2):
                    dve.wait_ge(z_done, t + i + 1)
                    stats(z2[i][:, :], 1 + i, var2_ready)
                for i in range(2):
                    dve.wait_ge(rstd2_ready, t + i + 1)
                    dve.wait_ge(out_stored[i], stored * 16)
                    norm(ob[i][:, :], z2[i][:, :], 1 + i, g2_b, n2_b, out_ready)

            def step(g, j, search, prev, first=False):
                t = g * J + j
                b = j % 2
                dve.wait_ge(gathered[b], g * (32 * CAP) + (j // 2 + 1) * 16 * CAP)
                st.mark(nc.vector.tensor_tensor(G[b][:, :, 0:D], G[b][:, :, 0:D], Qs[:, at(t), :].to_broadcast([P, CAP, D]), ALU.mult))
                st.mark(nc.vector.tensor_copy(sc[:, 0:1, :], s0[:, at(t), :]))
                st.wait()
                st.mark(nc.vector.tensor_reduce(sc[:, 1:CAP + 1, :], G[b][:, :, 0:D].rearrange("p s (h d) -> p s h d", h=H), AX, ALU.add))
                st.wait()
                st.mark(nc.vector.tensor_tensor(sc[:, 1:CAP + 1, :], sc[:, 1:CAP + 1, :],
                                                lim[:, j, :].unsqueeze(2).to_broadcast([P, CAP, H]), ALU.min))
                st.wait()
                st.mark(nc.vector.tensor_reduce(mx[:, :], sc[:, :, :].rearrange("p s h -> p h s"), AX, ALU.max))
                st.wait()
                nc.vector.tensor_tensor(dsh[:, :, :], sc[:, :, :], mx[:, :].unsqueeze(1).to_broadcast([P, CAP + 1, H]),
                                        ALU.subtract).then_inc(shifted, 1)
                if not first:
                    first_norm_stats(t - 1, (j - 1) % J)
                if search:
                    find(g * J + (2 * (EARLY + BETWEEN) + j), j, g + (NG + 2 * BETWEEN // J))
                if not first:
                    first_norm(t - 1, (j - 1) % J)
                dve.wait_ge(exp_done, t + 1)
                dve.wait_ge(ctx_summed, t + 1)
                st.mark(nc.vector.tensor_reduce(den[:, :], pe_[:, :, :].rearrange("p s h -> p h s"), AX, ALU.add))
                st.wait()
                st.mark(nc.vector.reciprocal(rden[:, :], den[:, :]))
                st.wait()
                st.mark(nc.vector.tensor_tensor(pn[:, :, :], pe_[:, :, :], rden[:, :].unsqueeze(1).to_broadcast([P, CAP + 1, H]), ALU.mult))
                st.wait()
                for dst, src, pw, n in ((wself[:, :].unsqueeze(1), Vs[:, at(t), :], pn[:, 0:1, :], 1),
                                        (G[b][:, :, 0:D], G[b][:, :, D:2 * D], pn[:, 1:CAP + 1, :], CAP)):
                    nc.vector.tensor_tensor(dst.rearrange("p s (h d) -> p s h d", h=H), src.rearrange("p s (h d) -> p s h d", h=H),
                                            pw.unsqueeze(3).to_broadcast([P, n, H, DK]), ALU.mult).then_inc(weighted, 1)
                stage(t + J, j)
                if search and j == J - 1:
                    lists(g * 2 + (EARLY + BETWEEN), g * J + (2 * (EARLY + BETWEEN) + J))
                if prev and j >= 2:
                    second_norm_pair((g - 1) * J + 2 * (j - 2), (g - 1) * 2 + (j - 2))
                st.wait()

            def run(g, search, prev):
                for j in range(J):
                    step(g, j, search, prev, first=(not prev and j == 0))

            TILE = 13
            NORM2 = 4 * 3
            base = st.base + st.n
            st.base, st.n = base, 0
            run(0, True, False)
            base += st.n
            per = TILE * J + LISTS + NORM2
            with dve.Fori(1, GS) as g:
                st.base, st.n = (g - 1) * per + base, 0
                run(g, True, True)
                assert st.n == per, (st.n, per)
            base += (GS - 1) * per

            st.base, st.n = base, 0
            dve.wait_ge(adj_squared, 2 * NT + J)
            st.mark(nc.vector.tensor_tensor(bad[:, :], sq[:, 0:2 * NT:2], sq[:, 1:2 * NT:2], ALU.add))
            st.wait()
            st.mark(nc.vector.tensor_tensor(bad[:, :], bad[:, :], cnt[:, :], ALU.not_equal))
            st.wait()
            nc.vector.tensor_tensor(bad2[:, :].unsqueeze(2), bad[:, :].unsqueeze(2), keys[:, 0:NT, CAP:CAP + 1],
                                    ALU.add).then_inc(bad_ready, 1)
            base += st.n

            per2 = TILE * J + NORM2
            with dve.Fori(GS, NG) as g:
                st.base, st.n = (g - GS) * per2 + base, 0
                run(g, False, True)
                assert st.n == per2, (st.n, per2)
            base += (NG - GS) * per2
            st.base, st.n = base, 0
            first_norm_stats(NT - 1, J - 1)
            first_norm(NT - 1, J - 1)
            dve.wait_ge(bad_summed, 1)
            st.mark(nc.vector.tensor_scalar(tfl[:, :], ctx_p[0][0:1, 0:NT], 0.0, None, ALU.is_gt))
            st.wait()
            st.mark(nc.vector.tensor_reduce(tlist[:, 0:1], tfl[:, :], AX, ALU.add))
            st.mark(nc.vector.tensor_tensor(tkey[:, :], tfl[:, :], tdown[:, :], ALU.mult))
            st.wait()
            for i in range(NT // FOUND):
                st.mark(nc.vector.max(tlist[:, 1 + i * FOUND:1 + (i + 1) * FOUND], tkey[:, :]))
                st.wait()
                if i < NT // FOUND - 1:
                    st.mark(nc.vector.match_replace(tkey[:, :], tlist[:, 1 + i * FOUND:1 + (i + 1) * FOUND], tkey[:, :], 0.0))
                    st.wait()
            st.mark(nc.vector.tensor_scalar(tlist[:, 1:], tlist[:, 1:], -1.0, float(NT), ALU.mult, ALU.add))
            st.wait()
            nc.vector.tensor_copy(flags[:, :], tlist[:, :]).then_inc(flags_ready, 1)
            for i in range(2):
                second_norm_pair((NG - 1) * J + 2 * i, (NG - 1) * 2 + i)
            st.wait()

            dve.wait_ge(flags_ready, 1)
            nf = dve.value_load(flags[0:1, 0:1], min_val=0, max_val=NT)
            with dve.If(nf > 0):
                with dve.Fori(0, nf) as r:
                    fs = Steps(dve, f_step, 0)
                    f = dve.value_load(flags[0:1, at(r + 1, 1)], min_val=0, max_val=NT - 1)
                    fs.base = r * F_STEPS
                    dve.wait_ge(f_in, r * 48 + 48)
                    blk = adjb[:, at(f * P, P)]
                    fs.mark(nc.vector.tensor_tensor(blk, blk, ident[:, :], ALU.add))
                    fs.wait()
                    fs.mark(nc.vector.tensor_scalar(vmask, fadj, 0.0, None, ALU.not_equal))
                    fs.wait()
                    fs.mark(nc.vector.tensor_scalar(pen, vmask, 1.0, -MASKED, ALU.subtract, ALU.mult))
                    fs.wait()
                    dve.wait_ge(f_q, r + 1)
                    for h in range(H):
                        dh = h // J
                        nc.vector.tensor_scalar(qz[:, h, :], ctx_p[1][:, dh * P:(dh + 1) * P], bqT[:, dh:dh + 1],
                                                headmask[:, h % J:h % J + 1], ALU.add, ALU.mult).then_inc(f_qz, 1)
                    for h in range(H):
                        hb = r * (H * NG) + h * NG
                        with dve.Fori(0, NG) as c:
                            dve.wait_ge(f_s, hb + c + 1)
                            nc.vector.scalar_tensor_tensor(S[:, at(c * 512, 512)], fs_p, SCALE, vmask[:, at(c * 512, 512)],
                                                           ALU.mult, ALU.mult).then_inc(f_sread, 1)
                            dve.wait_ge(f_sread, hb + c + 1)
                            nc.vector.tensor_tensor(S[:, at(c * 512, 512)], S[:, at(c * 512, 512)], pen[:, at(c * 512, 512)],
                                                    ALU.add).then_inc(f_step, 1)
                        fs.n += NG
                        fs.wait()
                        fs.mark(nc.vector.tensor_reduce(fmax, S, AX, ALU.max))
                        fs.wait()
                        nc.vector.tensor_scalar(fnmax, fmax, -1.0, None, ALU.mult).then_inc(f_max, 1)
                        dve.wait_ge(f_e, r * H + h + 1)
                        fs.mark(nc.vector.reciprocal(frden, fden))
                        fs.mark(nc.vector.memset(fctx[:, h * DK:(h + 1) * DK], 0.0))
                        fs.wait()
                        apart(dve)
                        with dve.Fori(0, NG) as c:
                            dve.wait_ge(f_t, hb + c)
                            nc.vector.tensor_copy(stg, S[:, at(c * 512, 512)]).then_inc(f_st, 1)
                            dve.wait_ge(f_pv, hb + c + 1)
                            nc.vector.tensor_tensor(fctx[:, h * DK:(h + 1) * DK], fctx[:, h * DK:(h + 1) * DK],
                                                    ctx_p[0][:, 0:DK], ALU.add).then_inc(f_acc, 1)
                            dve.wait_ge(f_acc, hb + c + 1)
                        fs.mark(nc.vector.tensor_scalar(fctx[:, h * DK:(h + 1) * DK], fctx[:, h * DK:(h + 1) * DK],
                                                        frden, None, ALU.mult))
                        fs.wait()
                        apart(dve)
                    nc.vector.tensor_tensor(xr[:, 0, :], xr[:, 0, :], bo_b[:, :], ALU.add).then_inc(f_ctx, 1)
                    dve.wait_ge(f_baton, r * F_TAIL + F_AO)
                    dve.wait_ge(f_ctx, r + 1)
                    fs.mark(nc.vector.tensor_tensor(y1[:, :], ao_p, xr[:, 0, :], ALU.add))
                    fs.wait()
                    fs.mark(nc.vector.bn_stats(st6[0][:, :], y1[:, :]))
                    fs.wait()
                    apart(dve)
                    nc.vector.bn_aggr(mv[0][:, :], st6[0][:, :]).then_inc(f_baton, 1)
                    dve.wait_ge(f_baton, r * F_TAIL + F_RSTD1)
                    fs.mark(nc.vector.tensor_scalar(h1[0][:, :], y1[:, :], mv[0][:, 0:1], rstd[0][:, 0:1], ALU.subtract, ALU.mult))
                    fs.wait()
                    fs.mark(nc.vector.tensor_tensor(h1[0][:, :], h1[0][:, :], g1_b[:, :], ALU.mult))
                    fs.wait()
                    nc.vector.tensor_tensor(h1[0][:, :], h1[0][:, :], n1_b[:, :], ALU.add).then_inc(f_baton, 1)
                    dve.wait_ge(f_baton, r * F_TAIL + F_H1)
                    fs.mark(nc.vector.tensor_tensor(h1[1][:, :], h1[0][:, :], b2_b[:, :], ALU.add))
                    fs.wait()
                    dve.wait_ge(f_baton, r * F_TAIL + F_FF2)
                    fs.mark(nc.vector.tensor_tensor(z2[0][:, :], ff2_p[0], h1[1][:, :], ALU.add))
                    fs.wait()
                    fs.mark(nc.vector.bn_stats(st6[1][:, :], z2[0][:, :]))
                    fs.wait()
                    apart(dve)
                    nc.vector.bn_aggr(mv[1][:, :], st6[1][:, :]).then_inc(f_baton, 1)
                    dve.wait_ge(f_baton, r * F_TAIL + F_RSTD2)
                    dve.wait_ge(f_out, r * 16)
                    dve.wait_ge(out_stored[0], 16 * NT // 2)
                    fs.mark(nc.vector.tensor_scalar(ob[0][:, :], z2[0][:, :], mv[1][:, 0:1], rstd[1][:, 0:1], ALU.subtract, ALU.mult))
                    fs.wait()
                    fs.mark(nc.vector.tensor_tensor(ob[0][:, :], ob[0][:, :], g2_b[:, :], ALU.mult))
                    fs.wait()
                    nc.vector.tensor_tensor(ob[0][:, :], ob[0][:, :], n2_b[:, :], ALU.add).then_inc(f_baton, 1)
                    assert fs.n == F_STEPS, fs.n

        @block.tensor
        def _(pe):
            pe.sem_inc(qkv_done, J)
            pe.sem_inc(ctx_summed, 1)
            pe.wait_ge(wq_in, 48)
            with pe.Fori(0, NG // 2) as i:
                for s in range(2):
                    g = i * 2 + s
                    pe.wait_ge(xT_in[s], i * 16 + 16)
                    for j in range(J):
                        b = j % 2
                        pe.wait_ge(qkv_copied, g * J + j + 1)
                        for c0, c1 in ((0, 2 * D), (2 * D, 3 * D)):
                            for k in range(KD):
                                last = nc.tensor.matmul(qkv_p[b][:, c0:c1], xTb[s][:, k, j * P:(j + 1) * P],
                                                        wqkv[:, k, c0:c1], start=(k == 0), stop=(k == KD - 1))
                        last.then_inc(qkv_done, 1)

            def transpose_h1(t, j):
                pe.wait_ge(h1_ready, t + 1)
                pe.wait_ge(h1T_ready, t)
                for k in range(KD):
                    last = nc.tensor.transpose(h1T_p[:, k * P:(k + 1) * P], h1[j % 2][:, k * P:(k + 1) * P], ident[:, :])
                last.then_inc(h1T_done, 1)

            def ff1(g, c0, c1):
                pe.wait_ge(h1T_ready, g * J + J)
                for c in range(c0, c1):
                    if c >= 2:
                        pe.wait_ge(hid_ready, g * KF + (c - 1))
                    for k in range(KD):
                        last = nc.tensor.matmul(ff1_p[c % 2], w1[:, k, c * P:(c + 1) * P], h1T[:, k, :],
                                                start=(k == 0), stop=(k == KD - 1))
                    last.then_inc(ff1_done, 1)

            def ff2(g, j0):
                pe.wait_ge(hid_ready, g * KF + KF)
                pe.wait_ge(z_done, g * J + j0)
                for i in range(2):
                    for c in range(KF):
                        last = nc.tensor.matmul(ff2_p[i], hid[:, c, (j0 + i) * P:(j0 + i + 1) * P], w2[:, c, :],
                                                start=(c == 0), stop=(c == KF - 1))
                    last.then_inc(ff2_done, 1)

            def step(g, j, prev, first=False):
                t = g * J + j
                if prev and j == 1:
                    ff1(g - 1, KF // 2, KF)
                if prev and j >= 2:
                    ff2(g - 1, 2 * (j - 2))
                if not first:
                    transpose_h1(t - 1, (j - 1) % J)
                if prev and j == 0:
                    ff1(g - 1, 0, KF // 2)
                pe.wait_ge(weighted, t * 2 + 6)
                for k in range(KD):
                    for s in range(CAP + 1):
                        src = G[j % 2][:, s - 1, k * P:(k + 1) * P] if s else wself[:, k * P:(k + 1) * P]
                        last = nc.tensor.matmul(ctx_p[j % 2][:, k * P:(k + 1) * P], src,
                                                ident[:, :], is_transpose=True, start=(s == 0), stop=(s == CAP))
                last.then_inc(ctx_summed, 1)
                pe.wait_ge(ctxT_ready, t + 1)
                pe.wait_ge(y_done, t + J)
                for k in range(KD):
                    last = nc.tensor.matmul(ao_p, ctxT[j % 2][:, k, :], wo[:, k, :], start=(k == 0), stop=(k == KD - 1))
                last.then_inc(ao_done, 1)

            pe.wait_ge(w_in, 48)
            pe.wait_ge(pool_const, 7)
            for j in range(J):
                step(0, j, False, first=(j == 0))
            with pe.Fori(1, NG) as g:
                for j in range(J):
                    step(g, j, True)
            pe.wait_ge(bad_ready, 1)
            nc.tensor.matmul(ctx_p[0][0:1, 0:NT], onesc[:, 0:1], bad2[:, :], start=True, stop=True).then_inc(bad_summed, 1)
            transpose_h1(NT - 1, J - 1)
            ff1(NG - 1, 0, KF)
            ff2(NG - 1, 0)
            ff2(NG - 1, 2)

            pe.wait_ge(flags_ready, 1)
            nf = pe.value_load(flags[0:1, 0:1], min_val=0, max_val=NT)
            with pe.If(nf > 0):
                pe.wait_ge(out_ready, NT)
                with pe.Fori(0, NG) as c:
                    pe.wait_ge(f_w, 48)
                    pe.wait_ge(f_x, c * 16 + 16)
                    for dh in range(KD):
                        for k in range(KD):
                            last = nc.tensor.matmul(ff1_p[dh], fw[:, k, dh * P:(dh + 1) * P], fxT[:, k, :],
                                                    start=(k == 0), stop=(k == KD - 1))
                        last.then_inc(f_ktmm, 1)
                with pe.Fori(0, nf) as r:
                    pe.wait_ge(f_in, r * 48 + 48)
                    pe.wait_ge(f_w, r * 48 + 96)
                    pe.wait_ge(f_baton, r * F_TAIL)
                    for dh in range(KD):
                        for k in range(KD):
                            last = nc.tensor.matmul(ctx_p[1][:, dh * P:(dh + 1) * P], fw[:, k, 2 * D + dh * P:2 * D + (dh + 1) * P],
                                                    fx[:, k, :], start=(k == 0), stop=(k == KD - 1))
                    last.then_inc(f_q, 1)
                    pe.wait_ge(f_qz, r * H + H)
                    pe.wait_ge(f_kt, KD * NG)
                    apart(pe)
                    for h in range(H):
                        hb = r * (H * NG) + h * NG
                        with pe.Fori(0, NG) as c:
                            pe.wait_ge(f_sread, hb + c)
                            nc.tensor.matmul(fs_p, qz[:, h, :], KT[:, h // J, at(c * 512, 512)], start=True, stop=True).then_inc(f_s, 1)
                        with pe.Fori(0, NG) as c:
                            pe.wait_ge(f_st, hb + c + 1)
                            pe.wait_ge(f_pt, hb + c)
                            for i in range(J):
                                last = nc.tensor.transpose(ff1_p[0][:, i * P:(i + 1) * P], stg[:, i * P:(i + 1) * P], ident[:, :])
                            last.then_inc(f_t, 1)
                            pe.wait_ge(f_pt, hb + c + 1)
                            pe.wait_ge(f_acc, hb + c)
                            for i in range(J):
                                last = nc.tensor.matmul(ctx_p[0][:, 0:DK], PT[:, i, :],
                                                        Vs[:, at(c * J + i), h * DK:(h + 1) * DK].rearrange("p o d -> p (o d)"),
                                                        start=(i == 0), stop=(i == J - 1))
                            last.then_inc(f_pv, 1)
                    pe.wait_ge(f_ctx, r + 1)
                    for k in range(KD):
                        last = nc.tensor.transpose(ctx_p[0][:, k * P:(k + 1) * P], fctx[:, k * P:(k + 1) * P], ident[:, :])
                    last.then_inc(f_baton, 1)
                    pe.wait_ge(f_baton, r * F_TAIL + F_CTXT)
                    for k in range(KD):
                        last = nc.tensor.matmul(ao_p, ctxT[0][:, k, :], wo[:, k, :], start=(k == 0), stop=(k == KD - 1))
                    last.then_inc(f_baton, 1)
                    pe.wait_ge(f_baton, r * F_TAIL + F_H1)
                    for k in range(KD):
                        last = nc.tensor.transpose(h1T_p[:, k * P:(k + 1) * P], h1[0][:, k * P:(k + 1) * P], ident[:, :])
                    last.then_inc(f_baton, 1)
                    for c in range(KF):
                        pe.wait_ge(f_baton, r * F_TAIL + F_FF + 2 * c)
                        for k in range(KD):
                            last = nc.tensor.matmul(ff1_p[c % 2][:, 0:P], w1[:, k, c * P:(c + 1) * P], h1T[:, k, 0:P],
                                                    start=(k == 0), stop=(k == KD - 1))
                        last.then_inc(f_baton, 1)
                    pe.wait_ge(f_baton, r * F_TAIL + F_FF + 2 * KF)
                    for c in range(KF):
                        last = nc.tensor.matmul(ff2_p[0], hid[:, c, 0:P], w2[:, c, :], start=(c == 0), stop=(c == KF - 1))
                    last.then_inc(f_baton, 1)


def kernel(**inputs):
    import numpy as np
    import concourse.bacc as bacc
    from concourse.bass_utils import run_bass_kernel_spmd

    nc = bacc.Bacc("TRN2", target_bir_lowering=False, num_devices=1)
    arrays = {}

    def given(name, transposed=False):
        a = np.asarray(inputs[name])
        a = np.ascontiguousarray(a.T if transposed else a)
        key = f"in_{name}_T" if transposed else f"in_{name}"
        arrays[key] = a
        return nc.dram_tensor(key, a.shape, mybir.dt.from_np(a.dtype), kind="ExternalInput").ap()

    p = "L0_gnn_"
    args = [given("x"), given("x", True), given("adj")]
    for m, b in (("Wq", "bq"), ("Wk", "bk"), ("Wv", "bv"), ("Wo", "bo"), ("W1", "b1"), ("W2", "b2")):
        args += [given(p + m, True), given(p + b)]
    args += [given(p + n) for n in ("ln1_g", "ln1_b", "ln2_g", "ln2_b")]
    n, d = inputs["x"].shape
    kv = nc.dram_tensor("kv", (n, 2 * d), mybir.dt.float32, kind="Internal").ap()
    out = nc.dram_tensor("out_rows", (n, d), mybir.dt.float32, kind="ExternalOutput").ap()
    build(nc, *args, kv, out)
    return run_bass_kernel_spmd(nc, [arrays], core_ids=[0]).results[0]["out_rows"]
```

```python
import concourse.bass as bass
from concourse import mybir
from contextlib import ExitStack


def build(nc, x, xT, adj, WqT, bq, WkT, bk, WvT, bv, WoT, bo, W1T, b1, W2T, b2, g1, n1, g2, n2, kv, qd, out):
    F32, I32, U32, U8 = mybir.dt.float32, mybir.dt.int32, mybir.dt.uint32, mybir.dt.uint8
    ALU, ACT, AX = mybir.AluOpType, mybir.ActivationFunctionType, mybir.AxisListType.X

    P = 128
    N, D = x.shape
    FF = W1T.shape[1]
    H = 8
    DK = D // H
    NT = N // P
    J = 4
    NG = NT // J
    KD = D // P
    KF = FF // P
    HALF = N // 2
    FOUND = 8
    LIST = 2 * FOUND
    CAP = 5
    HCAP = 2 * CAP
    KEYS = LIST + 1
    UW = HALF + FOUND
    SCALE = float(DK) ** -0.5
    EPS = 1e-5
    MASKED = -1e9
    LIFT = 8e34
    EARLY = 16
    BETWEEN = 4
    GS = (NT - EARLY - BETWEEN) // 2
    F1A = 3

    def at(i, n=1):
        return slice(i, i + n) if isinstance(i, int) else bass.DynSlice(i, n)

    ctx = ExitStack()
    with ctx:
        def sb(name, shape, dt=F32):
            return ctx.enter_context(nc.sbuf_tensor(name, shape, dt))

        def sem(name):
            return ctx.enter_context(nc.semaphore(name))

        wo = sb("wo", [P, KD, D])
        w1 = sb("w1", [P, KD, FF])
        w2 = sb("w2", [P, KF, D])
        g1_b, n1_b, nb2, g2_b, n2_b = (sb(n, [P, D]) for n in ("g1_b", "n1_b", "nb2", "g2_b", "n2_b"))
        bo_r = sb("bo_r", [1, D])
        b1_c = sb("b1_c", [P, KF])
        bkT, bqT, bvT, g1T, n1T = (sb(n, [P, KD]) for n in ("bkT", "bqT", "bvT", "g1T", "n1T"))
        ident = sb("ident", [P, P])
        upper = sb("upper", [P, P])
        ones_pp = sb("ones_pp", [P, P])
        rank_row = sb("rank_row", [P, P])
        ones8 = sb("ones8", [P, FOUND])
        eps_c = sb("eps_c", [P, 1])
        selfkey = sb("selfkey", [P, NT])
        headmask = sb("headmask", [P, J])

        adjb = sb("adjb", [P, J * UW], I32)
        sqjunk = sb("sqjunk", [P, HALF], U8)
        Qs = sb("Qs", [P, NT, D])
        Vs = sb("Vs", [P, NT, D])
        s0 = sb("s0", [P, NT, H])
        keys = sb("keys", [P, NT + J, KEYS])
        sq = sb("sq", [P, 2 * NT])
        cnt = sb("cnt", [P, NT])
        GW = CAP * 2 * D
        gbuf = sb("gbuf", [P, J * GW])
        G = [gbuf[:, i * GW:(i + 1) * GW].rearrange("p (s d) -> p s d", s=CAP) for i in range(J)]
        wself = sb("wself", [P, D])
        hh = sb("hh", [P, (KF + KD) * J * P])
        hid = hh[:, 0:KF * J * P].rearrange("p (c n) -> p c n", c=KF)
        h1T = hh[:, KF * J * P:(KF + KD) * J * P].rearrange("p (k n) -> p k n", k=KD)
        xTb = [gbuf[:, i * 1024:(i + 1) * 1024].rearrange("p (k n) -> p k n", k=KD) for i in range(2)]
        kst = [gbuf[:, 2048 + i * 1024:3072 + i * 1024].rearrange("p (j d) -> p j d", j=J) for i in range(2)]
        tmp = [gbuf[:, 4096 + i * 512:4608 + i * 512] for i in range(2)]
        sprod = gbuf[:, 5120:6144].rearrange("p (j d) -> p j d", j=J)
        wkqv = hh[:, 0:1536].rearrange("p (k n) -> p k n", k=KD)
        bkq = hh[:, 1536:2048]
        xr = sb("xr", [P, J, D])
        ctxT = [sb(f"ctxT{i}", [P, KD, P]) for i in range(2)]
        y1 = [sb(f"y1_{i}", [P, D]) for i in range(2)]
        nh = [sb(f"nh{i}", [P, D]) for i in range(2)]
        z2 = [sb(f"z2_{i}", [P, D]) for i in range(2)]
        ob = [sb(f"ob{i}", [P, D]) for i in range(2)]
        st6 = [sb(f"st6_{i}", [P, 6]) for i in range(5)]
        mv = [sb(f"mv{i}", [P, 2]) for i in range(5)]
        nmean, lnv, rstd, shift = ([sb(f"{n}{i}", [P, 1]) for i in range(5)] for n in ("nmean", "lnv", "rstd", "shift"))
        raw = sb("raw", [P, 2, LIST], U32)
        neg = sb("neg", [P, 2, LIST])
        off = sb("off", [P, 2, FOUND])
        hit = sb("hit", [P, 2, LIST])
        val = sb("val", [P, 2, LIST])
        ne = sb("ne", [P, 2, LIST])
        val2 = sb("val2", [P, 2, LIST])
        top = sb("top", [P, 2, LIST])
        gidx = sb("gidx", [P, J, CAP], U32)
        lim = sb("lim", [P, J, CAP])
        sc = sb("sc", [P, HCAP + 1, H])
        mx = sb("mx", [P, H])
        dsh = sb("dsh", [P, HCAP + 1, H])
        pe_ = sb("pe_", [P, HCAP + 1, H])
        den = sb("den", [P, H])
        rden = sb("rden", [P, H])
        pn = sb("pn", [P, HCAP + 1, H])
        hkey = sb("hkey", [P, KEYS])
        hidx = sb("hidx", [P, HCAP + 1], U32)
        hlim = sb("hlim", [P, HCAP])
        tfl = sb("tfl", [1, NT])
        tkey = sb("tkey", [1, NT])
        tdown = sb("tdown", [1, NT])
        tlist = sb("tlist", [1, NT + 1])
        flags = sb("flags", [1, NT + 1], I32)

        tail = adjb[:, 0:4096].bitcast(F32)
        t_hid = tail[:, 0:1024].rearrange("p (c n) -> p c n", c=KF)
        t_h1T = tail[:, 1024:1280].rearrange("p (k n) -> p k n", k=KD)
        t_nh, t_res, t_z, t_ob, t_y = (tail[:, 1280 + i * D:1280 + (i + 1) * D] for i in range(5))
        over, sums_a, sums_b = (tail[:, 2560 + i * 2 * NT:2560 + (i + 1) * 2 * NT] for i in range(3))
        none, place, bad, bad2 = (tail[:, 2560 + i * NT:2560 + (i + 1) * NT] for i in range(6, 10))
        onehot = adjb[:, 4096:8192].bitcast(F32).rearrange("p (t n) -> p t n", t=NT)
        hself = G[2][:, 0, :]
        hq, hx = G[2][:, 1, 0:D], G[2][:, 2, 0:D]

        KT = Qs[:, :, :].rearrange("p t d -> p (t d)").rearrange("p (k n) -> p k n", k=KD)
        S = gbuf[:, 0:N]
        vmask = gbuf[:, N:2 * N]
        fadj = adjb[:, 0:N]
        pen = adjb[:, N:2 * N].bitcast(F32)
        qz = hh[:, 0:1024].rearrange("p (h n) -> p h n", h=H)
        stg = hh[:, 1024:1536]
        PT = hh[:, 1536:2048].rearrange("p (c n) -> p c n", c=J)
        fw = hh[:, 2048:3584].rearrange("p (k n) -> p k n", k=KD)
        fxT = h1T
        fctx = z2[1]
        fx = ctxT[1]
        fsm = sb("fsm", [P, 4])
        fmax, fnmax, fden, frden = (fsm[:, i:i + 1] for i in range(4))

        ps = [ctx.enter_context(nc.psum_tensor(f"ps{i}", [P, 1024], F32)) for i in range(4)]
        qkv_p = ps[0:2]
        ff1_p = [ps[0][:, 0:512], ps[0][:, 512:1024]]
        fs_p = ps[1][:, 0:512]
        ff2_p = [ps[1][:, 0:D], ps[1][:, 512:512 + D]]
        ctx_p = [ps[2][:, 0:D], ps[2][:, 512:512 + D]]
        ao_p = ps[3][:, 0:D]
        h1T_p = ps[3][:, 512:512 + D]
        rank_p = ps[3][:, D:D + NT]
        bad_p = ps[2][0:1, 512:512 + NT]
        hkey_p = ps[3][:, D + NT:D + NT + KEYS]

        w_in = sem("w_in"); wq_in = sem("wq_in"); bias_in = sem("bias_in"); norm_in = sem("norm_in"); colb_in = sem("colb_in")
        pool_const = sem("pool_const"); dve_const = sem("dve_const")
        adj_in = [sem(f"adj_in{i}") for i in range(J)]
        adj_scanned = sem("adj_scanned"); adj_squared = sem("adj_squared")
        xT_in = [sem(f"xT_in{i}") for i in range(2)]
        qkv_done = sem("qkv_done"); kq_copied = sem("kq_copied"); v_ready = sem("v_ready")
        k_ready = sem("k_ready"); q_ready = sem("q_ready")
        self_scored = sem("self_scored"); k_stored = [sem(f"k_stored{i}") for i in range(2)]; v_stored = sem("v_stored")
        q_stored = sem("q_stored")
        staged = sem("staged"); gathered = [sem(f"gathered{i}") for i in range(J)]
        shifted = sem("shifted"); exp_done = sem("exp_done"); weighted = sem("weighted")
        ctx_summed = sem("ctx_summed"); ctxT_ready = sem("ctxT_ready"); ao_done = sem("ao_done")
        x_in = [sem(f"x_in{i}") for i in range(J)]
        y_done = sem("y_done"); var1_ready = sem("var1_ready"); nh_ready = sem("nh_ready")
        h1T_done = sem("h1T_done"); h1T_ready = sem("h1T_ready"); res_ready = sem("res_ready")
        ff1_done = sem("ff1_done"); hid_ready = sem("hid_ready"); ff2_done = sem("ff2_done"); z_done = sem("z_done")
        var2_ready = sem("var2_ready"); normed2 = sem("normed2")
        out_ready = sem("out_ready"); out_stored = [sem(f"out_stored{i}") for i in range(2)]
        carried = sem("carried"); dstep = sem("dstep"); astep = sem("astep"); pstep = sem("pstep")
        over_ready = sem("over_ready"); ranked = sem("ranked"); onehot_ready = sem("onehot_ready")
        hkey_done = sem("hkey_done"); h_idx = sem("h_idx"); h_gathered = sem("h_gathered")
        h_shifted = sem("h_shifted"); h_exp = sem("h_exp"); h_weighted = sem("h_weighted"); h_stored = sem("h_stored")
        bad_ready = sem("bad_ready"); bad_summed = sem("bad_summed"); flags_ready = sem("flags_ready")
        baton = sem("baton"); t_ff1 = sem("t_ff1"); t_relu = sem("t_relu"); t_resd = sem("t_resd")
        t_step = sem("t_step"); t_act = sem("t_act"); t_pool = sem("t_pool")
        f_w = sem("f_w"); f_x = sem("f_x"); f_ktmm = sem("f_ktmm"); f_kt = sem("f_kt"); f_in = sem("f_in"); f_q = sem("f_q")
        f_qz = sem("f_qz"); f_s = sem("f_s"); f_sread = sem("f_sread"); f_max = sem("f_max"); f_e = sem("f_e")
        f_st = sem("f_st"); f_t = sem("f_t"); f_pt = sem("f_pt"); f_pv = sem("f_pv"); f_acc = sem("f_acc")
        f_step = sem("f_step"); f_out = sem("f_out"); f_ctx = sem("f_ctx")

        xT_v = xT.rearrange("(k p) n -> p k n", p=P)
        kv_rows = kv.rearrange("(t p) c -> p t c", p=P)
        q_rows = qd.rearrange("(t p) c -> p t c", p=P)

        def apart(eng):
            eng.sem_inc(carried, 1)

        class Steps:
            def __init__(self, eng, s, base=0):
                self.eng, self.s, self.base, self.n = eng, s, base, 0

            def mark(self, ins):
                ins.then_inc(self.s, 1)
                self.n += 1

            def wait(self):
                self.eng.wait_ge(self.s, self.base + self.n)

        B_CTX = 1
        B_CTXT = B_CTX + KD
        B_AO, B_VAR1, B_NH, B_T = range(B_CTXT + 1, B_CTXT + 5)
        B_H1T = B_T + KD
        B_FF2, B_VAR2, B_N2, B_OUT = range(B_H1T + 1, B_H1T + 5)
        F_STEPS = 3 + H * (NG + 4)
        T_DVE, T_ACT, T_POOL = 6, 6, 2

        block = ctx.enter_context(nc.Block())

        @block.sync
        def _(sp):
            def load_unit(u_tile, half, b, k):
                sp.wait_ge(adj_scanned, k + 1)
                sp.wait_ge(adj_squared, k + 1)
                sp.dma_start(adjb[:, b * UW:b * UW + HALF],
                             adj[at(u_tile * P, P), half * HALF:(half + 1) * HALF]).then_inc(adj_in[b], 16)

            def load_wkqv(dst, s):
                for wT, c in ((WkT, 0), (WqT, 1), (WvT, 2)):
                    sp.dma_start(dst[:, :, c * D:(c + 1) * D], wT.rearrange("(k p) n -> p k n", p=P)).then_inc(s, 16)

            def load_xT(g, b, k):
                sp.wait_ge(qkv_done, k * J + J)
                sp.dma_start(xTb[b], xT_v[:, :, at(g * J * P, J * P)]).then_inc(xT_in[b], 16)

            def store_kv(g, b):
                sp.wait_ge(k_ready, g * J + J + 2)
                sp.dma_start(kv_rows[:, at(g * J, J), 0:D], kst[b]).then_inc(k_stored[b], 16)
                sp.wait_ge(v_ready, g * J + J + 2)
                sp.dma_start(kv_rows[:, at(g * J, J), D:2 * D], Vs[:, at(g * J, J), :]).then_inc(v_stored, 16)

            load_wkqv(wkqv, wq_in)
            load_xT(0, 0, 0)

            def group(g, s, first=False, last=False):
                if first:
                    load_xT(1, 1, 0)
                elif not last:
                    load_xT(g + 1, 1 - s, g)
                for k in range(J):
                    load_unit(g * 2 + k // 2, k % 2, k, g * J + k)
                    if k == 1 and not first:
                        store_kv(g - 1, 1 - s)
                if first:
                    with nc.allow_non_contiguous_dma("per-partition biases"):
                        for dst, b, s in ((bkT, bk, k_stored[0]), (bqT, bq, k_stored[1]), (bvT, bv, f_out)):
                            sp.dma_start(dst[:, :], b.rearrange("(c p) -> p c", p=P)).then_inc(s, 16)
                    for i, (dst, b) in enumerate(((g2_b, g2), (n2_b, n2))):
                        sp.dma_start(dst[:, :], b.partition_broadcast(P)).then_inc(out_stored[i], 16)

            group(0, 0, first=True)
            group(1, 1)
            with sp.Fori(1, NG // 2 - 1) as i:
                for s in range(2):
                    group(i * 2 + s, s)
            group(NG - 2, 0)
            group(NG - 1, 1, last=True)
            for k in range(2 * BETWEEN):
                load_unit(EARLY + k // 2, k % 2, k % J, 2 * EARLY + k)
                if k == 1:
                    store_kv(NG - 1, 1)

            def step(g, j, search, prev):
                sp.wait_ge(y_done, g * J + j + 1)
                sp.dma_start(xr[:, j, :], x[at((g * J + j) * P, P), :]).then_inc(x_in[j], 16)
                if j == 0:
                    sp.wait_ge(q_ready, NT + 2)
                    sp.dma_start(q_rows[:, at(g * J, J), :], Qs[:, at(g * J, J), :]).then_inc(q_stored, 16)
                if search:
                    load_unit(g * 2 + (EARLY + BETWEEN + j // 2), j % 2, j, g * J + (2 * (EARLY + BETWEEN) + j))
                if prev and j < 2:
                    store_pair((g - 2) * J + 2 * j)

            def store_pair(t):
                for i in range(2):
                    sp.wait_ge(out_ready, t + i + 1)
                    sp.dma_start(out[at((t + i) * P, P), :], ob[i][:, :]).then_inc(out_stored[i], 16)

            for g in range(2):
                for j in range(J):
                    step(g, j, True, False)
            with sp.Fori(2, GS) as g:
                for j in range(J):
                    step(g, j, True, True)
            with sp.Fori(GS, NG) as g:
                for j in range(J):
                    step(g, j, False, True)
            for t in range((NG - 2) * J, NT, 2):
                store_pair(t)
            sp.wait_ge(h_stored, 16)

            sp.wait_ge(flags_ready, 1)
            nf = sp.value_load(flags[0:1, 0:1], min_val=0, max_val=NT)
            with sp.If(nf > 0):
                load_wkqv(fw, f_w)
                with sp.Fori(0, NG) as c:
                    sp.wait_ge(f_kt, c * KD + KD)
                    sp.dma_start(fxT, xT_v[:, :, at(c * 512, 512)]).then_inc(f_x, 16)
                with sp.Fori(0, nf) as r:
                    f = sp.value_load(flags[0:1, at(r + 1, 1)], min_val=0, max_val=NT - 1)
                    sp.wait_ge(f_kt, KD * NG + KD)
                    sp.wait_ge(f_out, r * 16 + 16)
                    sp.dma_start(fadj, adj[at(f * P, P), :]).then_inc(f_in, 16)
                    load_wkqv(fw, f_w)
                    sp.dma_start(fx[:, :, :], xT_v[:, :, at(f * P, P)]).then_inc(f_in, 16)
                    sp.dma_start(xr[:, 0, :], x[at(f * P, P), :]).then_inc(f_in, 16)
                    sp.wait_ge(baton, r * B_OUT + 2 * B_OUT)
                    sp.dma_start(out[at(f * P, P), :], t_ob).then_inc(f_out, 16)
                    sp.wait_ge(f_out, r * 16 + 32)
                    apart(sp)

        @block.gpsimd
        def _(pool):
            for s in (k_ready, q_ready, res_ready):
                pool.sem_inc(s, 2)
            nc.gpsimd.memset(ident[:, :], 0.0).then_inc(pool_const, 1)
            nc.gpsimd.memset(upper[:, :], 1.0).then_inc(pool_const, 1)
            nc.gpsimd.memset(headmask[:, :], 1.0).then_inc(pool_const, 1)
            for dst, step_, base, chan in ((selfkey, -P, N, -1), (tdown, -1, NT, 0), (rank_row, 1, 0, 0)):
                nc.gpsimd.iota(dst[:, :], pattern=[[step_, dst.shape[1]]], base=base, channel_multiplier=chan,
                               allow_small_or_imprecise_dtypes=True).then_inc(pool_const, 1)
            pool.wait_ge(pool_const, 6)
            nc.gpsimd.affine_select(out=ident[:, :], in_=ident[:, :], compare_op=ALU.not_equal, fill=1.0,
                                    base=0, pattern=[[-1, P]], channel_multiplier=1).then_inc(pool_const, 1)
            nc.gpsimd.affine_select(out=upper[:, :], in_=upper[:, :], compare_op=ALU.is_ge, fill=0.0,
                                    base=-1, pattern=[[1, P]], channel_multiplier=-1).then_inc(pool_const, 1)
            nc.gpsimd.affine_select(out=headmask[:, :], in_=headmask[:, :], compare_op=ALU.is_ge, fill=0.0,
                                    base=0, pattern=[[-DK, J]], channel_multiplier=1).then_inc(pool_const, 1)
            pool.wait_ge(pool_const, 9)
            nc.gpsimd.affine_select(out=headmask[:, :], in_=headmask[:, :], compare_op=ALU.is_ge, fill=0.0,
                                    base=DK - 1, pattern=[[DK, J]], channel_multiplier=-1).then_inc(pool_const, 1)

            pool.wait_ge(bias_in, 16 * 2)
            with pool.Fori(0, NG // 2) as i:
                for s in range(2):
                    g = i * 2 + s
                    pool.wait_ge(self_scored, g + 1)
                    pool.wait_ge(k_stored[s], i * 16 + 16)
                    for j in range(J):
                        t = g * J + j
                        pool.wait_ge(kq_copied, t + 3)
                        nc.gpsimd.tensor_tensor(kst[s][:, j, :], tmp[j % 2][:, 0:D], bkq[:, 0:D],
                                                ALU.add).then_inc(k_ready, 1)
                        nc.gpsimd.tensor_tensor(Qs[:, at(t), :], tmp[j % 2][:, D:2 * D].unsqueeze(1),
                                                bkq[:, D:2 * D].unsqueeze(1), ALU.add).then_inc(q_ready, 1)

            pst = Steps(pool, pstep)
            pool.wait_ge(norm_in, 16 * 3)
            pst.mark(nc.gpsimd.tensor_tensor(nb2[:, :], n1_b[:, :], nb2[:, :], ALU.add))
            pst.wait()

            for s in range(2):
                pool.wait_ge(k_stored[s], 16 * NG // 2 + 16)
            pool.wait_ge(v_stored, 16 * NG)
            pool.wait_ge(self_scored, NG + 2)
            pool.wait_ge(q_ready, NT + 2)
            pool.wait_ge(dve_const, 3)

            def gather(dst, src, idx, done):
                pool.indirect_dma_start(out=dst, out_offset=None, in_=src,
                                        in_offset=bass.IndirectOffsetOnAxis(ap=idx, axis=0),
                                        bounds_check=N - 1, oob_is_err=False).then_inc(done, 16)

            def gathers(g, j):
                t = g * J + j
                pool.wait_ge(staged, t + 1)
                pool.wait_ge(ctx_summed, t + 1)
                apart(pool)
                for s in range(CAP):
                    gather(G[j][:, s, :], kv[:, :], gidx[:, j, s:s + 1], gathered[j])

            def residual(g, j, t):
                pool.wait_ge(nh_ready, t + 3)
                pool.wait_ge(q_stored, g * 16 + 16)
                apart(pool)
                row = Qs[:, at(t), :]
                pst.mark(nc.gpsimd.tensor_tensor(row, nh[j % 2][:, :].unsqueeze(1), g1_b[:, :].unsqueeze(1), ALU.mult))
                pst.wait()
                apart(pool)
                nc.gpsimd.tensor_tensor(row, row, nb2[:, :].unsqueeze(1), ALU.add).then_inc(res_ready, 1)

            def out_pair(t):
                for i in range(2):
                    pool.wait_ge(normed2, t + i + 3)
                    pst.mark(nc.gpsimd.tensor_tensor(ob[i][:, :], ob[i][:, :], g2_b[:, :], ALU.mult))
                    pst.wait()
                    nc.gpsimd.tensor_tensor(ob[i][:, :], ob[i][:, :], n2_b[:, :], ALU.add).then_inc(out_ready, 1)

            def step(g, j, res, outs):
                gathers(g, j)
                if res:
                    residual(g if j == 3 else g - 1, (j + 1) % J, g * J + j - 3)
                if outs and j < 2:
                    out_pair((g - 2) * J + 2 * j)

            pool.wait_ge(out_stored[0], 16)
            pool.wait_ge(out_stored[1], 16)
            for g in range(2):
                for j in range(J):
                    step(g, j, g > 0 or j == 3, False)
            base, pst.n, per = pst.n, 0, J + 4
            with pool.Fori(2, NG) as g:
                pst.base, pst.n = (g - 2) * per + base, 0
                for j in range(J):
                    step(g, j, True, True)
                assert pst.n == per, pst.n
            pst.base, pst.n = base + (NG - 2) * per, 0

            pool.wait_ge(h_idx, 3)
            pool.wait_ge(q_stored, 16 * NG)
            for i in range(2):
                pool.wait_ge(ctx_summed, NT - 4 + i + 1 + J)
                for s in range(CAP):
                    gather(G[i][:, s, :], kv[:, :], hidx[:, i * CAP + s:i * CAP + s + 1], h_gathered)
                residual(NG - 1, (i + 1) % J, NT - 3 + i)
                if i == 0:
                    out_pair((NG - 2) * J)
            pool.wait_ge(ctx_summed, NT - 1 + J)
            me = hidx[:, HCAP:HCAP + 1]
            gather(hself, kv[:, :], me, h_gathered)
            gather(hq, qd[:, :], me, h_gathered)
            gather(hx, x[:, :], me, h_gathered)
            out_pair((NG - 2) * J + 2)
            residual(NG - 1, J - 1, NT - 1)

            def rest(r, parts):
                ts = Steps(pool, t_pool, r * T_POOL)
                if "residual" in parts:
                    pool.wait_ge(baton, r * B_OUT + B_NH)
                    ts.mark(nc.gpsimd.tensor_tensor(t_res, t_nh, g1_b[:, :], ALU.mult))
                    ts.wait()
                    nc.gpsimd.tensor_tensor(t_res, t_res, nb2[:, :], ALU.add).then_inc(t_resd, 1)
                if "out" in parts:
                    ts.n = 1
                    pool.wait_ge(baton, r * B_OUT + B_N2)
                    ts.mark(nc.gpsimd.tensor_tensor(t_ob, t_ob, g2_b[:, :], ALU.mult))
                    ts.wait()
                    nc.gpsimd.tensor_tensor(t_ob, t_ob, n2_b[:, :], ALU.add).then_inc(baton, 1)

            out_pair((NG - 1) * J)
            rest(0, ("residual",))
            out_pair((NG - 1) * J + 2)
            rest(0, ("out",))
            for i in range(2):
                pool.wait_ge(out_stored[i], 16 * NT // 2 + 16)
            pool.wait_ge(baton, B_OUT)
            pool.indirect_dma_start(out=out[:, :], out_offset=bass.IndirectOffsetOnAxis(ap=me, axis=0), in_=t_ob,
                                    in_offset=None, bounds_check=N - 1, oob_is_err=False).then_inc(h_stored, 16)
            pool.wait_ge(h_stored, 16)

            pool.wait_ge(flags_ready, 1)
            nf = pool.value_load(flags[0:1, 0:1], min_val=0, max_val=NT)
            with pool.If(nf > 0):
                with pool.Fori(0, nf) as r:
                    rest(r + 1, ("residual", "out"))

        @block.scalar
        def _(act):
            nc.scalar.preload_act_table_set("natural_log_exp_and_others")
            act.sem_inc(adj_squared, J)
            act.sem_inc(h1T_ready, KD)
            act.sem_inc(f_kt, KD)
            act.sem_inc(f_pt, 1)
            for s in (kq_copied, v_ready, nh_ready, normed2):
                act.sem_inc(s, 2)
            for c, b in enumerate((bk, bq)):
                act.dma_start(bkq[:, c * D:(c + 1) * D], b.partition_broadcast(P)).then_inc(bias_in, 16)
            for dst, b in ((g1_b, g1), (n1_b, n1), (nb2, b2)):
                act.dma_start(dst[:, :], b.partition_broadcast(P)).then_inc(norm_in, 16)
            act.dma_start(wo[:, :, :], WoT.rearrange("(k p) n -> p k n", p=P)).then_inc(w_in, 16)
            act.dma_start(w1[:, :, :], W1T.rearrange("(k p) n -> p k n", p=P)).then_inc(w_in, 16)
            act.dma_start(w2[:, :, :], W2T.rearrange("(k p) n -> p k n", p=P)).then_inc(w_in, 16)
            act.dma_start(bo_r[:, :], bo.unsqueeze(0)).then_inc(w_in, 16)
            with nc.allow_non_contiguous_dma("per-partition biases"):
                act.dma_start(b1_c[:, :], b1.rearrange("(c p) -> p c", p=P)).then_inc(colb_in, 16)
                act.dma_start(g1T[:, :], g1.rearrange("(c p) -> p c", p=P)).then_inc(colb_in, 16)
                act.dma_start(n1T[:, :], n1.rearrange("(c p) -> p c", p=P)).then_inc(colb_in, 16)

            def square(k, b, visit):
                act.wait_ge(adj_in[b], visit * 16 + 16)
                act.wait_ge(adj_squared, k + J)
                nc.scalar.activation(sqjunk[:, :], adjb[:, b * UW:b * UW + HALF], ACT.Square,
                                     accum_out=sq[:, at(k)]).then_inc(adj_squared, 1)

            def copy_qkv(t, b):
                act.wait_ge(qkv_done, t + 1 + J)
                act.wait_ge(q_ready, t + 1)
                act.wait_ge(k_ready, t + 1)
                nc.scalar.copy(tmp[b], qkv_p[b][:, 0:2 * D]).then_inc(kq_copied, 1)
                nc.scalar.copy(Vs[:, at(t), :], qkv_p[b][:, 2 * D:3 * D].unsqueeze(1)).then_inc(v_ready, 1)

            with act.Fori(0, NG // 2) as i:
                for s in range(2):
                    g = i * 2 + s
                    for j in range(J):
                        copy_qkv(g * J + j, j % 2)
                        square(g * J + j, j, g)
            for k in range(2 * BETWEEN):
                square(2 * EARLY + k, k % J, NG + k // J)

            act.wait_ge(colb_in, 48)
            act.wait_ge(dve_const, 3)
            act.wait_ge(k_stored[0], 16)
            act.wait_ge(k_stored[1], 16)
            act.wait_ge(f_out, 16)

            def normalize(st, i, dst, y):
                st.mark(nc.scalar.activation(lnv[i][:, :], mv[i][:, 1:2], ACT.Ln, bias=eps_c[:, 0:1]))
                st.wait()
                st.mark(nc.scalar.activation(rstd[i][:, :], lnv[i][:, :], ACT.Exp, scale=-0.5))
                st.wait()
                st.mark(nc.scalar.activation(shift[i][:, :], nmean[i][:, :], ACT.Identity, scale=rstd[i][:, 0:1]))
                st.wait()
                return nc.scalar.activation(dst, y, ACT.Identity, scale=rstd[i][:, 0:1], bias=shift[i][:, 0:1])

            def relu(c, n):
                act.wait_ge(ff1_done, n + 1)
                nc.scalar.activation(hid[:, c, :], ff1_p[c % 2], ACT.Relu, bias=b1_c[:, c:c + 1]).then_inc(hid_ready, 1)

            def first_norm(t, i):
                act.wait_ge(var1_ready, t + 1)
                act.wait_ge(h1T_done, t + 1)
                act.wait_ge(res_ready, t + 1)
                normalize(ast, i, nh[i][:, :], y1[i][:, :]).then_inc(nh_ready, 1)

            def second_norms(t, pairs):
                for i in range(2):
                    act.wait_ge(var2_ready, t + i + 1)
                    act.wait_ge(out_stored[i], pairs * 16 + 16)
                    normalize(ast, 2 + i, ob[i][:, :], z2[i][:, :]).then_inc(normed2, 1)

            def copy_h1T(j, t):
                act.wait_ge(h1T_done, t + 3)
                for k in range(KD):
                    nc.scalar.activation(h1T[:, k, j * P:(j + 1) * P], h1T_p[:, k * P:(k + 1) * P], ACT.Identity,
                                         scale=g1T[:, k:k + 1], bias=n1T[:, k:k + 1]).then_inc(h1T_ready, 1)

            def copy_ctxT(i, src, done):
                for k in range(KD):
                    nc.scalar.activation(ctxT[i][:, k, :], src[:, k * P:(k + 1) * P], ACT.Identity,
                                         bias=bvT[:, k:k + 1]).then_inc(done, 1)

            ast = Steps(act, astep)

            def step(g, j, search, prev, first=False):
                t = g * J + j
                if prev and j == 1:
                    for c in range(F1A, F1A + 2):
                        relu(c, (g - 1) * KF + c)
                act.wait_ge(shifted, t + 1)
                nc.scalar.activation(pe_[:, 0:CAP + 1, :], dsh[:, 0:CAP + 1, :], ACT.Exp, scale=SCALE).then_inc(exp_done, 1)
                if prev and j == 1:
                    relu(F1A + 2, (g - 1) * KF + F1A + 2)
                if not first:
                    first_norm(t - 1, (j - 1) % 2)
                if prev and j == 1:
                    for c in range(F1A + 3, KF):
                        relu(c, (g - 1) * KF + c)
                if search:
                    square(g * J + (2 * (EARLY + BETWEEN) + j), j, g + (NG + 2 * BETWEEN // J))
                if not first:
                    copy_h1T((j - 1) % J, t - 1)
                if prev and j == 0:
                    for c in range(F1A):
                        relu(c, (g - 1) * KF + c)
                act.wait_ge(ctx_summed, t + 1 + J)
                copy_ctxT(j % 2, ctx_p[j % 2], ctxT_ready)
                if prev and j >= 2:
                    second_norms((g - 1) * J + 2 * (j - 2), (g - 1) * 2 + (j - 2))

            for j in range(J):
                step(0, j, True, False, first=j == 0)
            base, ast.n, per = ast.n, 0, J * 3 + 4 * 3
            with act.Fori(1, GS) as g:
                ast.base, ast.n = (g - 1) * per + base, 0
                for j in range(J):
                    step(g, j, True, True)
                assert ast.n == per, ast.n
            with act.Fori(GS, NG) as g:
                ast.base, ast.n = (g - 1) * per + base, 0
                for j in range(J):
                    step(g, j, False, True)
                assert ast.n == per, ast.n
            ast.base, ast.n = base + (NG - 1) * per, 0

            def rest(r, parts):
                ts = Steps(act, t_act, r * T_ACT)
                if "context" in parts:
                    act.wait_ge(baton, r * B_OUT + B_CTX)
                    copy_ctxT(0, ctx_p[0], baton)
                if "norm1" in parts:
                    act.wait_ge(baton, r * B_OUT + B_VAR1)
                    normalize(ts, 4, t_nh, t_y).then_inc(baton, 1)
                if "feed" in parts:
                    act.wait_ge(baton, r * B_OUT + B_T)
                    for k in range(KD):
                        nc.scalar.activation(t_h1T[:, k, :], h1T_p[:, k * P:(k + 1) * P], ACT.Identity,
                                             scale=g1T[:, k:k + 1], bias=n1T[:, k:k + 1]).then_inc(baton, 1)
                    for c in range(KF):
                        act.wait_ge(t_ff1, r * KF + c + 1)
                        nc.scalar.activation(t_hid[:, c, :], ff1_p[c % 2][:, 0:P], ACT.Relu,
                                             bias=b1_c[:, c:c + 1]).then_inc(t_relu, 1)
                if "norm2" in parts:
                    ts.n = 3
                    act.wait_ge(baton, r * B_OUT + B_VAR2)
                    normalize(ts, 4, t_ob, t_z).then_inc(baton, 1)

            last = (NG - 1) * J
            first_norm(NT - 1, (J - 1) % 2)
            copy_h1T(J - 1, NT - 1)
            for c in range(KF):
                relu(c, (NG - 1) * KF + c)
                if c == J - 1:
                    act.wait_ge(h_shifted, 1)
                    nc.scalar.activation(pe_[:, :, :], dsh[:, :, :], ACT.Exp, scale=SCALE).then_inc(h_exp, 1)
            rest(0, ("context",))
            second_norms(last, (NG - 1) * 2)
            rest(0, ("norm1",))
            second_norms(last + 2, (NG - 1) * 2 + 1)
            rest(0, ("feed", "norm2"))

            act.wait_ge(flags_ready, 1)
            nf = act.value_load(flags[0:1, 0:1], min_val=0, max_val=NT)
            with act.If(nf > 0):
                act.wait_ge(h_stored, 16)
                with act.Fori(0, NG) as c:
                    for dh in range(KD):
                        act.wait_ge(f_ktmm, c * KD + dh + 1)
                        nc.scalar.activation(KT[:, dh, at(c * 512, 512)], ff1_p[dh], ACT.Identity,
                                             bias=bkT[:, dh:dh + 1]).then_inc(f_kt, 1)
                with act.Fori(0, nf) as r:
                    for h in range(H):
                        act.wait_ge(f_max, r * H + h + 1)
                        nc.scalar.activation(S, S, ACT.Exp, bias=fnmax, accum_out=fden).then_inc(f_e, 1)
                        with act.Fori(0, NG) as c:
                            act.wait_ge(f_t, r * (H * NG) + h * NG + c + 2)
                            act.wait_ge(f_pv, r * (H * NG) + h * NG + c + 1)
                            nc.scalar.copy(PT, ff1_p[0].rearrange("p (c n) -> p c n", c=J)).then_inc(f_pt, 1)
                    rest(r + 1, ("context", "norm1", "feed", "norm2"))

        @block.vector
        def _(dve):
            nc.vector.memset(ones8[:, :], 1.0).then_inc(dve_const, 1)
            nc.vector.memset(ones_pp[:, :], 1.0).then_inc(dve_const, 1)
            nc.vector.memset(eps_c[:, :], EPS).then_inc(dve_const, 1)
            st = Steps(dve, dstep)
            for b in range(J):
                nc.vector.memset(adjb[:, b * UW + HALF:(b + 1) * UW], 1).then_inc(adj_scanned, 1)
            st.mark(nc.vector.memset(gbuf[:, 6144:], 0.0))
            st.mark(nc.vector.memset(keys[:, NT:NT + J, :], 0.0))
            for s, n in ((self_scored, 2), (z_done, 2), (y_done, J), (f_sread, 1), (f_acc, 1)):
                dve.sem_inc(s, n)
            dve.wait_ge(pool_const, 10)
            st.mark(nc.vector.tensor_copy(keys[:, 0:NT, LIST:KEYS], selfkey[:, :].unsqueeze(2)))
            dve.wait_ge(dve_const, 3)
            st.wait()

            def find(k, b, visit):
                dve.wait_ge(adj_in[b], visit * 16 + 16)
                apart(dve)
                i = b // 2
                nc.vector.max_index(raw[:, i, (b % 2) * FOUND:(b % 2 + 1) * FOUND], ones8[:, :],
                                    adjb[:, b * UW:(b + 1) * UW]).then_inc(adj_scanned, 1)

            def lists(t, k):
                dve.wait_ge(adj_scanned, k + J)
                st.mark(nc.vector.tensor_scalar(neg[:, :, :], raw[:, :, :], float(HALF), 0.0, ALU.subtract, ALU.min))
                st.wait()
                st.mark(nc.vector.tensor_scalar(off[:, :, :], neg[:, :, 0:FOUND], 0.0, float(HALF), ALU.is_lt, ALU.mult))
                st.mark(nc.vector.tensor_scalar(val[:, :, FOUND:LIST], neg[:, :, FOUND:LIST], -1.0, None, ALU.mult))
                st.mark(nc.vector.tensor_scalar(hit[:, :, :], neg[:, :, :], 0.0, None, ALU.is_lt))
                st.wait()
                st.mark(nc.vector.tensor_tensor(val[:, :, 0:FOUND], off[:, :, :], neg[:, :, 0:FOUND], ALU.subtract))
                st.mark(nc.vector.tensor_reduce(cnt[:, at(t, 2)], hit[:, :, :], AX, ALU.add))
                st.wait()
                st.mark(nc.vector.tensor_tensor(ne[:, :, :], val[:, :, :],
                                                selfkey[:, at(t, 2)].unsqueeze(2).to_broadcast([P, 2, LIST]), ALU.not_equal))
                st.wait()
                st.mark(nc.vector.tensor_tensor(val[:, :, :], val[:, :, :], ne[:, :, :], ALU.mult))
                st.wait()
                apart(dve)
                for i in range(2):
                    st.mark(nc.vector.max(top[:, i, 0:FOUND], val[:, i, :]))
                st.wait()
                apart(dve)
                for i in range(2):
                    st.mark(nc.vector.match_replace(val2[:, i, :], top[:, i, 0:FOUND], val[:, i, :], 0.0))
                st.wait()
                apart(dve)
                for i in range(2):
                    st.mark(nc.vector.max(top[:, i, FOUND:LIST], val2[:, i, :]))
                st.wait()
                st.mark(nc.vector.tensor_copy(keys[:, at(t, 2), 0:LIST], top[:, :, :]))
                st.wait()

            LISTS = 15
            first_steps = st.n
            with dve.Fori(0, NG // 2) as i:
                st.base, st.n = i * (2 * (LISTS + 1)) + first_steps, 0
                for s in range(2):
                    g = i * 2 + s
                    for k in range(J):
                        find(g * J + k, k, g)
                    lists(g * 2, g * J + J)
                    dve.wait_ge(k_ready, g * J + J + 2)
                    dve.wait_ge(q_ready, g * J + J + 2)
                    st.mark(nc.vector.tensor_tensor(sprod, kst[s], Qs[:, at(g * J, J), :], ALU.mult))
                    st.wait()
                    nc.vector.tensor_reduce(s0[:, at(g * J, J), :], sprod.rearrange("p j (h d) -> p j h d", h=H),
                                            AX, ALU.add).then_inc(self_scored, 1)
                assert st.n == 2 * (LISTS + 1), st.n
            st.base, st.n = first_steps + NG * (LISTS + 1), 0
            for i in range(BETWEEN // 2):
                for k in range(J):
                    find(2 * EARLY + i * J + k, k, NG + i)
                lists(EARLY + 2 * i, 2 * EARLY + (i + 1) * J)

            def stage(t, j):
                nc.vector.tensor_scalar(gidx[:, j, :].unsqueeze(1), keys[:, at(t), 0:CAP], -1.0, float(N),
                                        ALU.mult, ALU.add).then_inc(staged, 1)
                st.mark(nc.vector.tensor_scalar(lim[:, j, :].unsqueeze(1), keys[:, at(t), 0:CAP], LIFT, MASKED,
                                                ALU.mult, ALU.add))

            for j in range(J):
                stage(j, j)
            st.wait()
            dve.wait_ge(self_scored, NG + 2)

            def stats(st, y, i, done):
                st.mark(nc.vector.bn_stats(st6[i][:, :], y))
                st.wait()
                apart(dve)
                st.mark(nc.vector.bn_aggr(mv[i][:, :], st6[i][:, :]))
                st.wait()
                nc.vector.tensor_scalar(nmean[i][:, :], mv[i][:, 0:1], -1.0, None, ALU.mult).then_inc(done, 1)

            def heads(rows):
                return rows.rearrange("p s (h d) -> p s h d", h=H)

            def scores_less_max(blocks, own, n, done):
                for s0_, k_rows, q_row, limits in blocks:
                    m = k_rows.shape[1]
                    st.mark(nc.vector.tensor_tensor(k_rows, k_rows, q_row.to_broadcast([P, m, D]), ALU.mult))
                own()
                st.wait()
                for s0_, k_rows, q_row, limits in blocks:
                    m = k_rows.shape[1]
                    st.mark(nc.vector.tensor_reduce(sc[:, s0_:s0_ + m, :], heads(k_rows), AX, ALU.add))
                st.wait()
                for s0_, k_rows, q_row, limits in blocks:
                    m = k_rows.shape[1]
                    if limits is not None:
                        st.mark(nc.vector.tensor_tensor(sc[:, s0_:s0_ + m, :], sc[:, s0_:s0_ + m, :],
                                                        limits.unsqueeze(2).to_broadcast([P, m, H]), ALU.min))
                st.wait()
                st.mark(nc.vector.tensor_reduce(mx[:, :], sc[:, 0:n, :].rearrange("p s h -> p h s"), AX, ALU.max))
                st.wait()
                nc.vector.tensor_tensor(dsh[:, 0:n, :], sc[:, 0:n, :], mx[:, :].unsqueeze(1).to_broadcast([P, n, H]),
                                        ALU.subtract).then_inc(done, 1)

            def weigh(blocks, n, done):
                st.mark(nc.vector.tensor_reduce(den[:, :], pe_[:, 0:n, :].rearrange("p s h -> p h s"), AX, ALU.add))
                st.wait()
                st.mark(nc.vector.reciprocal(rden[:, :], den[:, :]))
                st.wait()
                st.mark(nc.vector.tensor_tensor(pn[:, 0:n, :], pe_[:, 0:n, :], rden[:, :].unsqueeze(1).to_broadcast([P, n, H]), ALU.mult))
                st.wait()
                for s0_, v_rows, dst in blocks:
                    m = v_rows.shape[1]
                    nc.vector.tensor_tensor(heads(dst), heads(v_rows), pn[:, s0_:s0_ + m, :].unsqueeze(3).to_broadcast([P, m, H, DK]),
                                            ALU.mult).then_inc(done, 1)

            def first_norm_stats(t, j):
                dve.wait_ge(ao_done, t + 1)
                dve.wait_ge(x_in[j], (t - j) // J * 16 + 16 if isinstance(t, int) else (t - j) * (16 // J) + 16)
                dve.wait_ge(nh_ready, t + 1)
                nc.vector.tensor_tensor(y1[j % 2][:, :], ao_p, xr[:, j, :], ALU.add).then_inc(y_done, 1)
                dve.wait_ge(y_done, t + 1 + J)
                stats(st, y1[j % 2][:, :], j % 2, var1_ready)

            def second_norm_stats(t):
                for i in range(2):
                    dve.wait_ge(ff2_done, t + i + 1)
                    dve.wait_ge(res_ready, t + i + 3)
                    dve.wait_ge(normed2, t + i + 1)
                    nc.vector.tensor_tensor(z2[i][:, :], ff2_p[i], Qs[:, at(t + i), :].rearrange("p o d -> p (o d)"),
                                            ALU.add).then_inc(z_done, 1)
                for i in range(2):
                    dve.wait_ge(z_done, t + i + 3)
                    stats(st, z2[i][:, :], 2 + i, var2_ready)

            def step(g, j, search, prev, first=False):
                t = g * J + j
                dve.wait_ge(gathered[j], g * (16 * CAP) + 16 * CAP)
                scores_less_max([(1, G[j][:, :, 0:D], Qs[:, at(t), :], lim[:, j, :])],
                                lambda: st.mark(nc.vector.tensor_copy(sc[:, 0:1, :], s0[:, at(t), :])), CAP + 1, shifted)
                if not first:
                    first_norm_stats(t - 1, (j - 1) % J)
                if search:
                    find(g * J + (2 * (EARLY + BETWEEN) + j), j, g + (NG + 2 * BETWEEN // J))
                dve.wait_ge(exp_done, t + 1)
                dve.wait_ge(ctx_summed, t + J)
                weigh([(0, Vs[:, at(t), :], wself[:, :].unsqueeze(1)), (1, G[j][:, :, D:2 * D], G[j][:, :, 0:D])], CAP + 1, weighted)
                stage(t + J, j)
                if search and j == J - 1:
                    lists(g * 2 + (EARLY + BETWEEN), g * J + (2 * (EARLY + BETWEEN) + J))
                if prev and j >= 2:
                    second_norm_stats((g - 1) * J + 2 * (j - 2))
                st.wait()

            def run(g, search, prev):
                for j in range(J):
                    step(g, j, search, prev, first=(not prev and j == 0))

            TILE = 11
            base = st.base + st.n
            st.base, st.n = base, 0
            run(0, True, False)
            base += st.n
            per = TILE * J + LISTS + 4 * 2
            with dve.Fori(1, GS) as g:
                st.base, st.n = (g - 1) * per + base, 0
                run(g, True, True)
                assert st.n == per, (st.n, per)
            base += (GS - 1) * per

            st.base, st.n = base, 0
            over_now = over[:, NT:2 * NT]
            dve.wait_ge(adj_squared, 2 * NT + J)
            for b in (over, sums_a, sums_b):
                st.mark(nc.vector.memset(b[:, 0:NT], 0.0))
            st.mark(nc.vector.tensor_scalar(over_now.unsqueeze(2), keys[:, 0:NT, CAP:CAP + 1], 0.0, None, ALU.is_gt))
            st.wait()
            src, dst = over, sums_a
            for k in range(5):
                sh = 1 << k
                st.mark(nc.vector.tensor_tensor(dst[:, NT:2 * NT], src[:, NT:2 * NT], src[:, NT - sh:2 * NT - sh], ALU.add))
                st.wait()
                src, dst = (dst, sums_b) if dst is sums_a else (dst, sums_a)
            assert src is sums_a and 1 << 5 == NT
            nc.vector.tensor_scalar(none[:, :], over_now, 0.0, float(N), ALU.is_equal, ALU.mult).then_inc(over_ready, 1)
            dve.wait_ge(over_ready, 1)
            dve.wait_ge(ranked, 1)
            st.mark(nc.vector.tensor_tensor(place[:, :], rank_p, none[:, :], ALU.add))
            st.wait()
            st.mark(nc.vector.tensor_scalar(bad2[:, :], place[:, :], float(P), None, ALU.is_ge))
            st.mark(nc.vector.tensor_tensor(bad[:, :], sq[:, 0:2 * NT:2], sq[:, 1:2 * NT:2], ALU.add))
            st.wait()
            st.mark(nc.vector.tensor_tensor(bad2[:, :], bad2[:, :], over_now, ALU.mult))
            st.mark(nc.vector.tensor_tensor(bad[:, :], bad[:, :], cnt[:, :], ALU.not_equal))
            st.wait()
            st.mark(nc.vector.tensor_tensor(bad[:, :].unsqueeze(2), bad[:, :].unsqueeze(2), keys[:, 0:NT, HCAP:HCAP + 1], ALU.add))
            st.wait()
            nc.vector.tensor_tensor(bad2[:, :], bad2[:, :], bad[:, :], ALU.add).then_inc(bad_ready, 1)
            for c in range(J):
                n = NT // J
                nc.vector.tensor_tensor(onehot[:, c * n:(c + 1) * n, :], rank_row[:, :].unsqueeze(1).to_broadcast([P, n, P]),
                                        place[:, c * n:(c + 1) * n].unsqueeze(2).to_broadcast([P, n, P]),
                                        ALU.is_equal).then_inc(onehot_ready, 1)
            dve.wait_ge(bad_summed, 1)
            st.mark(nc.vector.tensor_scalar(tfl[:, :], bad_p, 0.0, None, ALU.is_gt))
            st.wait()
            st.mark(nc.vector.tensor_reduce(tlist[:, 0:1], tfl[:, :], AX, ALU.add))
            st.mark(nc.vector.tensor_tensor(tkey[:, :], tfl[:, :], tdown[:, :], ALU.mult))
            st.wait()
            for i in range(NT // FOUND):
                st.mark(nc.vector.max(tlist[:, 1 + i * FOUND:1 + (i + 1) * FOUND], tkey[:, :]))
                st.wait()
                if i < NT // FOUND - 1:
                    st.mark(nc.vector.match_replace(tkey[:, :], tlist[:, 1 + i * FOUND:1 + (i + 1) * FOUND], tkey[:, :], 0.0))
                    st.wait()
            st.mark(nc.vector.tensor_scalar(tlist[:, 1:], tlist[:, 1:], -1.0, float(NT), ALU.mult, ALU.add))
            st.wait()
            nc.vector.tensor_copy(flags[:, :], tlist[:, :]).then_inc(flags_ready, 1)
            dve.wait_ge(hkey_done, 1)
            st.mark(nc.vector.tensor_copy(hkey[:, :], hkey_p))
            st.wait()
            for d0, s0_, n in ((0, 0, HCAP), (HCAP, LIST, 1)):
                nc.vector.tensor_scalar(hidx[:, d0:d0 + n], hkey[:, s0_:s0_ + n], -1.0, float(N), ALU.mult,
                                        ALU.add).then_inc(h_idx, 1)
            nc.vector.tensor_scalar(hlim[:, :], hkey[:, 0:HCAP], LIFT, MASKED, ALU.mult, ALU.add).then_inc(h_idx, 1)
            base += st.n

            per2 = TILE * J + 4 * 2
            with dve.Fori(GS, NG) as g:
                st.base, st.n = (g - GS) * per2 + base, 0
                run(g, False, True)
                assert st.n == per2, (st.n, per2)
            base += (NG - GS) * per2
            st.base, st.n = base, 0
            first_norm_stats(NT - 1, J - 1)

            dve.wait_ge(h_idx, 3)
            dve.wait_ge(h_gathered, 16 * (HCAP + 3))
            q_row = hq.unsqueeze(1)
            scores_less_max([(1, G[0][:, :, 0:D], q_row, hlim[:, 0:CAP]), (1 + CAP, G[1][:, :, 0:D], q_row, hlim[:, CAP:HCAP]),
                             (0, hself[:, 0:D].unsqueeze(1), q_row, None)], lambda: None, HCAP + 1, h_shifted)
            dve.wait_ge(h_exp, 1)
            dve.wait_ge(ctx_summed, NT + J)
            weigh([(0, hself[:, D:2 * D].unsqueeze(1), wself[:, :].unsqueeze(1)), (1, G[0][:, :, D:2 * D], G[0][:, :, 0:D]),
                   (1 + CAP, G[1][:, :, D:2 * D], G[1][:, :, 0:D])], HCAP + 1, h_weighted)

            def rest(r, parts, rows):
                ts = Steps(dve, t_step, r * T_DVE)
                if "norm1" in parts:
                    dve.wait_ge(baton, r * B_OUT + B_AO)
                    ts.mark(nc.vector.tensor_tensor(t_y, ao_p, rows, ALU.add))
                    ts.wait()
                    stats(ts, t_y, 4, baton)
                if "norm2" in parts:
                    ts.n = 3
                    dve.wait_ge(baton, r * B_OUT + B_FF2)
                    dve.wait_ge(t_resd, r + 1)
                    ts.mark(nc.vector.tensor_tensor(t_z, ff2_p[0], t_res, ALU.add))
                    ts.wait()
                    stats(ts, t_z, 4, baton)

            second_norm_stats((NG - 1) * J)
            rest(0, ("norm1",), hx)
            second_norm_stats((NG - 1) * J + 2)
            rest(0, ("norm2",), hx)

            nf = dve.value_load(flags[0:1, 0:1], min_val=0, max_val=NT)
            with dve.If(nf > 0):
                dve.wait_ge(h_stored, 16)
                with dve.Fori(0, nf) as r:
                    fs = Steps(dve, f_step, 0)
                    f = dve.value_load(flags[0:1, at(r + 1, 1)], min_val=0, max_val=NT - 1)
                    fs.base = r * F_STEPS
                    dve.wait_ge(f_in, r * 48 + 48)
                    blk = adjb[:, at(f * P, P)]
                    fs.mark(nc.vector.tensor_tensor(blk, blk, ident[:, :], ALU.add))
                    fs.wait()
                    fs.mark(nc.vector.tensor_scalar(vmask, fadj, 0.0, None, ALU.not_equal))
                    fs.wait()
                    fs.mark(nc.vector.tensor_scalar(pen, vmask, 1.0, -MASKED, ALU.subtract, ALU.mult))
                    fs.wait()
                    dve.wait_ge(f_q, r + 1)
                    for h in range(H):
                        dh = h // J
                        nc.vector.tensor_scalar(qz[:, h, :], ctx_p[1][:, dh * P:(dh + 1) * P], bqT[:, dh:dh + 1],
                                                headmask[:, h % J:h % J + 1], ALU.add, ALU.mult).then_inc(f_qz, 1)
                    for h in range(H):
                        hb = r * (H * NG) + h * NG
                        with dve.Fori(0, NG) as c:
                            dve.wait_ge(f_s, hb + c + 1)
                            nc.vector.scalar_tensor_tensor(S[:, at(c * 512, 512)], fs_p, SCALE, vmask[:, at(c * 512, 512)],
                                                           ALU.mult, ALU.mult).then_inc(f_sread, 1)
                            dve.wait_ge(f_sread, hb + c + 2)
                            nc.vector.tensor_tensor(S[:, at(c * 512, 512)], S[:, at(c * 512, 512)], pen[:, at(c * 512, 512)],
                                                    ALU.add).then_inc(f_step, 1)
                        fs.n += NG
                        fs.wait()
                        fs.mark(nc.vector.tensor_reduce(fmax, S, AX, ALU.max))
                        fs.wait()
                        nc.vector.tensor_scalar(fnmax, fmax, -1.0, None, ALU.mult).then_inc(f_max, 1)
                        dve.wait_ge(f_e, r * H + h + 1)
                        fs.mark(nc.vector.reciprocal(frden, fden))
                        fs.mark(nc.vector.memset(fctx[:, h * DK:(h + 1) * DK], 0.0))
                        fs.wait()
                        apart(dve)
                        with dve.Fori(0, NG) as c:
                            dve.wait_ge(f_t, hb + c + 1)
                            nc.vector.tensor_copy(stg, S[:, at(c * 512, 512)]).then_inc(f_st, 1)
                            dve.wait_ge(f_pv, hb + c + 2)
                            nc.vector.tensor_tensor(fctx[:, h * DK:(h + 1) * DK], fctx[:, h * DK:(h + 1) * DK],
                                                    ctx_p[0][:, 0:DK], ALU.add).then_inc(f_acc, 1)
                            dve.wait_ge(f_acc, hb + c + 2)
                        fs.mark(nc.vector.tensor_scalar(fctx[:, h * DK:(h + 1) * DK], fctx[:, h * DK:(h + 1) * DK],
                                                        frden, None, ALU.mult))
                        fs.wait()
                        apart(dve)
                    dve.sem_inc(f_ctx, 1)
                    assert fs.n == F_STEPS, fs.n
                    rest(r + 1, ("norm1", "norm2"), xr[:, 0, :])

        @block.tensor
        def _(pe):
            for s, n in ((qkv_done, J), (ctx_summed, J), (h1T_done, 2), (f_t, 1), (f_pv, 1)):
                pe.sem_inc(s, n)
            pe.wait_ge(wq_in, 48)
            with pe.Fori(0, NG // 2) as i:
                for s in range(2):
                    g = i * 2 + s
                    pe.wait_ge(xT_in[s], i * 16 + 16)
                    for j in range(J):
                        b = j % 2
                        pe.wait_ge(kq_copied, g * J + j + 1)
                        pe.wait_ge(v_ready, g * J + j + 1)
                        for c0, c1 in ((0, 2 * D), (2 * D, 3 * D)):
                            for k in range(KD):
                                last = nc.tensor.matmul(qkv_p[b][:, c0:c1], xTb[s][:, k, j * P:(j + 1) * P],
                                                        wkqv[:, k, c0:c1], start=(k == 0), stop=(k == KD - 1))
                        last.then_inc(qkv_done, 1)

            def transpose_first(src, t):
                pe.wait_ge(h1T_ready, t * KD + KD)
                for k in range(KD):
                    last = nc.tensor.transpose(h1T_p[:, k * P:(k + 1) * P], src[:, k * P:(k + 1) * P], ident[:, :])
                return last

            def transpose_h1(t, j):
                pe.wait_ge(nh_ready, t + 3)
                transpose_first(nh[j % 2], t).then_inc(h1T_done, 1)

            def ff1(g, c0, c1):
                pe.wait_ge(h1T_ready, g * (J * KD) + (J * KD + KD))
                for c in range(c0, c1):
                    if c >= 2:
                        pe.wait_ge(hid_ready, g * KF + (c - 1))
                    for k in range(KD):
                        last = nc.tensor.matmul(ff1_p[c % 2], w1[:, k, c * P:(c + 1) * P], h1T[:, k, :],
                                                start=(k == 0), stop=(k == KD - 1))
                    last.then_inc(ff1_done, 1)

            def ff2(g, j0):
                pe.wait_ge(hid_ready, g * KF + KF)
                pe.wait_ge(z_done, g * J + (j0 + 2))
                for i in range(2):
                    for c in range(KF):
                        last = nc.tensor.matmul(ff2_p[i], hid[:, c, (j0 + i) * P:(j0 + i + 1) * P], w2[:, c, :],
                                                start=(c == 0), stop=(c == KF - 1))
                    last.then_inc(ff2_done, 1)

            def sum_transposed(dst, rows):
                for k in range(KD):
                    for i, src in enumerate(rows):
                        last = nc.tensor.matmul(dst[:, k * P:(k + 1) * P], src[:, k * P:(k + 1) * P], ident[:, :],
                                                is_transpose=True, start=(i == 0), stop=(i == len(rows) - 1))
                return last

            def project_out(src):
                nc.tensor.matmul(ao_p, ones_pp[0:1, :], bo_r[:, :], start=True, stop=False)
                for k in range(KD):
                    last = nc.tensor.matmul(ao_p, src[:, k, :], wo[:, k, :], start=False, stop=(k == KD - 1))
                return last

            def step(g, j, prev, first=False):
                t = g * J + j
                if prev and j == 1:
                    ff1(g - 1, F1A, KF)
                if prev and j >= 2:
                    ff2(g - 1, 2 * (j - 2))
                if not first:
                    transpose_h1(t - 1, (j - 1) % J)
                if prev and j == 0:
                    ff1(g - 1, 0, F1A)
                pe.wait_ge(weighted, t * 2 + 2)
                sum_transposed(ctx_p[j % 2], [wself[:, :]] + [G[j][:, s, 0:D] for s in range(CAP)]).then_inc(ctx_summed, 1)
                pe.wait_ge(ctxT_ready, t * KD + KD)
                pe.wait_ge(y_done, t + J)
                project_out(ctxT[j % 2]).then_inc(ao_done, 1)

            pe.wait_ge(w_in, 64)
            pe.wait_ge(pool_const, 10)
            pe.wait_ge(dve_const, 3)
            for j in range(J):
                step(0, j, False, first=(j == 0))
            with pe.Fori(1, GS) as g:
                for j in range(J):
                    step(g, j, True)
            pe.wait_ge(over_ready, 1)
            nc.tensor.matmul(rank_p, upper[:, :], over[:, NT:2 * NT], start=True, stop=False)
            nc.tensor.matmul(rank_p, ones_pp[:, :], sums_a[:, NT - 1:2 * NT - 1], start=False, stop=True).then_inc(ranked, 1)
            pe.wait_ge(bad_ready, 1)
            nc.tensor.matmul(bad_p, ones_pp[:, 0:1], bad2[:, :], start=True, stop=True).then_inc(bad_summed, 1)
            for t in range(NT):
                pe.wait_ge(onehot_ready, t // (NT // J) + 1)
                last = nc.tensor.matmul(hkey_p, onehot[:, t, :], keys[:, t, :], start=(t == 0), stop=(t == NT - 1))
            last.then_inc(hkey_done, 1)
            with pe.Fori(GS, NG) as g:
                for j in range(J):
                    step(g, j, True)

            def rest(r, parts, ao_free=None, h1T_free=None):
                if "norm1" in parts:
                    pe.wait_ge(baton, r * B_OUT + B_CTXT)
                    project_out(ctxT[0]).then_inc(baton, 1)
                if "feed" in parts:
                    pe.wait_ge(baton, r * B_OUT + B_NH)
                    for k in range(KD):
                        last = nc.tensor.transpose(h1T_p[:, k * P:(k + 1) * P], t_nh[:, k * P:(k + 1) * P], ident[:, :])
                    last.then_inc(baton, 1)
                    pe.wait_ge(baton, r * B_OUT + B_H1T)
                    for c in range(KF):
                        if c >= 2:
                            pe.wait_ge(t_relu, r * KF + c - 1)
                        for k in range(KD):
                            last = nc.tensor.matmul(ff1_p[c % 2][:, 0:P], w1[:, k, c * P:(c + 1) * P], t_h1T[:, k, :],
                                                    start=(k == 0), stop=(k == KD - 1))
                        last.then_inc(t_ff1, 1)
                    pe.wait_ge(t_relu, r * KF + KF)
                    for c in range(KF):
                        last = nc.tensor.matmul(ff2_p[0], t_hid[:, c, :], w2[:, c, :], start=(c == 0), stop=(c == KF - 1))
                    last.then_inc(baton, 1)

            transpose_h1(NT - 1, J - 1)
            ff1(NG - 1, 0, KF)
            pe.wait_ge(h_weighted, 3)
            sum_transposed(ctx_p[0], [wself[:, :]] + [G[i][:, s, 0:D] for i in range(2) for s in range(CAP)]).then_inc(baton, 1)
            ff2(NG - 1, 0)
            pe.wait_ge(y_done, NT + J)
            rest(0, ("norm1",))
            ff2(NG - 1, 2)
            pe.wait_ge(h1T_ready, NT * KD + KD)
            pe.wait_ge(z_done, NT + 1)
            rest(0, ("feed",))

            pe.wait_ge(flags_ready, 1)
            nf = pe.value_load(flags[0:1, 0:1], min_val=0, max_val=NT)
            with pe.If(nf > 0):
                pe.wait_ge(h_stored, 16)
                with pe.Fori(0, NG) as c:
                    pe.wait_ge(f_w, 48)
                    pe.wait_ge(f_x, c * 16 + 16)
                    for dh in range(KD):
                        for k in range(KD):
                            last = nc.tensor.matmul(ff1_p[dh], fw[:, k, dh * P:(dh + 1) * P], fxT[:, k, :],
                                                    start=(k == 0), stop=(k == KD - 1))
                        last.then_inc(f_ktmm, 1)
                with pe.Fori(0, nf) as r:
                    pe.wait_ge(f_in, r * 48 + 48)
                    pe.wait_ge(f_w, r * 48 + 96)
                    pe.wait_ge(baton, r * B_OUT + B_OUT)
                    for dh in range(KD):
                        for k in range(KD):
                            last = nc.tensor.matmul(ctx_p[1][:, dh * P:(dh + 1) * P], fw[:, k, D + dh * P:D + (dh + 1) * P],
                                                    fx[:, k, :], start=(k == 0), stop=(k == KD - 1))
                    last.then_inc(f_q, 1)
                    pe.wait_ge(f_qz, r * H + H)
                    pe.wait_ge(f_kt, KD * NG + KD)
                    apart(pe)
                    for h in range(H):
                        hb = r * (H * NG) + h * NG
                        with pe.Fori(0, NG) as c:
                            pe.wait_ge(f_sread, hb + c + 1)
                            nc.tensor.matmul(fs_p, qz[:, h, :], KT[:, h // J, at(c * 512, 512)], start=True, stop=True).then_inc(f_s, 1)
                        with pe.Fori(0, NG) as c:
                            pe.wait_ge(f_st, hb + c + 1)
                            pe.wait_ge(f_pt, hb + c + 1)
                            for i in range(J):
                                last = nc.tensor.transpose(ff1_p[0][:, i * P:(i + 1) * P], stg[:, i * P:(i + 1) * P], ident[:, :])
                            last.then_inc(f_t, 1)
                            pe.wait_ge(f_pt, hb + c + 2)
                            pe.wait_ge(f_acc, hb + c + 1)
                            for i in range(J):
                                last = nc.tensor.matmul(ctx_p[0][:, 0:DK], PT[:, i, :],
                                                        Vs[:, at(c * J + i), h * DK:(h + 1) * DK].rearrange("p o d -> p (o d)"),
                                                        start=(i == 0), stop=(i == J - 1))
                            last.then_inc(f_pv, 1)
                    pe.wait_ge(f_ctx, r + 1)
                    for k in range(KD):
                        last = nc.tensor.transpose(ctx_p[0][:, k * P:(k + 1) * P], fctx[:, k * P:(k + 1) * P], ident[:, :])
                    last.then_inc(baton, 1)
                    rest(r + 1, ("norm1", "feed"))


def kernel(**inputs):
    import numpy as np
    import concourse.bacc as bacc
    from concourse.bass_utils import run_bass_kernel_spmd

    nc = bacc.Bacc("TRN2", target_bir_lowering=False, num_devices=1)
    arrays = {}

    def given(name, transposed=False):
        a = np.asarray(inputs[name])
        a = np.ascontiguousarray(a.T if transposed else a)
        key = f"in_{name}_T" if transposed else f"in_{name}"
        arrays[key] = a
        return nc.dram_tensor(key, a.shape, mybir.dt.from_np(a.dtype), kind="ExternalInput").ap()

    p = "L0_gnn_"
    args = [given("x"), given("x", True), given("adj")]
    for m, b in (("Wq", "bq"), ("Wk", "bk"), ("Wv", "bv"), ("Wo", "bo"), ("W1", "b1"), ("W2", "b2")):
        args += [given(p + m, True), given(p + b)]
    args += [given(p + n) for n in ("ln1_g", "ln1_b", "ln2_g", "ln2_b")]
    n, d = inputs["x"].shape
    kv = nc.dram_tensor("kv", (n, 2 * d), mybir.dt.float32, kind="Internal").ap()
    qd = nc.dram_tensor("qd", (n, d), mybir.dt.float32, kind="Internal").ap()
    out = nc.dram_tensor("out_rows", (n, d), mybir.dt.float32, kind="ExternalOutput").ap()
    build(nc, *args, kv, qd, out)
    return run_bass_kernel_spmd(nc, [arrays], core_ids=[0]).results[0]["out_rows"]
```

```python
import concourse.bass as bass
from concourse import mybir
from contextlib import ExitStack


def build(nc, x, xT, adj, WqT, bq, WkT, bk, WvT, bv, WoT, bo, W1T, b1, W2T, b2, g1, n1, g2, n2, kv, qd, out):
    F32, F16, I32, U32, U8 = mybir.dt.float32, mybir.dt.float16, mybir.dt.int32, mybir.dt.uint32, mybir.dt.uint8
    ALU, ACT, AX = mybir.AluOpType, mybir.ActivationFunctionType, mybir.AxisListType.X

    P = 128
    N, D = x.shape
    FF = W1T.shape[1]
    H = 8
    DK = D // H
    NT = N // P
    J = 4
    NG = NT // J
    KD = D // P
    KF = FF // P
    HALF = N // 2
    FOUND = 8
    LIST = 2 * FOUND
    CAP = 5
    HCAP = 2 * CAP
    KEYS = LIST + 1
    UW = HALF + FOUND
    SCALE = float(DK) ** -0.5
    EPS = 1e-5
    MASKED = -1e9
    LIFT = 8e34
    EARLY = 2 * NG
    BETWEEN = 2
    AHEAD = EARLY + BETWEEN
    GS = (NT - AHEAD) // 2
    assert GS == NG - 1
    W = 2 * P
    KU = KF // 2

    def at(i, n=1):
        return slice(i, i + n) if isinstance(i, int) else bass.DynSlice(i, n)

    ctx = ExitStack()
    with ctx:
        def sb(name, shape, dt=F32):
            return ctx.enter_context(nc.sbuf_tensor(name, shape, dt))

        def sem(name):
            return ctx.enter_context(nc.semaphore(name))

        wo = sb("wo", [P, KD, D])
        w1 = sb("w1", [P, KD, FF])
        w2 = sb("w2", [P, KF, D])
        bo_b, g1_b, n1_b, nb2, g2_b, n2_b = (sb(n, [P, D]) for n in ("bo_b", "g1_b", "n1_b", "nb2", "g2_b", "n2_b"))
        b1_c = sb("b1_c", [P, KF])
        bkT, bqT, bvT, g1T, n1T = (sb(n, [P, KD]) for n in ("bkT", "bqT", "bvT", "g1T", "n1T"))
        ident = sb("ident", [P, P])
        upper = sb("upper", [P, P])
        ones_pp = sb("ones_pp", [P, P])
        rank_row = sb("rank_row", [P, P])
        ones8 = sb("ones8", [P, FOUND])
        eps_c = sb("eps_c", [P, 1])
        selfkey = sb("selfkey", [P, NT])
        headmask = sb("headmask", [P, J])

        adjb = sb("adjb", [P, J * UW], I32)
        sqjunk = sb("sqjunk", [P, HALF], U8)
        Qs = sb("Qs", [P, NT, D])
        Vs = sb("Vs", [P, NT, D])
        s0 = sb("s0", [P, NT, H])
        keys = sb("keys", [P, NT + J, KEYS])
        sq = sb("sq", [P, 2 * NT])
        cnt = sb("cnt", [P, NT])
        GW = CAP * 2 * D
        gbuf = sb("gbuf", [P, J * GW])
        G = [gbuf[:, i * GW:(i + 1) * GW].rearrange("p (s d) -> p s d", s=CAP) for i in range(J)]
        wself = sb("wself", [P, D])
        hh = sb("hh", [P, 2048 + 1536 + KD * 512])
        hid = hh[:, 0:KF * W].rearrange("p (c n) -> p c n", c=KF)
        h1T = hh[:, KF * W:(KF + KD) * W].rearrange("p (k n) -> p k n", k=KD)
        xTb = [gbuf[:, i * 1024:(i + 1) * 1024].rearrange("p (k n) -> p k n", k=KD) for i in range(2)]
        kst = [gbuf[:, 2048 + i * 1024:3072 + i * 1024].rearrange("p (j d) -> p j d", j=J) for i in range(2)]
        tmp = [gbuf[:, 4096 + i * 512:4608 + i * 512] for i in range(2)]
        sprod = gbuf[:, 5120:6144].rearrange("p (j d) -> p j d", j=J)
        wkqv = hh[:, 0:1536].rearrange("p (k n) -> p k n", k=KD)
        bkq = hh[:, 1536:2048]
        xr = sb("xr", [P, J, D])
        ctxT = [sb(f"ctxT{i}", [P, KD, P]) for i in range(2)]
        y1 = [sb(f"y1_{i}", [P, D]) for i in range(2)]
        nh = [sb(f"nh{i}", [P, D]) for i in range(2)]
        z2 = [sb(f"z2_{i}", [P, D]) for i in range(2)]
        ob = [sb(f"ob{i}", [P, D]) for i in range(2)]
        st6 = [sb(f"st6_{i}", [P, 6]) for i in range(5)]
        mv = [sb(f"mv{i}", [P, 2]) for i in range(5)]
        nmean, lnv, rstd, shift = ([sb(f"{n}{i}", [P, 1]) for i in range(5)] for n in ("nmean", "lnv", "rstd", "shift"))
        raw = sb("raw", [P, 2, LIST], U32)
        ends = sb("ends", [P, 2, LIST])
        hit = sb("hit", [P, 2, LIST])
        val = sb("val", [P, 2, LIST])
        ne = sb("ne", [P, 2, LIST])
        val2 = sb("val2", [P, 2, LIST])
        top = sb("top", [P, 2, LIST])
        gidx = sb("gidx", [P, J, CAP], U32)
        lim = sb("lim", [P, J, CAP])
        sc = sb("sc", [P, HCAP + 1, H])
        mx = sb("mx", [P, H])
        dsh = sb("dsh", [P, HCAP + 1, H])
        pe_ = sb("pe_", [P, HCAP + 1, H])
        den = sb("den", [P, H])
        rden = sb("rden", [P, H])
        pn = sb("pn", [P, HCAP + 1, H])
        hsum = sb("hsum", [P, KEYS + 1])
        hkey = sb("hkey", [P, KEYS])
        hidx = sb("hidx", [P, HCAP + 1], U32)
        hlim = sb("hlim", [P, HCAP])
        tfl = sb("tfl", [1, NT])
        tkey = sb("tkey", [1, NT])
        tdown = sb("tdown", [1, NT])
        tlist = sb("tlist", [1, NT + 1])
        flags = sb("flags", [1, NT + 1], I32)

        tail = adjb[:, 0:4096].bitcast(F32)
        t_hid = tail[:, 0:1024].rearrange("p (c n) -> p c n", c=KF)
        t_h1T = tail[:, 1024:1280].rearrange("p (k n) -> p k n", k=KD)
        t_nh, t_res, t_z, t_ob, t_y = (tail[:, 1280 + i * D:1280 + (i + 1) * D] for i in range(5))
        over, sums_a, sums_b = (tail[:, 2560 + i * 2 * NT:2560 + (i + 1) * 2 * NT] for i in range(3))
        none, place, bad, bad2 = (tail[:, 2560 + i * NT:2560 + (i + 1) * NT] for i in range(6, 10))
        onehot = adjb[:, 4096:4096 + NT * P // 2].bitcast(F16).rearrange("p (t n) -> p t n", t=NT)
        pick = adjb[:, 4096 + NT * P // 2:4096 + NT * P // 2 + NT * (KEYS + 1) // 2].bitcast(F16).rearrange("p (t n) -> p t n", t=NT)
        own0 = 4096 + NT * P // 2 + NT * (KEYS + 1) // 2
        h_own = adjb[:, own0:own0 + 4 * D].bitcast(F32)
        hself = h_own[:, 0:2 * D]
        hq, hx = h_own[:, 2 * D:3 * D], h_own[:, 3 * D:4 * D]

        KT = Qs[:, :, :].rearrange("p t d -> p (t d)").rearrange("p (k n) -> p k n", k=KD)
        S = gbuf[:, 0:N]
        vmask = gbuf[:, N:2 * N]
        fadj = adjb[:, 0:N]
        pen = adjb[:, N:2 * N].bitcast(F32)
        qz = hh[:, 0:1024].rearrange("p (h n) -> p h n", h=H)
        stg = hh[:, 1024:1536]
        PT = hh[:, 1536:2048].rearrange("p (c n) -> p c n", c=J)
        fw = hh[:, 2048:3584].rearrange("p (k n) -> p k n", k=KD)
        fxT = hh[:, 3584:3584 + KD * 512].rearrange("p (k n) -> p k n", k=KD)
        fctx = z2[1]
        fx = ctxT[1]
        fsm = sb("fsm", [P, 4])
        fmax, fnmax, fden, frden = (fsm[:, i:i + 1] for i in range(4))

        ps = [ctx.enter_context(nc.psum_tensor(f"ps{i}", [P, 1024], F32)) for i in range(4)]
        qkv_p = ps[0:2]
        ff1_p = [ps[0][:, 0:512], ps[0][:, 512:1024]]
        fs_p = ps[1][:, 0:512]
        ff2_p = [ps[1][:, 0:D], ps[1][:, 512:512 + D]]
        ctx_p = [ps[2][:, 0:D], ps[2][:, 512:512 + D]]
        ao_p = ps[3][:, 0:D]
        h1T_p = ps[3][:, 512:512 + D]
        rank_p = ps[2][:, 768:768 + NT]
        bad_p = ps[2][0:1, 768 + NT:768 + 2 * NT]
        hkey_p = ps[2][:, 768 + 2 * NT:768 + 2 * NT + KEYS + 1]

        wq_in = sem("wq_in"); wo_in = sem("wo_in"); w1_in = sem("w1_in"); w2_in = sem("w2_in")
        bias_in = sem("bias_in"); norm_in = sem("norm_in"); colb_in = sem("colb_in")
        pool_const = sem("pool_const"); dve_const = sem("dve_const")
        adj_in = [sem(f"adj_in{i}") for i in range(J)]
        adj_scanned = sem("adj_scanned"); adj_squared = sem("adj_squared")
        xT_in = [sem(f"xT_in{i}") for i in range(2)]
        qkv_done = sem("qkv_done"); kq_copied = sem("kq_copied"); v_ready = sem("v_ready")
        k_ready = sem("k_ready"); q_ready = sem("q_ready")
        self_scored = sem("self_scored"); k_stored = [sem(f"k_stored{i}") for i in range(2)]; v_stored = sem("v_stored")
        q_stored = sem("q_stored")
        staged = sem("staged"); gathered = [sem(f"gathered{i}") for i in range(J)]
        shifted = sem("shifted"); exp_done = sem("exp_done"); weighted = sem("weighted")
        ctx_summed = sem("ctx_summed"); ctxT_ready = sem("ctxT_ready"); ao_done = sem("ao_done")
        x_in = [sem(f"x_in{i}") for i in range(J)]
        x_biased = sem("x_biased"); y_done = sem("y_done"); var1_ready = sem("var1_ready"); nh_ready = sem("nh_ready")
        h1T_done = sem("h1T_done"); h1T_ready = sem("h1T_ready"); res_ready = sem("res_ready")
        ff1_done = sem("ff1_done"); hid_ready = sem("hid_ready"); ff2_done = sem("ff2_done"); z_done = sem("z_done")
        var2_ready = sem("var2_ready"); normed2 = sem("normed2")
        out_ready = sem("out_ready"); out_stored = [sem(f"out_stored{i}") for i in range(2)]
        carried = sem("carried"); dstep = sem("dstep"); astep = sem("astep"); pstep = sem("pstep")
        over_ready = sem("over_ready"); ranked = sem("ranked"); onehot_ready = sem("onehot_ready")
        hkey_done = sem("hkey_done"); h_idx = sem("h_idx"); h_gathered = sem("h_gathered")
        h_shifted = sem("h_shifted"); h_exp = sem("h_exp"); h_weighted = sem("h_weighted"); h_stored = sem("h_stored")
        bad_ready = sem("bad_ready"); bad_summed = sem("bad_summed"); flags_ready = sem("flags_ready")
        baton = sem("baton"); t_ff1 = sem("t_ff1"); t_relu = sem("t_relu"); t_resd = sem("t_resd")
        t_step = sem("t_step"); t_act = sem("t_act"); t_pool = sem("t_pool")
        f_w = sem("f_w"); f_x = sem("f_x"); f_ktmm = sem("f_ktmm"); f_kt = sem("f_kt"); f_in = sem("f_in"); f_q = sem("f_q")
        f_qz = sem("f_qz"); f_s = sem("f_s"); f_sread = sem("f_sread"); f_max = sem("f_max"); f_e = sem("f_e")
        f_st = sem("f_st"); f_t = sem("f_t"); f_pt = sem("f_pt"); f_pv = sem("f_pv"); f_acc = sem("f_acc")
        f_step = sem("f_step"); f_out = sem("f_out"); f_ctx = sem("f_ctx")

        xT_v = xT.rearrange("(k p) n -> p k n", p=P)
        kv_rows = kv.rearrange("(t p) c -> p t c", p=P)
        q_rows = qd.rearrange("(t p) c -> p t c", p=P)

        def apart(eng):
            eng.sem_inc(carried, 1)

        class Steps:
            def __init__(self, eng, s, base=0):
                self.eng, self.s, self.base, self.n = eng, s, base, 0

            def mark(self, ins):
                ins.then_inc(self.s, 1)
                self.n += 1

            def wait(self, n=None):
                self.eng.wait_ge(self.s, self.base + (self.n if n is None else n))

        B_CTX = 1
        B_CTXT = B_CTX + KD
        B_AO, B_VAR1, B_NH, B_T = range(B_CTXT + 1, B_CTXT + 5)
        B_H1T = B_T + KD
        B_FF2, B_VAR2, B_N2, B_OUT = range(B_H1T + 1, B_H1T + 5)
        F_STEPS = 3 + H * (NG + 4)
        T_DVE, T_ACT, T_POOL = 7, 6, 2

        block = ctx.enter_context(nc.Block())

        @block.sync
        def _(sp):
            def load_unit(u_tile, half, b, k):
                sp.wait_ge(adj_scanned, k + 1)
                sp.wait_ge(adj_squared, k + 1)
                sp.dma_start(adjb[:, b * UW:b * UW + HALF],
                             adj[at(u_tile * P, P), half * HALF:(half + 1) * HALF]).then_inc(adj_in[b], 16)

            def load_wkqv(dst, s):
                for wT, c in ((WkT, 0), (WqT, 1), (WvT, 2)):
                    sp.dma_start(dst[:, :, c * D:(c + 1) * D], wT.rearrange("(k p) n -> p k n", p=P)).then_inc(s, 16)

            def load_xT(g, b=None, done=None):
                b = g % 2 if b is None else b
                sp.wait_ge(qkv_done, (max(g - 1, 0) if done is None else done) * J + J)
                sp.dma_start(xTb[b], xT_v[:, :, at(g * J * P, J * P)]).then_inc(xT_in[b], 16)

            def store_kv(g, b=None):
                b = g % 2 if b is None else b
                sp.wait_ge(k_ready, g * J + J + 2)
                sp.dma_start(kv_rows[:, at(g * J, J), 0:D], kst[b]).then_inc(k_stored[b], 16)
                sp.wait_ge(v_ready, g * J + J + 2)
                sp.dma_start(kv_rows[:, at(g * J, J), D:2 * D], Vs[:, at(g * J, J), :]).then_inc(v_stored, 16)

            def load_x(g, j):
                sp.wait_ge(y_done, g * J + j + 1)
                sp.dma_start(xr[:, j, :], x[at((g * J + j) * P, P), :]).then_inc(x_in[j], 16)

            load_wkqv(wkqv, wq_in)
            load_xT(0)
            with nc.allow_non_contiguous_dma("per-partition biases"):
                for dst, b, s in ((bkT, bk, k_stored[0]), (bqT, bq, k_stored[1]), (bvT, bv, f_out)):
                    sp.dma_start(dst[:, :], b.rearrange("(c p) -> p c", p=P)).then_inc(s, 16)

            def group(g, s):
                for k in range(J):
                    load_unit(g * 2 + k // 2, k % 2, k, g * J + k)
                    if k == 1:
                        store_kv(g - 1, 1 - s)

            load_xT(1)
            for k in range(J):
                load_unit(k // 2, k % 2, k, k)
            load_xT(2)
            group(1, 1)
            with sp.Fori(1, NG // 2 - 1) as i:
                for s in range(2):
                    load_xT(i * 2 + s + 1, 1 - s, i * 2 + s)
                    group(i * 2 + s, s)
            load_xT(NG - 1)
            group(NG - 2, 0)
            group(NG - 1, 1)
            store_kv(NG - 1)
            for j in range(J):
                load_x(0, j)
            for k in range(2 * BETWEEN):
                load_unit(EARLY + k // 2, k % 2, k % J, 2 * EARLY + k)

            def step(g, j, search, prev, first=False):
                if not first:
                    load_x(g, j)
                if first and j == 1:
                    for i, (dst, b) in enumerate(((g2_b, g2), (n2_b, n2))):
                        sp.dma_start(dst[:, :], b.partition_broadcast(P)).then_inc(out_stored[i], 16)
                if first:
                    sp.wait_ge(x_biased, j + 1)
                if j == 1:
                    sp.wait_ge(q_ready, NT + 2)
                    sp.dma_start(q_rows[:, at(g * J, J), :], Qs[:, at(g * J, J), :]).then_inc(q_stored, 16)
                if search:
                    load_unit(g * 2 + (AHEAD + j // 2), j % 2, j, g * J + (2 * AHEAD + j))
                if prev and j % 2 == 0:
                    store_pair((g - 2) * J + j)

            def store_pair(t):
                for i in range(2):
                    sp.wait_ge(out_ready, t + i + 1)
                    sp.dma_start(out[at((t + i) * P, P), :], ob[i][:, :]).then_inc(out_stored[i], 16)

            for g in range(2):
                for j in range(J):
                    step(g, j, True, False, first=(g == 0))
                    if g == 0 and j >= 2:
                        w, wT, s = ((w1, W1T, w1_in), (w2, W2T, w2_in))[j - 2]
                        sp.dma_start(w[:, :, :], wT.rearrange("(k p) n -> p k n", p=P)).then_inc(s, 16)
            with sp.Fori(2, GS) as g:
                for j in range(J):
                    step(g, j, True, True)
            for j in range(J):
                step(GS, j, False, True)
            for t in range(NT - 8, NT, 2):
                store_pair(t)
            sp.wait_ge(h_stored, 16)

            sp.wait_ge(flags_ready, 1)
            nf = sp.value_load(flags[0:1, 0:1], min_val=0, max_val=NT)
            with sp.If(nf > 0):
                load_wkqv(fw, f_w)
                with sp.Fori(0, NG) as c:
                    sp.wait_ge(f_kt, c * KD + KD)
                    sp.dma_start(fxT, xT_v[:, :, at(c * 512, 512)]).then_inc(f_x, 16)
                with sp.Fori(0, nf) as r:
                    f = sp.value_load(flags[0:1, at(r + 1, 1)], min_val=0, max_val=NT - 1)
                    sp.wait_ge(f_kt, KD * NG + KD)
                    sp.wait_ge(f_out, r * 16 + 16)
                    sp.dma_start(fadj, adj[at(f * P, P), :]).then_inc(f_in, 16)
                    load_wkqv(fw, f_w)
                    sp.dma_start(fx[:, :, :], xT_v[:, :, at(f * P, P)]).then_inc(f_in, 16)
                    sp.dma_start(xr[:, 0, :], x[at(f * P, P), :]).then_inc(f_in, 16)
                    sp.wait_ge(baton, r * B_OUT + 2 * B_OUT)
                    sp.dma_start(out[at(f * P, P), :], t_ob).then_inc(f_out, 16)
                    sp.wait_ge(f_out, r * 16 + 32)
                    apart(sp)

        @block.gpsimd
        def _(pool):
            for s in (k_ready, q_ready, res_ready):
                pool.sem_inc(s, 2)
            nc.gpsimd.memset(ident[:, :], 0.0).then_inc(pool_const, 1)
            nc.gpsimd.memset(upper[:, :], 1.0).then_inc(pool_const, 1)
            nc.gpsimd.memset(headmask[:, :], 1.0).then_inc(pool_const, 1)
            for dst, step_, base, chan in ((selfkey, -P, N, -1), (tdown, -1, NT, 0), (rank_row, 1, 0, 0)):
                nc.gpsimd.iota(dst[:, :], pattern=[[step_, dst.shape[1]]], base=base, channel_multiplier=chan,
                               allow_small_or_imprecise_dtypes=True).then_inc(pool_const, 1)
            pool.wait_ge(pool_const, 6)
            nc.gpsimd.affine_select(out=ident[:, :], in_=ident[:, :], compare_op=ALU.not_equal, fill=1.0,
                                    base=0, pattern=[[-1, P]], channel_multiplier=1).then_inc(pool_const, 1)
            nc.gpsimd.affine_select(out=upper[:, :], in_=upper[:, :], compare_op=ALU.is_ge, fill=0.0,
                                    base=-1, pattern=[[1, P]], channel_multiplier=-1).then_inc(pool_const, 1)
            nc.gpsimd.affine_select(out=headmask[:, :], in_=headmask[:, :], compare_op=ALU.is_ge, fill=0.0,
                                    base=0, pattern=[[-DK, J]], channel_multiplier=1).then_inc(pool_const, 1)
            pool.wait_ge(pool_const, 9)
            nc.gpsimd.affine_select(out=headmask[:, :], in_=headmask[:, :], compare_op=ALU.is_ge, fill=0.0,
                                    base=DK - 1, pattern=[[DK, J]], channel_multiplier=-1).then_inc(pool_const, 1)

            pool.wait_ge(bias_in, 16 * 3)
            with pool.Fori(0, NG // 2) as i:
                for s in range(2):
                    g = i * 2 + s
                    pool.wait_ge(self_scored, g + 1)
                    pool.wait_ge(k_stored[s], i * 16 + 16)
                    for j in range(J):
                        t = g * J + j
                        pool.wait_ge(kq_copied, t + 3)
                        nc.gpsimd.tensor_tensor(kst[s][:, j, :], tmp[j % 2][:, 0:D], bkq[:, 0:D],
                                                ALU.add).then_inc(k_ready, 1)
                        nc.gpsimd.tensor_tensor(Qs[:, at(t), :], tmp[j % 2][:, D:2 * D].unsqueeze(1),
                                                bkq[:, D:2 * D].unsqueeze(1), ALU.add).then_inc(q_ready, 1)

            pst = Steps(pool, pstep)
            for s in range(2):
                pool.wait_ge(k_stored[s], 16 * NG // 2 + 16)
            pool.wait_ge(v_stored, 16 * NG)
            pool.wait_ge(self_scored, NG + 1)
            pool.wait_ge(q_ready, NT + 2)
            pool.wait_ge(dve_const, 3)

            def gather(dst, src, idx, done):
                pool.indirect_dma_start(out=dst, out_offset=None, in_=src,
                                        in_offset=bass.IndirectOffsetOnAxis(ap=idx, axis=0),
                                        bounds_check=N - 1, oob_is_err=False).then_inc(done, 16)

            def gathers(g, j):
                t = g * J + j
                pool.wait_ge(staged, t + 1)
                pool.wait_ge(ctx_summed, t + 1)
                apart(pool)
                for s in range(CAP):
                    gather(G[j][:, s, :], kv[:, :], gidx[:, j, s:s + 1], gathered[j])

            def bias_x(g, j):
                pool.wait_ge(x_in[j], g * 16 + 16)
                nc.gpsimd.tensor_tensor(xr[:, j, :], xr[:, j, :], bo_b[:, :], ALU.add).then_inc(x_biased, 1)

            def residual(g, j, t):
                pool.wait_ge(nh_ready, t + 3)
                pool.wait_ge(q_stored, g * 16 + 16)
                apart(pool)
                row = Qs[:, at(t), :]
                pst.mark(nc.gpsimd.tensor_tensor(row, nh[j % 2][:, :].unsqueeze(1), g1_b[:, :].unsqueeze(1), ALU.mult))
                pst.wait()
                apart(pool)
                nc.gpsimd.tensor_tensor(row, row, nb2[:, :].unsqueeze(1), ALU.add).then_inc(res_ready, 1)

            def out_pair(t):
                for i in range(2):
                    pool.wait_ge(normed2, t + i + 3)
                    pst.mark(nc.gpsimd.tensor_tensor(ob[i][:, :], ob[i][:, :], g2_b[:, :], ALU.mult))
                    pst.wait()
                    nc.gpsimd.tensor_tensor(ob[i][:, :], ob[i][:, :], n2_b[:, :], ALU.add).then_inc(out_ready, 1)

            def step(g, j, res, outs):
                gathers(g, j)
                bias_x(g, j)
                if res:
                    residual(g if j == 3 else g - 1, (j + 1) % J, g * J + j - 3)
                if outs and j % 2 == 0:
                    out_pair((g - 2) * J + j)

            for g in range(2):
                for j in range(J):
                    if g == 0 and j == 1:
                        pool.wait_ge(self_scored, NG + 2)
                    if g == 0 and j == 3:
                        pool.wait_ge(norm_in, 16 * 3)
                        pst.mark(nc.gpsimd.tensor_tensor(nb2[:, :], n1_b[:, :], nb2[:, :], ALU.add))
                        pst.wait()
                    step(g, j, g > 0 or j == 3, False)
            pool.wait_ge(out_stored[0], 16)
            pool.wait_ge(out_stored[1], 16)
            base, pst.n, per = pst.n, 0, J + 4
            with pool.Fori(2, NG) as g:
                pst.base, pst.n = (g - 2) * per + base, 0
                for j in range(J):
                    step(g, j, True, True)
                assert pst.n == per, pst.n
            pst.base, pst.n = base + (NG - 2) * per, 0

            pool.wait_ge(over_ready, 1)
            pst.mark(nc.gpsimd.memset(h_own, 0.0))
            pst.wait()
            pool.wait_ge(h_idx, 3)
            pool.wait_ge(q_stored, 16 * NG)
            me = hidx[:, HCAP:HCAP + 1]
            for dst, src in ((hself, kv), (hq, qd), (hx, x)):
                gather(dst, src[:, :], me, h_gathered)
            for i in range(2):
                pool.wait_ge(ctx_summed, NT - 4 + i + 1 + J)
                for s in range(CAP):
                    gather(G[i][:, s, :], kv[:, :], hidx[:, i * CAP + s:i * CAP + s + 1], h_gathered)
            for i in range(3):
                residual(NG - 1, i + 1, NT - 3 + i)
                out_pair(NT - 8 + 2 * i)

            def rest(r, parts):
                ts = Steps(pool, t_pool, r * T_POOL)
                if "residual" in parts:
                    pool.wait_ge(baton, r * B_OUT + B_NH)
                    ts.mark(nc.gpsimd.tensor_tensor(t_res, t_nh, g1_b[:, :], ALU.mult))
                    ts.wait()
                    nc.gpsimd.tensor_tensor(t_res, t_res, nb2[:, :], ALU.add).then_inc(t_resd, 1)
                if "out" in parts:
                    ts.n = 1
                    pool.wait_ge(baton, r * B_OUT + B_N2)
                    ts.mark(nc.gpsimd.tensor_tensor(t_ob, t_ob, g2_b[:, :], ALU.mult))
                    ts.wait()
                    nc.gpsimd.tensor_tensor(t_ob, t_ob, n2_b[:, :], ALU.add).then_inc(baton, 1)

            rest(0, ("residual",))
            out_pair(NT - 2)
            rest(0, ("out",))
            for i in range(2):
                pool.wait_ge(out_stored[i], 16 * NT // 2 + 16)
            pool.wait_ge(baton, B_OUT)
            pool.indirect_dma_start(out=out[:, :], out_offset=bass.IndirectOffsetOnAxis(ap=me, axis=0), in_=t_ob,
                                    in_offset=None, bounds_check=N - 1, oob_is_err=False).then_inc(h_stored, 16)
            pool.wait_ge(h_stored, 16)

            pool.wait_ge(flags_ready, 1)
            nf = pool.value_load(flags[0:1, 0:1], min_val=0, max_val=NT)
            with pool.If(nf > 0):
                with pool.Fori(0, nf) as r:
                    rest(r + 1, ("residual", "out"))

        @block.scalar
        def _(act):
            nc.scalar.preload_act_table_set("natural_log_exp_and_others")
            act.sem_inc(adj_squared, J)
            act.sem_inc(h1T_ready, KD)
            act.sem_inc(f_kt, KD)
            act.sem_inc(f_pt, 1)
            for s in (kq_copied, v_ready, nh_ready, normed2):
                act.sem_inc(s, 2)
            for c, b in enumerate((bk, bq)):
                act.dma_start(bkq[:, c * D:(c + 1) * D], b.partition_broadcast(P)).then_inc(bias_in, 16)
            act.dma_start(bo_b[:, :], bo.partition_broadcast(P)).then_inc(bias_in, 16)
            with nc.allow_non_contiguous_dma("per-partition biases"):
                act.dma_start(b1_c[:, :], b1.rearrange("(c p) -> p c", p=P)).then_inc(colb_in, 16)
                act.dma_start(g1T[:, :], g1.rearrange("(c p) -> p c", p=P)).then_inc(colb_in, 16)
                act.dma_start(n1T[:, :], n1.rearrange("(c p) -> p c", p=P)).then_inc(colb_in, 16)

            def square(k, b, visit):
                act.wait_ge(adj_in[b], visit * 16 + 16)
                act.wait_ge(adj_squared, k + J)
                nc.scalar.activation(sqjunk[:, :], adjb[:, b * UW:b * UW + HALF], ACT.Square,
                                     accum_out=sq[:, at(k)]).then_inc(adj_squared, 1)

            def copy_qkv(t, b):
                act.wait_ge(qkv_done, t + 1 + J)
                act.wait_ge(q_ready, t + 1)
                act.wait_ge(k_ready, t + 1)
                nc.scalar.copy(tmp[b], qkv_p[b][:, 0:2 * D]).then_inc(kq_copied, 1)
                nc.scalar.copy(Vs[:, at(t), :], qkv_p[b][:, 2 * D:3 * D].unsqueeze(1)).then_inc(v_ready, 1)

            with act.Fori(0, NG) as g:
                for j in range(0, J, 2):
                    for i in range(2):
                        copy_qkv(g * J + j + i, i)
                    for i in range(2):
                        square(g * J + j + i, j + i, g)
            for k in range(2 * BETWEEN):
                square(2 * EARLY + k, k, NG)

            act.dma_start(wo[:, :, :], WoT.rearrange("(k p) n -> p k n", p=P)).then_inc(wo_in, 16)
            for dst, b in ((g1_b, g1), (n1_b, n1), (nb2, b2)):
                act.dma_start(dst[:, :], b.partition_broadcast(P)).then_inc(norm_in, 16)

            act.wait_ge(colb_in, 48)
            act.wait_ge(dve_const, 3)
            act.wait_ge(k_stored[0], 16)
            act.wait_ge(k_stored[1], 16)
            act.wait_ge(f_out, 16)

            def normalize(st, i, dst, y):
                st.mark(nc.scalar.activation(lnv[i][:, :], mv[i][:, 1:2], ACT.Ln, bias=eps_c[:, 0:1]))
                st.wait()
                st.mark(nc.scalar.activation(rstd[i][:, :], lnv[i][:, :], ACT.Exp, scale=-0.5))
                st.wait()
                st.mark(nc.scalar.activation(shift[i][:, :], nmean[i][:, :], ACT.Identity, scale=rstd[i][:, 0:1]))
                st.wait()
                return nc.scalar.activation(dst, y, ACT.Identity, scale=rstd[i][:, 0:1], bias=shift[i][:, 0:1])

            def relu(u, p):
                act.wait_ge(ff1_done, p * KU + u + 1)
                for i in range(2):
                    c = 2 * u + i
                    nc.scalar.activation(hid[:, c, :], ff1_p[u % 2][:, i * W:(i + 1) * W], ACT.Relu,
                                         bias=b1_c[:, c:c + 1]).then_inc(hid_ready, 1)

            def first_norm(t, i):
                act.wait_ge(var1_ready, t + 1)
                act.wait_ge(h1T_done, t + 1)
                act.wait_ge(res_ready, t + 1)
                normalize(ast, i, nh[i][:, :], y1[i][:, :]).then_inc(nh_ready, 1)

            def second_norms(t, pairs):
                for i in range(2):
                    act.wait_ge(var2_ready, t + i + 1)
                    act.wait_ge(out_stored[i], pairs * 16 + 16)
                    normalize(ast, 2 + i, ob[i][:, :], z2[i][:, :]).then_inc(normed2, 1)

            def copy_h1T(i, t):
                act.wait_ge(h1T_done, t + 3)
                for k in range(KD):
                    nc.scalar.activation(h1T[:, k, i * P:(i + 1) * P], h1T_p[:, k * P:(k + 1) * P], ACT.Identity,
                                         scale=g1T[:, k:k + 1], bias=n1T[:, k:k + 1]).then_inc(h1T_ready, 1)

            def copy_ctxT(i, src, done):
                for k in range(KD):
                    nc.scalar.activation(ctxT[i][:, k, :], src[:, k * P:(k + 1) * P], ACT.Identity,
                                         bias=bvT[:, k:k + 1]).then_inc(done, 1)

            ast = Steps(act, astep)

            def step(g, j, search, before=6, exp_last=False):
                t = g * J + j

                def exp():
                    act.wait_ge(shifted, t + 1)
                    nc.scalar.activation(pe_[:, 0:CAP + 1, :], dsh[:, 0:CAP + 1, :], ACT.Exp, scale=SCALE).then_inc(exp_done, 1)

                if not exp_last:
                    exp()
                if before >= 3 and j % 2:
                    for u in range(KU):
                        relu(u, g * (J // 2) + (j - 3) // 2)
                if exp_last:
                    exp()
                if before >= 6 and j % 2 == 0:
                    second_norms(g * J + (j - 6), g * (J // 2) + (j - 6) // 2)
                if before >= 1:
                    first_norm(t - 1, (j - 1) % 2)
                act.wait_ge(ctx_summed, t + 1 + J)
                copy_ctxT(j % 2, ctx_p[j % 2], ctxT_ready)
                if before >= 1:
                    copy_h1T((j - 1) % 2, t - 1)
                if search:
                    square(g * J + (2 * AHEAD + j), j, g + 2 * AHEAD // J)

            for g in range(2):
                for j in range(J):
                    step(g, j, True, before=g * J + j)
            base, ast.n, per = ast.n, 0, J * 3 + 4 * 3
            with act.Fori(2, GS) as g:
                ast.base, ast.n = (g - 2) * per + base, 0
                for j in range(J):
                    step(g, j, True)
                assert ast.n == per, ast.n
            ast.base, ast.n = base + (GS - 2) * per, 0
            for j in range(J):
                step(GS, j, False, exp_last=(j == 1))

            def rest(r, parts):
                ts = Steps(act, t_act, r * T_ACT)
                if "context" in parts:
                    act.wait_ge(baton, r * B_OUT + B_CTX)
                    copy_ctxT(0, ctx_p[0], baton)
                if "norm1" in parts:
                    act.wait_ge(baton, r * B_OUT + B_VAR1)
                    normalize(ts, 4, t_nh, t_y).then_inc(baton, 1)
                if "turn" in parts:
                    act.wait_ge(baton, r * B_OUT + B_T)
                    for k in range(KD):
                        nc.scalar.activation(t_h1T[:, k, :], h1T_p[:, k * P:(k + 1) * P], ACT.Identity,
                                             scale=g1T[:, k:k + 1], bias=n1T[:, k:k + 1]).then_inc(baton, 1)
                if "feed" in parts:
                    for u in range(2):
                        act.wait_ge(t_ff1, r * 2 + u + 1)
                        for i in range(KF // 2):
                            c = u * (KF // 2) + i
                            nc.scalar.activation(t_hid[:, c, :], ff1_p[u][:, i * P:(i + 1) * P], ACT.Relu,
                                                 bias=b1_c[:, c:c + 1]).then_inc(t_relu, 1)
                if "norm2" in parts:
                    ts.n = 3
                    act.wait_ge(baton, r * B_OUT + B_VAR2)
                    normalize(ts, 4, t_ob, t_z).then_inc(baton, 1)

            act.wait_ge(h_shifted, 1)
            nc.scalar.activation(pe_[:, :, :], dsh[:, :, :], ACT.Exp, scale=SCALE).then_inc(h_exp, 1)
            first_norm(NT - 1, (J - 1) % 2)
            copy_h1T(1, NT - 1)
            second_norms(NT - 6, NT // 2 - 3)
            relu(0, NT // 2 - 1)
            rest(0, ("context",))
            relu(1, NT // 2 - 1)
            rest(0, ("norm1",))
            for u in range(2, KU):
                relu(u, NT // 2 - 1)
            rest(0, ("turn",))
            second_norms(NT - 4, NT // 2 - 2)
            rest(0, ("feed",))
            second_norms(NT - 2, NT // 2 - 1)
            rest(0, ("norm2",))

            act.wait_ge(flags_ready, 1)
            nf = act.value_load(flags[0:1, 0:1], min_val=0, max_val=NT)
            with act.If(nf > 0):
                act.wait_ge(h_stored, 16)
                with act.Fori(0, NG) as c:
                    for dh in range(KD):
                        act.wait_ge(f_ktmm, c * KD + dh + 1)
                        nc.scalar.activation(KT[:, dh, at(c * 512, 512)], ff1_p[dh], ACT.Identity,
                                             bias=bkT[:, dh:dh + 1]).then_inc(f_kt, 1)
                with act.Fori(0, nf) as r:
                    for h in range(H):
                        act.wait_ge(f_max, r * H + h + 1)
                        nc.scalar.activation(S, S, ACT.Exp, bias=fnmax, accum_out=fden).then_inc(f_e, 1)
                        with act.Fori(0, NG) as c:
                            act.wait_ge(f_t, r * (H * NG) + h * NG + c + 2)
                            act.wait_ge(f_pv, r * (H * NG) + h * NG + c + 1)
                            nc.scalar.copy(PT, ff1_p[0].rearrange("p (c n) -> p c n", c=J)).then_inc(f_pt, 1)
                    rest(r + 1, ("context", "norm1", "turn", "feed", "norm2"))

        @block.vector
        def _(dve):
            nc.vector.memset(ones8[:, :], 1.0).then_inc(dve_const, 1)
            nc.vector.memset(ones_pp[:, :], 1.0).then_inc(dve_const, 1)
            nc.vector.memset(eps_c[:, :], EPS).then_inc(dve_const, 1)
            st = Steps(dve, dstep)
            for b in range(J):
                nc.vector.memset(adjb[:, b * UW + HALF:(b + 1) * UW], 1).then_inc(adj_scanned, 1)
            st.mark(nc.vector.memset(gbuf[:, 6144:], 0.0))
            st.mark(nc.vector.memset(keys[:, NT:NT + J, :], 0.0))
            for s, n in ((self_scored, 2), (z_done, 2), (y_done, J), (f_sread, 1), (f_acc, 1)):
                dve.sem_inc(s, n)
            nc.vector.memset(ends[:, :, 0:FOUND], float(N)).then_inc(dve_const, 1)
            nc.vector.memset(ends[:, :, FOUND:LIST], float(HALF)).then_inc(dve_const, 1)
            dve.wait_ge(pool_const, 10)
            st.mark(nc.vector.tensor_copy(keys[:, 0:NT, LIST:KEYS], selfkey[:, :].unsqueeze(2)))
            dve.wait_ge(dve_const, 5)
            st.wait()

            def find(k, b, visit):
                dve.wait_ge(adj_in[b], visit * 16 + 16)
                apart(dve)
                i = b // 2
                nc.vector.max_index(raw[:, i, (b % 2) * FOUND:(b % 2 + 1) * FOUND], ones8[:, :],
                                    adjb[:, b * UW:(b + 1) * UW]).then_inc(adj_scanned, 1)

            def list_part(part, t, k, since=None):
                if part == 0:
                    dve.wait_ge(adj_scanned, k + J)
                else:
                    st.wait(since)
                if part == 0:
                    st.mark(nc.vector.scalar_tensor_tensor(val[:, :, :], raw[:, :, :], -1.0, ends[:, :, :], ALU.mult, ALU.add))
                    st.mark(nc.vector.tensor_scalar(hit[:, :, :], raw[:, :, :], float(HALF), None, ALU.is_lt))
                if part == 1:
                    st.mark(nc.vector.tensor_tensor(ne[:, :, :], val[:, :, :],
                                                    selfkey[:, at(t, 2)].unsqueeze(2).to_broadcast([P, 2, LIST]), ALU.not_equal))
                    st.mark(nc.vector.tensor_tensor(val2[:, :, :], val[:, :, :], hit[:, :, :], ALU.mult))
                    st.mark(nc.vector.tensor_reduce(cnt[:, at(t, 2)], hit[:, :, :], AX, ALU.add))
                if part == 2:
                    st.mark(nc.vector.tensor_tensor(val[:, :, :], val2[:, :, :], ne[:, :, :], ALU.mult))
                if part == 3:
                    apart(dve)
                    for i in range(2):
                        st.mark(nc.vector.max(top[:, i, 0:FOUND], val[:, i, :]))
                if part == 4:
                    apart(dve)
                    for i in range(2):
                        st.mark(nc.vector.match_replace(val2[:, i, :], top[:, i, 0:FOUND], val[:, i, :], 0.0))
                if part == 5:
                    apart(dve)
                    for i in range(2):
                        st.mark(nc.vector.max(top[:, i, FOUND:LIST], val2[:, i, :]))
                if part == 6:
                    st.mark(nc.vector.tensor_copy(keys[:, at(t, 2), 0:LIST], top[:, :, :]))
                return st.n

            def lists(t, k):
                n = None
                for part in range(7):
                    n = list_part(part, t, k, n)
                st.wait()

            LISTS = 13

            def score_self(g, b):
                dve.wait_ge(self_scored, g + 2)
                dve.wait_ge(k_ready, g * J + J + 2)
                dve.wait_ge(q_ready, g * J + J + 2)
                st.mark(nc.vector.tensor_tensor(sprod, kst[b], Qs[:, at(g * J, J), :], ALU.mult))
                st.wait()
                nc.vector.tensor_reduce(s0[:, at(g * J, J), :], sprod.rearrange("p j (h d) -> p j h d", h=H),
                                        AX, ALU.add).then_inc(self_scored, 1)

            def group(g, s, first=False):
                for k in range(J):
                    find(g * J + k, k, g)
                    if k == 1 and not first:
                        score_self(g - 1, 1 - s)
                lists(g * 2, g * J + J)

            for s in range(2):
                group(s, s, first=(s == 0))
            base, per = st.n, 2 * (LISTS + 1)
            with dve.Fori(1, NG // 2) as i:
                st.base, st.n = (i - 1) * per + base, 0
                for s in range(2):
                    group(i * 2 + s, s)
                assert st.n == per, st.n
            st.base, st.n = base + (NG // 2 - 1) * per, 0
            def stage(t, j):
                nc.vector.tensor_scalar(gidx[:, j, :].unsqueeze(1), keys[:, at(t), 0:CAP], -1.0, float(N),
                                        ALU.mult, ALU.add).then_inc(staged, 1)
                st.mark(nc.vector.tensor_scalar(lim[:, j, :].unsqueeze(1), keys[:, at(t), 0:CAP], LIFT, MASKED,
                                                ALU.mult, ALU.add))

            for j in range(J - 1):
                stage(j, j)
            score_self(NG - 1, 1)

            for k in range(2 * BETWEEN):
                find(2 * EARLY + k, k, NG)
            lists(EARLY, 2 * AHEAD)
            dve.wait_ge(self_scored, NG + 2)

            def stats(st, ys, done):
                for y, i in ys:
                    st.mark(nc.vector.bn_stats(st6[i][:, :], y))
                st.wait()
                apart(dve)
                for y, i in ys:
                    st.mark(nc.vector.bn_aggr(mv[i][:, :], st6[i][:, :]))
                st.wait()
                for y, i in ys:
                    nc.vector.tensor_scalar(nmean[i][:, :], mv[i][:, 0:1], -1.0, None, ALU.mult).then_inc(done, 1)

            def heads(rows):
                return rows.rearrange("p s (h d) -> p s h d", h=H)

            def scores_less_max(blocks, own, n, done, pair=None):
                for s0_, k_rows, q_row, limits in blocks:
                    m = k_rows.shape[1]
                    st.mark(nc.vector.tensor_tensor(k_rows, k_rows, q_row.to_broadcast([P, m, D]), ALU.mult))
                own()
                if pair is not None:
                    second_sum(pair, 0)
                st.wait()
                for s0_, k_rows, q_row, limits in blocks:
                    m = k_rows.shape[1]
                    st.mark(nc.vector.tensor_reduce(sc[:, s0_:s0_ + m, :], heads(k_rows), AX, ALU.add))
                if pair is not None:
                    second_sum(pair, 1)
                st.wait()
                for s0_, k_rows, q_row, limits in blocks:
                    m = k_rows.shape[1]
                    if limits is not None:
                        st.mark(nc.vector.tensor_tensor(sc[:, s0_:s0_ + m, :], sc[:, s0_:s0_ + m, :],
                                                        limits.unsqueeze(2).to_broadcast([P, m, H]), ALU.min))
                limited = st.n
                if pair is not None:
                    dve.wait_ge(z_done, pair + 3)
                    st.mark(nc.vector.bn_stats(st6[2][:, :], z2[0][:, :]))
                st.wait(limited)
                st.mark(nc.vector.tensor_reduce(mx[:, :], sc[:, 0:n, :].rearrange("p s h -> p h s"), AX, ALU.max))
                found = st.n
                if pair is not None:
                    dve.wait_ge(z_done, pair + 4)
                    st.mark(nc.vector.bn_stats(st6[3][:, :], z2[1][:, :]))
                st.wait(found)
                nc.vector.tensor_tensor(dsh[:, 0:n, :], sc[:, 0:n, :], mx[:, :].unsqueeze(1).to_broadcast([P, n, H]),
                                        ALU.subtract).then_inc(done, 1)
                if pair is not None:
                    st.wait()
                    apart(dve)
                    for i in (2, 3):
                        st.mark(nc.vector.bn_aggr(mv[i][:, :], st6[i][:, :]))

            def weigh(blocks, n, done, norm_of=None, lists_of=None):
                listed = [None]

                def more_lists(part):
                    if lists_of:
                        listed[0] = list_part(part, *lists_of, listed[0])

                if norm_of:
                    t, i = norm_of[0], norm_of[1] % 2
                    y = y1[i][:, :]
                    dve.wait_ge(ao_done, t + 1)
                    dve.wait_ge(x_biased, t + 1)
                    dve.wait_ge(nh_ready, t + 1)
                    nc.vector.tensor_tensor(y, ao_p, xr[:, norm_of[1], :], ALU.add).then_inc(y_done, 1)
                more_lists(0)
                st.mark(nc.vector.tensor_reduce(den[:, :], pe_[:, 0:n, :].rearrange("p s h -> p h s"), AX, ALU.add))
                summed = st.n
                more_lists(1)
                if norm_of:
                    dve.wait_ge(y_done, t + 1 + J)
                    st.mark(nc.vector.bn_stats(st6[i][:, :], y))
                counted = st.n
                st.wait(summed)
                st.mark(nc.vector.reciprocal(rden[:, :], den[:, :]))
                inverted = st.n
                more_lists(2)
                if norm_of:
                    st.wait(counted)
                    apart(dve)
                    st.mark(nc.vector.bn_aggr(mv[i][:, :], st6[i][:, :]))
                averaged = st.n
                more_lists(3)
                st.wait(inverted)
                st.mark(nc.vector.tensor_tensor(pn[:, 0:n, :], pe_[:, 0:n, :], rden[:, :].unsqueeze(1).to_broadcast([P, n, H]), ALU.mult))
                scaled = st.n
                more_lists(4)
                if norm_of:
                    st.wait(averaged)
                    nc.vector.tensor_scalar(nmean[i][:, :], mv[i][:, 0:1], -1.0, None, ALU.mult).then_inc(var1_ready, 1)
                st.wait(scaled)
                for s0_, v_rows, dst in blocks:
                    more_lists(5 if s0_ == 0 else 6)
                    m = v_rows.shape[1]
                    nc.vector.tensor_tensor(heads(dst), heads(v_rows), pn[:, s0_:s0_ + m, :].unsqueeze(3).to_broadcast([P, m, H, DK]),
                                            ALU.mult).then_inc(done, 1)

            def first_norm_stats(t, j):
                dve.wait_ge(ao_done, t + 1)
                dve.wait_ge(x_biased, t + 1)
                dve.wait_ge(nh_ready, t + 1)
                nc.vector.tensor_tensor(y1[j % 2][:, :], ao_p, xr[:, j, :], ALU.add).then_inc(y_done, 1)
                dve.wait_ge(y_done, t + 1 + J)
                stats(st, [(y1[j % 2][:, :], j % 2)], var1_ready)

            def second_sum(t, i):
                dve.wait_ge(ff2_done, t + i + 1)
                dve.wait_ge(res_ready, t + i + 3)
                dve.wait_ge(normed2, t + i + 1)
                nc.vector.tensor_tensor(z2[i][:, :], ff2_p[i], Qs[:, at(t + i), :].rearrange("p o d -> p (o d)"),
                                        ALU.add).then_inc(z_done, 1)

            def second_sums(t):
                for i in range(2):
                    second_sum(t, i)
                dve.wait_ge(z_done, t + 4)
                stats(st, [(z2[i][:, :], 2 + i) for i in range(2)], var2_ready)

            def step(g, j, search, before=6, between=None):
                t = g * J + j
                dve.wait_ge(gathered[j], g * (16 * CAP) + 16 * CAP)
                pair = t - 5 if before >= 5 and j % 2 else None
                scores_less_max([(1, G[j][:, :, 0:D], Qs[:, at(t), :], lim[:, j, :])],
                                lambda: st.mark(nc.vector.tensor_copy(sc[:, 0:1, :], s0[:, at(t), :])), CAP + 1, shifted, pair)
                if search:
                    find(g * J + (2 * AHEAD + j), j, g + 2 * AHEAD // J)
                if between:
                    between()
                if pair is not None:
                    st.wait()
                    for i in (2, 3):
                        nc.vector.tensor_scalar(nmean[i][:, :], mv[i][:, 0:1], -1.0, None, ALU.mult).then_inc(var2_ready, 1)
                dve.wait_ge(exp_done, t + 1)
                dve.wait_ge(ctx_summed, t + J)
                weigh([(0, Vs[:, at(t), :], wself[:, :].unsqueeze(1)), (1, G[j][:, :, D:2 * D], G[j][:, :, 0:D])], CAP + 1, weighted,
                      norm_of=(t - 1, (j - 1) % J) if before else None,
                      lists_of=(g * 2 + AHEAD, g * J + (2 * AHEAD + J)) if search and j == J - 1 else None)
                st.wait()
                stage(t + (J - 1), (j - 1) % J)

            def run(g):
                for j in range(J):
                    step(g, j, True, before=g * J + j if isinstance(g, int) else 6)

            TILE = 11
            base = st.base + st.n
            st.base, st.n = base, 0
            run(0)
            run(1)
            base += st.n
            per = TILE * J + LISTS + 4 * 2
            with dve.Fori(2, GS) as g:
                st.base, st.n = (g - 2) * per + base, 0
                run(g)
                assert st.n == per, (st.n, per)
            base += (GS - 2) * per

            st.base, st.n = base, 0
            over_now = over[:, NT:2 * NT]

            def number_heavy():
                dve.wait_ge(adj_squared, 2 * NT + J)
                for b in (over, sums_a, sums_b):
                    st.mark(nc.vector.memset(b[:, 0:NT], 0.0))
                st.mark(nc.vector.tensor_scalar(over_now.unsqueeze(2), keys[:, 0:NT, CAP:CAP + 1], 0.0, None, ALU.is_gt))
                st.wait()
                src, dst = over, sums_a
                for k in range(5):
                    sh = 1 << k
                    st.mark(nc.vector.tensor_tensor(dst[:, NT:2 * NT], src[:, NT:2 * NT], src[:, NT - sh:2 * NT - sh], ALU.add))
                    st.wait()
                    src, dst = (dst, sums_b) if dst is sums_a else (dst, sums_a)
                assert src is sums_a and 1 << 5 == NT
                nc.vector.tensor_scalar(none[:, :], over_now, 0.0, float(N), ALU.is_equal, ALU.mult).then_inc(over_ready, 1)

            step(GS, 0, False, between=number_heavy)
            dve.wait_ge(over_ready, 1)
            dve.wait_ge(ranked, 1)
            st.mark(nc.vector.tensor_tensor(place[:, :], rank_p, none[:, :], ALU.add))
            st.wait()
            st.mark(nc.vector.tensor_scalar(bad2[:, :], place[:, :], float(P), None, ALU.is_ge))
            st.mark(nc.vector.tensor_tensor(bad[:, :], sq[:, 0:2 * NT:2], sq[:, 1:2 * NT:2], ALU.add))
            st.wait()
            st.mark(nc.vector.tensor_tensor(bad2[:, :], bad2[:, :], over_now, ALU.mult))
            st.mark(nc.vector.tensor_tensor(bad[:, :], bad[:, :], cnt[:, :], ALU.not_equal))
            st.wait()
            st.mark(nc.vector.tensor_tensor(bad[:, :].unsqueeze(2), bad[:, :].unsqueeze(2), keys[:, 0:NT, HCAP:HCAP + 1], ALU.add))
            st.wait()
            nc.vector.tensor_tensor(bad2[:, :], bad2[:, :], bad[:, :], ALU.add).then_inc(bad_ready, 1)
            nc.vector.tensor_scalar(pick[:, :, 0:KEYS], keys[:, 0:NT, :], float(HALF), None, ALU.subtract).then_inc(onehot_ready, 1)
            nc.vector.memset(pick[:, :, KEYS:KEYS + 1], 1.0).then_inc(onehot_ready, 1)
            for c in range(J):
                n = NT // J
                nc.vector.tensor_tensor(onehot[:, c * n:(c + 1) * n, :], rank_row[:, :].unsqueeze(1).to_broadcast([P, n, P]),
                                        place[:, c * n:(c + 1) * n].unsqueeze(2).to_broadcast([P, n, P]),
                                        ALU.is_equal).then_inc(onehot_ready, 1)

            def heavy_lists():
                dve.wait_ge(hkey_done, 1)
                st.mark(nc.vector.tensor_copy(hsum[:, :], hkey_p))
                st.wait()
                st.mark(nc.vector.scalar_tensor_tensor(hkey[:, :], hsum[:, KEYS:KEYS + 1].to_broadcast([P, KEYS]), float(HALF),
                                                       hsum[:, 0:KEYS], ALU.mult, ALU.add))
                st.wait()
                for d0, s0_, n in ((0, 0, HCAP), (HCAP, LIST, 1)):
                    nc.vector.tensor_scalar(hidx[:, d0:d0 + n], hkey[:, s0_:s0_ + n], -1.0, float(N), ALU.mult,
                                            ALU.add).then_inc(h_idx, 1)
                nc.vector.tensor_scalar(hlim[:, :], hkey[:, 0:HCAP], LIFT, MASKED, ALU.mult, ALU.add).then_inc(h_idx, 1)

            step(GS, 1, False, between=heavy_lists)
            step(GS, 2, False)
            step(GS, J - 1, False)

            dve.wait_ge(h_idx, 3)
            dve.wait_ge(h_gathered, 16 * (HCAP + 3))
            q_row = hq.unsqueeze(1)
            scores_less_max([(1, G[0][:, :, 0:D], q_row, hlim[:, 0:CAP]), (1 + CAP, G[1][:, :, 0:D], q_row, hlim[:, CAP:HCAP]),
                             (0, hself[:, 0:D].unsqueeze(1), q_row, None)], lambda: None, HCAP + 1, h_shifted)
            first_norm_stats(NT - 1, J - 1)
            dve.wait_ge(h_exp, 1)
            dve.wait_ge(ctx_summed, NT + J)
            weigh([(0, hself[:, D:2 * D].unsqueeze(1), wself[:, :].unsqueeze(1)), (1, G[0][:, :, D:2 * D], G[0][:, :, 0:D]),
                   (1 + CAP, G[1][:, :, D:2 * D], G[1][:, :, 0:D])], HCAP + 1, h_weighted)

            def rest(r, parts, rows):
                ts = Steps(dve, t_step, r * T_DVE)
                if "norm1" in parts:
                    dve.wait_ge(baton, r * B_OUT + B_AO)
                    ts.mark(nc.vector.tensor_tensor(t_y, ao_p, rows, ALU.add))
                    ts.wait()
                    ts.mark(nc.vector.tensor_tensor(t_y, t_y, bo_b[:, :], ALU.add))
                    ts.wait()
                    stats(ts, [(t_y, 4)], baton)
                if "norm2" in parts:
                    ts.n = 4
                    dve.wait_ge(baton, r * B_OUT + B_FF2)
                    dve.wait_ge(t_resd, r + 1)
                    ts.mark(nc.vector.tensor_tensor(t_z, ff2_p[0], t_res, ALU.add))
                    ts.wait()
                    stats(ts, [(t_z, 4)], baton)

            second_sums(NT - 4)
            rest(0, ("norm1",), hx)
            dve.wait_ge(bad_summed, 1)
            st.mark(nc.vector.tensor_scalar(tfl[:, :], bad_p, 0.0, None, ALU.is_gt))
            st.wait()
            st.mark(nc.vector.tensor_reduce(tlist[:, 0:1], tfl[:, :], AX, ALU.add))
            st.mark(nc.vector.tensor_tensor(tkey[:, :], tfl[:, :], tdown[:, :], ALU.mult))
            st.wait()
            for i in range(NT // FOUND):
                st.mark(nc.vector.max(tlist[:, 1 + i * FOUND:1 + (i + 1) * FOUND], tkey[:, :]))
                st.wait()
                if i < NT // FOUND - 1:
                    st.mark(nc.vector.match_replace(tkey[:, :], tlist[:, 1 + i * FOUND:1 + (i + 1) * FOUND], tkey[:, :], 0.0))
                    st.wait()
            st.mark(nc.vector.tensor_scalar(tlist[:, 1:], tlist[:, 1:], -1.0, float(NT), ALU.mult, ALU.add))
            st.wait()
            nc.vector.tensor_copy(flags[:, :], tlist[:, :]).then_inc(flags_ready, 1)
            second_sums(NT - 2)
            rest(0, ("norm2",), hx)

            nf = dve.value_load(flags[0:1, 0:1], min_val=0, max_val=NT)
            with dve.If(nf > 0):
                dve.wait_ge(h_stored, 16)
                with dve.Fori(0, nf) as r:
                    fs = Steps(dve, f_step, 0)
                    f = dve.value_load(flags[0:1, at(r + 1, 1)], min_val=0, max_val=NT - 1)
                    fs.base = r * F_STEPS
                    dve.wait_ge(f_in, r * 48 + 48)
                    blk = adjb[:, at(f * P, P)]
                    fs.mark(nc.vector.tensor_tensor(blk, blk, ident[:, :], ALU.add))
                    fs.wait()
                    fs.mark(nc.vector.tensor_scalar(vmask, fadj, 0.0, None, ALU.not_equal))
                    fs.wait()
                    fs.mark(nc.vector.tensor_scalar(pen, vmask, 1.0, -MASKED, ALU.subtract, ALU.mult))
                    fs.wait()
                    dve.wait_ge(f_q, r + 1)
                    for h in range(H):
                        dh = h // J
                        nc.vector.tensor_scalar(qz[:, h, :], ctx_p[1][:, dh * P:(dh + 1) * P], bqT[:, dh:dh + 1],
                                                headmask[:, h % J:h % J + 1], ALU.add, ALU.mult).then_inc(f_qz, 1)
                    for h in range(H):
                        hb = r * (H * NG) + h * NG
                        with dve.Fori(0, NG) as c:
                            dve.wait_ge(f_s, hb + c + 1)
                            nc.vector.scalar_tensor_tensor(S[:, at(c * 512, 512)], fs_p, SCALE, vmask[:, at(c * 512, 512)],
                                                           ALU.mult, ALU.mult).then_inc(f_sread, 1)
                            dve.wait_ge(f_sread, hb + c + 2)
                            nc.vector.tensor_tensor(S[:, at(c * 512, 512)], S[:, at(c * 512, 512)], pen[:, at(c * 512, 512)],
                                                    ALU.add).then_inc(f_step, 1)
                        fs.n += NG
                        fs.wait()
                        fs.mark(nc.vector.tensor_reduce(fmax, S, AX, ALU.max))
                        fs.wait()
                        nc.vector.tensor_scalar(fnmax, fmax, -1.0, None, ALU.mult).then_inc(f_max, 1)
                        dve.wait_ge(f_e, r * H + h + 1)
                        fs.mark(nc.vector.reciprocal(frden, fden))
                        fs.mark(nc.vector.memset(fctx[:, h * DK:(h + 1) * DK], 0.0))
                        fs.wait()
                        apart(dve)
                        with dve.Fori(0, NG) as c:
                            dve.wait_ge(f_t, hb + c + 1)
                            nc.vector.tensor_copy(stg, S[:, at(c * 512, 512)]).then_inc(f_st, 1)
                            dve.wait_ge(f_pv, hb + c + 2)
                            nc.vector.tensor_tensor(fctx[:, h * DK:(h + 1) * DK], fctx[:, h * DK:(h + 1) * DK],
                                                    ctx_p[0][:, 0:DK], ALU.add).then_inc(f_acc, 1)
                            dve.wait_ge(f_acc, hb + c + 2)
                        fs.mark(nc.vector.tensor_scalar(fctx[:, h * DK:(h + 1) * DK], fctx[:, h * DK:(h + 1) * DK],
                                                        frden, None, ALU.mult))
                        fs.wait()
                        apart(dve)
                    dve.sem_inc(f_ctx, 1)
                    assert fs.n == F_STEPS, fs.n
                    rest(r + 1, ("norm1", "norm2"), xr[:, 0, :])

        @block.tensor
        def _(pe):
            for s, n in ((qkv_done, J), (ctx_summed, J), (h1T_done, 2), (f_t, 1), (f_pv, 1)):
                pe.sem_inc(s, n)
            pe.wait_ge(wq_in, 48)
            with pe.Fori(0, NG // 2) as i:
                for s in range(2):
                    g = i * 2 + s
                    pe.wait_ge(xT_in[s], i * 16 + 16)
                    for j in range(J):
                        b = j % 2
                        pe.wait_ge(kq_copied, g * J + j + 1)
                        pe.wait_ge(v_ready, g * J + j + 1)
                        for c0, c1 in ((0, 2 * D), (2 * D, 3 * D)):
                            for k in range(KD):
                                last = nc.tensor.matmul(qkv_p[b][:, c0:c1], xTb[s][:, k, j * P:(j + 1) * P],
                                                        wkqv[:, k, c0:c1], start=(k == 0), stop=(k == KD - 1))
                        last.then_inc(qkv_done, 1)

            def transpose_first(src, t):
                pe.wait_ge(h1T_ready, t * KD + KD)
                for k in range(KD):
                    last = nc.tensor.transpose(h1T_p[:, k * P:(k + 1) * P], src[:, k * P:(k + 1) * P], ident[:, :])
                return last

            def transpose_h1(t, j):
                pe.wait_ge(nh_ready, t + 3)
                transpose_first(nh[j % 2], t).then_inc(h1T_done, 1)

            def ff1(p, units=range(KU)):
                pe.wait_ge(h1T_ready, p * (2 * KD) + 3 * KD)
                for u in units:
                    if u >= 2:
                        pe.wait_ge(hid_ready, p * KF + (2 * u - 2))
                    for c in (2 * u, 2 * u + 1):
                        for k in range(KD):
                            last = nc.tensor.matmul(ff1_p[u % 2][:, c % 2 * W:(c % 2 + 1) * W], w1[:, k, c * P:(c + 1) * P],
                                                    h1T[:, k, :], start=(k == 0), stop=(k == KD - 1))
                    last.then_inc(ff1_done, 1)

            def ff2(p, i):
                pe.wait_ge(hid_ready, p * KF + KF)
                pe.wait_ge(z_done, p * 2 + (i + 1))
                for c in range(KF):
                    last = nc.tensor.matmul(ff2_p[i], hid[:, c, i * P:(i + 1) * P], w2[:, c, :],
                                            start=(c == 0), stop=(c == KF - 1))
                last.then_inc(ff2_done, 1)

            def sum_transposed(dst, rows):
                for k in range(KD):
                    for i, src in enumerate(rows):
                        last = nc.tensor.matmul(dst[:, k * P:(k + 1) * P], src[:, k * P:(k + 1) * P], ident[:, :],
                                                is_transpose=True, start=(i == 0), stop=(i == len(rows) - 1))
                return last

            def project_out(src):
                for k in range(KD):
                    last = nc.tensor.matmul(ao_p, src[:, k, :], wo[:, k, :], start=(k == 0), stop=(k == KD - 1))
                return last

            def step(g, j, before=6, last=False):
                t = g * J + j
                pe.wait_ge(weighted, t * 2 + 2)
                sum_transposed(ctx_p[j % 2], [wself[:, :]] + [G[j][:, s, 0:D] for s in range(CAP)]).then_inc(ctx_summed, 1)
                if before >= 1:
                    transpose_h1(t - 1, (j - 1) % J)
                pe.wait_ge(ctxT_ready, t * KD + KD)
                pe.wait_ge(y_done, t + J)
                project_out(ctxT[j % 2]).then_inc(ao_done, 1)
                if before == 2:
                    pe.wait_ge(w1_in, 16)
                if before == 3:
                    pe.wait_ge(w2_in, 16)
                if before >= 2 and j % 2 == 0:
                    ff1(g * (J // 2) + (j - 2) // 2)
                if before >= 3 and j % 2:
                    ff2(g * (J // 2) + (j - 3) // 2, 0)
                    if last:
                        transpose_h1(t, j)
                if before >= 3 and j % 2:
                    ff2(g * (J // 2) + (j - 3) // 2, 1)

            pe.wait_ge(wo_in, 16)
            pe.wait_ge(pool_const, 10)
            pe.wait_ge(dve_const, 3)
            for j in range(J):
                step(0, j, before=j)
            with pe.Fori(1, GS) as g:
                for j in range(J):
                    step(g, j)
            pe.wait_ge(over_ready, 1)
            nc.tensor.matmul(rank_p, upper[:, :], over[:, NT:2 * NT], start=True, stop=False)
            nc.tensor.matmul(rank_p, ones_pp[:, :], sums_a[:, NT - 1:2 * NT - 1], start=False, stop=True).then_inc(ranked, 1)
            step(GS, 0)
            pe.wait_ge(bad_ready, 1)
            nc.tensor.matmul(bad_p, ones_pp[:, 0:1], bad2[:, :], start=True, stop=True).then_inc(bad_summed, 1)
            for t in range(NT):
                pe.wait_ge(onehot_ready, t // (NT // J) + 3)
                last = nc.tensor.matmul(hkey_p, onehot[:, t, :], pick[:, t, :], start=(t == 0), stop=(t == NT - 1))
            last.then_inc(hkey_done, 1)
            for j in range(1, J):
                step(GS, j, last=(j == J - 1))

            def rest(r, parts):
                if "norm1" in parts:
                    pe.wait_ge(baton, r * B_OUT + B_CTXT)
                    project_out(ctxT[0]).then_inc(baton, 1)
                if "turn" in parts:
                    pe.wait_ge(baton, r * B_OUT + B_NH)
                    for k in range(KD):
                        last = nc.tensor.transpose(h1T_p[:, k * P:(k + 1) * P], t_nh[:, k * P:(k + 1) * P], ident[:, :])
                    last.then_inc(baton, 1)
                if "feed" in parts:
                    pe.wait_ge(baton, r * B_OUT + B_H1T)
                    for u in range(2):
                        for i in range(KF // 2):
                            c = u * (KF // 2) + i
                            for k in range(KD):
                                last = nc.tensor.matmul(ff1_p[u][:, i * P:(i + 1) * P], w1[:, k, c * P:(c + 1) * P],
                                                        t_h1T[:, k, :], start=(k == 0), stop=(k == KD - 1))
                        last.then_inc(t_ff1, 1)
                if "feed2" in parts:
                    pe.wait_ge(t_relu, r * KF + KF)
                    for c in range(KF):
                        last = nc.tensor.matmul(ff2_p[0], t_hid[:, c, :], w2[:, c, :], start=(c == 0), stop=(c == KF - 1))
                    last.then_inc(baton, 1)

            ff1(NT // 2 - 1, [0])
            pe.wait_ge(h_weighted, 3)
            sum_transposed(ctx_p[0], [wself[:, :]] + [G[i][:, s, 0:D] for i in range(2) for s in range(CAP)]).then_inc(baton, 1)
            ff1(NT // 2 - 1, [1])
            pe.wait_ge(y_done, NT + J)
            rest(0, ("norm1",))
            ff1(NT // 2 - 1, [2, 3])
            pe.wait_ge(h1T_ready, NT * KD + KD)
            rest(0, ("turn",))
            ff2(NT // 2 - 1, 0)
            rest(0, ("feed",))
            ff2(NT // 2 - 1, 1)
            pe.wait_ge(z_done, NT + 1)
            rest(0, ("feed2",))

            pe.wait_ge(flags_ready, 1)
            nf = pe.value_load(flags[0:1, 0:1], min_val=0, max_val=NT)
            with pe.If(nf > 0):
                pe.wait_ge(h_stored, 16)
                with pe.Fori(0, NG) as c:
                    pe.wait_ge(f_w, 48)
                    pe.wait_ge(f_x, c * 16 + 16)
                    for dh in range(KD):
                        for k in range(KD):
                            last = nc.tensor.matmul(ff1_p[dh], fw[:, k, dh * P:(dh + 1) * P], fxT[:, k, :],
                                                    start=(k == 0), stop=(k == KD - 1))
                        last.then_inc(f_ktmm, 1)
                with pe.Fori(0, nf) as r:
                    pe.wait_ge(f_in, r * 48 + 48)
                    pe.wait_ge(f_w, r * 48 + 96)
                    pe.wait_ge(baton, r * B_OUT + B_OUT)
                    for dh in range(KD):
                        for k in range(KD):
                            last = nc.tensor.matmul(ctx_p[1][:, dh * P:(dh + 1) * P], fw[:, k, D + dh * P:D + (dh + 1) * P],
                                                    fx[:, k, :], start=(k == 0), stop=(k == KD - 1))
                    last.then_inc(f_q, 1)
                    pe.wait_ge(f_qz, r * H + H)
                    pe.wait_ge(f_kt, KD * NG + KD)
                    apart(pe)
                    for h in range(H):
                        hb = r * (H * NG) + h * NG
                        with pe.Fori(0, NG) as c:
                            pe.wait_ge(f_sread, hb + c + 1)
                            nc.tensor.matmul(fs_p, qz[:, h, :], KT[:, h // J, at(c * 512, 512)], start=True, stop=True).then_inc(f_s, 1)
                        with pe.Fori(0, NG) as c:
                            pe.wait_ge(f_st, hb + c + 1)
                            pe.wait_ge(f_pt, hb + c + 1)
                            for i in range(J):
                                last = nc.tensor.transpose(ff1_p[0][:, i * P:(i + 1) * P], stg[:, i * P:(i + 1) * P], ident[:, :])
                            last.then_inc(f_t, 1)
                            pe.wait_ge(f_pt, hb + c + 2)
                            pe.wait_ge(f_acc, hb + c + 1)
                            for i in range(J):
                                last = nc.tensor.matmul(ctx_p[0][:, 0:DK], PT[:, i, :],
                                                        Vs[:, at(c * J + i), h * DK:(h + 1) * DK].rearrange("p o d -> p (o d)"),
                                                        start=(i == 0), stop=(i == J - 1))
                            last.then_inc(f_pv, 1)
                    pe.wait_ge(f_ctx, r + 1)
                    for k in range(KD):
                        last = nc.tensor.transpose(ctx_p[0][:, k * P:(k + 1) * P], fctx[:, k * P:(k + 1) * P], ident[:, :])
                    last.then_inc(baton, 1)
                    rest(r + 1, ("norm1", "turn", "feed", "feed2"))


def kernel(**inputs):
    import numpy as np
    import concourse.bacc as bacc
    from concourse.bass_utils import run_bass_kernel_spmd

    nc = bacc.Bacc("TRN2", target_bir_lowering=False, num_devices=1)
    arrays = {}

    def given(name, transposed=False):
        a = np.asarray(inputs[name])
        a = np.ascontiguousarray(a.T if transposed else a)
        key = f"in_{name}_T" if transposed else f"in_{name}"
        arrays[key] = a
        return nc.dram_tensor(key, a.shape, mybir.dt.from_np(a.dtype), kind="ExternalInput").ap()

    p = "L0_gnn_"
    args = [given("x"), given("x", True), given("adj")]
    for m, b in (("Wq", "bq"), ("Wk", "bk"), ("Wv", "bv"), ("Wo", "bo"), ("W1", "b1"), ("W2", "b2")):
        args += [given(p + m, True), given(p + b)]
    args += [given(p + n) for n in ("ln1_g", "ln1_b", "ln2_g", "ln2_b")]
    n, d = inputs["x"].shape
    kv = nc.dram_tensor("kv", (n, 2 * d), mybir.dt.float32, kind="Internal").ap()
    qd = nc.dram_tensor("qd", (n, d), mybir.dt.float32, kind="Internal").ap()
    out = nc.dram_tensor("out_rows", (n, d), mybir.dt.float32, kind="ExternalOutput").ap()
    build(nc, *args, kv, qd, out)
    return run_bass_kernel_spmd(nc, [arrays], core_ids=[0]).results[0]["out_rows"]
```
